# Optimizing a Trainium2 kernel written in Bass

```python
import numpy as np
import jax
import jax.numpy as jnp

def _softmax(x, axis=-1):
    return jax.nn.softmax(x, axis=axis)

def _gelu(x):
    return jax.nn.gelu(x, approximate=True)

def _silu(x):
    return jax.nn.silu(x)

def _sigmoid(x):
    return jax.nn.sigmoid(x)

def _layernorm(x, axis=-1, eps=1e-05):
    m = jnp.mean(x, axis=axis, keepdims=True)
    v = jnp.var(x, axis=axis, keepdims=True)
    return (x - m) / jnp.sqrt(v + eps)

def _scatter_add(tgt, idx, src, axis=0):
    return tgt.at[idx].add(src)

def _segment_sum(src, seg, n):
    return jax.ops.segment_sum(src, seg, n)
kernel_name = 'mk_decoder_postln_d1_seqx_r8_cbb2b7'

def setup_inputs(seed: int=0):
    np.random.seed(seed)
    _w = jnp.asarray

    def _rec_inputs():
        import jax
        import jax.numpy as jnp
        _rk = jax.random.key(seed)
        x = 7.22e-05 + 1 * jax.random.normal(jax.random.fold_in(_rk, 1), (32, 128, 128), jnp.float32)
        _lenS = 128 - jax.random.randint(jax.random.fold_in(_rk, 7), (32,), 0, max(1, 128 // 4) + 1, jnp.int32)
        _lenS2 = 128 - jax.random.randint(jax.random.fold_in(_rk, 8), (32,), 0, max(1, 128 // 4) + 1, jnp.int32)
        _ctx_1024P = jax.random.normal(jax.random.fold_in(_rk, 11), (32, 16, 128), jnp.float32)
        _ctx_1024c = jax.random.dirichlet(jax.random.fold_in(_rk, 511), 0.3 * jnp.ones((16,), jnp.float32), (32, 128))
        _ctx_1024t = jnp.einsum('bsk,bkd->bsd', _ctx_1024c, _ctx_1024P)
        _ctx_1024t = _ctx_1024t * jax.lax.rsqrt(jnp.mean(jnp.square(_ctx_1024t)) + 1e-12) * 0.953939
        ctx_1024 = 4.13588e-05 + 0.999923 * (_ctx_1024t + 0.3 * jax.random.normal(jax.random.fold_in(_rk, 611), (32, 128, 128), jnp.float32))
        _validS = jnp.arange(128)[None, :] < _lenS[:, None]
        _validS2 = jnp.arange(128)[None, :] < _lenS2[:, None]
        _causal = jnp.tril(jnp.ones((128, 128), dtype=bool))
        mask_Bx1xSxS2_bk1 = jnp.broadcast_to(_validS2[:, None, None, :], (32, 1, 128, 128))
        return (x, ctx_1024, mask_Bx1xSxS2_bk1)
    x, ctx_1024, mask_Bx1xSxS2_bk1 = _rec_inputs()

    def _L0_attn_setup():
        import jax, jax.numpy as jnp
        import numpy as np
        import math
        D_MODEL = 128
        D_STATE = 128
        EXPAND = 2
        HEADDIM = 64
        NGROUPS = 1
        ROPE_FRACTION = 0.5
        A_FLOOR = 0.0001
        D_INNER = EXPAND * D_MODEL
        NHEADS = D_INNER // HEADDIM
        SPLIT = int(D_STATE * ROPE_FRACTION)
        R = SPLIT // 2
        D_IN_PROJ = 2 * D_INNER + 2 * D_STATE * NGROUPS + 3 * NHEADS + R
        BATCH = 1
        SEQLEN = 128

        def _mamba3_forward(u, w_in, w_out, dt_bias, D):
            b, l, _ = u.shape
            proj = u @ w_in.T
            sizes = [D_INNER, D_INNER, D_STATE * NGROUPS, D_STATE * NGROUPS, NHEADS, NHEADS, NHEADS, R]
            idx = np.cumsum(sizes)[:-1]
            z, x, B, C, dd_dt, dd_A, trap, angles = jnp.split(proj, idx, axis=-1)
            A = jnp.minimum(-jax.nn.softplus(dd_A), -A_FLOOR)
            dt = jax.nn.softplus(dd_dt + dt_bias)
            tr = jax.nn.sigmoid(trap)
            theta = jnp.cumsum(jnp.tanh(angles)[:, :, None, :] * dt[..., None] * jnp.pi, axis=1)
            x_h = x.reshape(b, l, NHEADS, HEADDIM)
            z_h = z.reshape(b, l, NHEADS, HEADDIM)
            B_h = B.reshape(b, l, NGROUPS, D_STATE)[:, :, 0, :]
            C_h = C.reshape(b, l, NGROUPS, D_STATE)[:, :, 0, :]

            def step(carry, inp):
                sr, si, px = carry
                dt_t, A_t, tr_t, th, bt, ct, xt = inp
                alpha = jnp.exp(A_t * dt_t)[:, :, None, None]
                beta = ((1.0 - tr_t) * dt_t)[:, :, None, None] * alpha
                gamma = (tr_t * dt_t)[:, :, None, None]
                base = bt[:, None, None, :] * (px[..., None] * beta + xt[..., None] * gamma)
                rc = jnp.cos(th)[:, :, None, :]
                rs = jnp.sin(th)[:, :, None, :]
                sr = sr * alpha + jnp.concatenate([base[..., :R] * rc, base[..., R:]], axis=-1)
                si = si * alpha + base[..., :R] * rs
                ctb = ct[:, None, None, :]
                y = jnp.sum((sr[..., :R] * rc + si * rs) * ctb[..., :R], axis=-1) + jnp.sum(sr[..., R:] * ctb[..., R:], axis=-1)
                return ((sr, si, xt), y)
            sr0 = jnp.zeros((b, NHEADS, HEADDIM, D_STATE), u.dtype)
            si0 = jnp.zeros((b, NHEADS, HEADDIM, R), u.dtype)
            px0 = jnp.zeros((b, NHEADS, HEADDIM), u.dtype)
            xs = (jnp.moveaxis(dt, 1, 0), jnp.moveaxis(A, 1, 0), jnp.moveaxis(tr, 1, 0), jnp.moveaxis(theta, 1, 0), jnp.moveaxis(B_h, 1, 0), jnp.moveaxis(C_h, 1, 0), jnp.moveaxis(x_h, 1, 0))
            _, ys = jax.lax.scan(step, (sr0, si0, px0), xs)
            y = jnp.moveaxis(ys, 0, 1) + D[None, None, :, None] * x_h
            out = y * jax.nn.silu(z_h)
            return out.reshape(b, l, D_INNER) @ w_out.T
        key = jax.random.key(seed)
        k0, k1, k2, k3 = jax.random.split(key, 4)
        u = jax.random.normal(k0, (BATCH, SEQLEN, D_MODEL), jnp.float32)
        w_in = jax.random.normal(k1, (D_IN_PROJ, D_MODEL), jnp.float32) * D_MODEL ** (-0.5)
        w_out = jax.random.normal(k2, (D_MODEL, D_INNER), jnp.float32) * D_INNER ** (-0.5)
        dt = jnp.exp(jax.random.uniform(k3, (NHEADS,), jnp.float32) * (math.log(0.1) - math.log(0.001)) + math.log(0.001))
        dt = jnp.maximum(dt, 0.0001)
        dt_bias = dt + jnp.log(-jnp.expm1(-dt))
        D = jnp.ones((NHEADS,), jnp.float32)
        return {'u': u, 'w_in': w_in, 'w_out': w_out, 'dt_bias': dt_bias, 'D': D}
    _L0_attn_all = _L0_attn_setup()
    _L0_attn_in = {k: v for k, v in _L0_attn_all.items() if k in ('w_in', 'w_out', 'dt_bias', 'D')}
    del _L0_attn_all

    def _L0_xattn_setup():
        import jax, jax.numpy as jnp
        import numpy as np
        B, S, D, H = (4, 256, 128, 16)
        HD = D // H
        key = jax.random.key(seed)
        ks = jax.random.split(key, 12)
        scale = 1.0 / np.sqrt(D)
        inp = {'queries': jax.random.normal(ks[0], (B, S, D), jnp.float32), 'keys': jax.random.normal(ks[1], (B, S, D), jnp.float32), 'values': jax.random.normal(ks[2], (B, S, D), jnp.float32), 'mask': jax.random.randint(ks[3], (B, 1, S, S), 0, 2).astype(bool), 'Wq': jax.random.normal(ks[4], (D, D), jnp.float32) * scale, 'bq': jnp.zeros((D,), jnp.float32), 'Wk': jax.random.normal(ks[5], (D, D), jnp.float32) * scale, 'bk': jnp.zeros((D,), jnp.float32), 'Wv': jax.random.normal(ks[6], (D, D), jnp.float32) * scale, 'bv': jnp.zeros((D,), jnp.float32), 'Wo': jax.random.normal(ks[7], (D, D), jnp.float32) * scale, 'bo': jnp.zeros((D,), jnp.float32)}
        return inp
    _L0_xattn_all = _L0_xattn_setup()
    _L0_xattn_in = {k: v for k, v in _L0_xattn_all.items() if k in ('Wq', 'bq', 'Wk', 'bk', 'Wv', 'bv', 'Wo', 'bo')}
    del _L0_xattn_all

    def _L0_ffn_setup():
        import jax, jax.numpy as jnp
        import numpy as np
        E = 16
        K = 4
        NG = 4
        TG = 2
        SCALE = 2.5
        NORM_TOPK = True
        H = 128
        I = 64
        SH_I = I * 2
        B, S = (2, 256)
        key = jax.random.key(seed)
        ks = jax.random.split(key, 9)

        def w(k, shape, fan_in):
            return jax.random.normal(k, shape, jnp.float32) * (1.0 / np.sqrt(fan_in))
        return {'hidden_states': jax.random.normal(ks[0], (B, S, H), jnp.float32), 'gate_w': w(ks[1], (E, H), H), 'gate_bias': jnp.zeros((E,), jnp.float32), 'Wg': w(ks[2], (E, I, H), H), 'Wu': w(ks[3], (E, I, H), H), 'Wd': w(ks[4], (E, H, I), I), 'Ws_g': w(ks[5], (SH_I, H), H), 'Ws_u': w(ks[6], (SH_I, H), H), 'Ws_d': w(ks[7], (H, SH_I), SH_I)}
    _L0_ffn_all = _L0_ffn_setup()
    _L0_ffn_in = {k: v for k, v in _L0_ffn_all.items() if k in ('gate_w', 'gate_bias', 'Wg', 'Wu', 'Wd', 'Ws_g', 'Ws_u', 'Ws_d')}
    del _L0_ffn_all
    return {'x': x, 'ctx_1024': ctx_1024, 'mask_Bx1xSxS2_bk1': mask_Bx1xSxS2_bk1, 'L0_attn_w_in': _L0_attn_in['w_in'], 'L0_attn_w_out': _L0_attn_in['w_out'], 'L0_attn_dt_bias': _L0_attn_in['dt_bias'], 'L0_attn_D': _L0_attn_in['D'], 'L0_xattn_Wq': _L0_xattn_in['Wq'], 'L0_xattn_bq': _L0_xattn_in['bq'], 'L0_xattn_Wk': _L0_xattn_in['Wk'], 'L0_xattn_bk': _L0_xattn_in['bk'], 'L0_xattn_Wv': _L0_xattn_in['Wv'], 'L0_xattn_bv': _L0_xattn_in['bv'], 'L0_xattn_Wo': _L0_xattn_in['Wo'], 'L0_xattn_bo': _L0_xattn_in['bo'], 'L0_ffn_gate_w': _L0_ffn_in['gate_w'], 'L0_ffn_gate_bias': _L0_ffn_in['gate_bias'], 'L0_ffn_Wg': _L0_ffn_in['Wg'], 'L0_ffn_Wu': _L0_ffn_in['Wu'], 'L0_ffn_Wd': _L0_ffn_in['Wd'], 'L0_ffn_Ws_g': _L0_ffn_in['Ws_g'], 'L0_ffn_Ws_u': _L0_ffn_in['Ws_u'], 'L0_ffn_Ws_d': _L0_ffn_in['Ws_d']}

def reference(x, ctx_1024, mask_Bx1xSxS2_bk1, L0_attn_w_in, L0_attn_w_out, L0_attn_dt_bias, L0_attn_D, L0_xattn_Wq, L0_xattn_bq, L0_xattn_Wk, L0_xattn_bk, L0_xattn_Wv, L0_xattn_bv, L0_xattn_Wo, L0_xattn_bo, L0_ffn_gate_w, L0_ffn_gate_bias, L0_ffn_Wg, L0_ffn_Wu, L0_ffn_Wd, L0_ffn_Ws_g, L0_ffn_Ws_u, L0_ffn_Ws_d):
    import jax
    import jax.numpy as jnp

    def _L0_attn_ref(u, w_in, w_out, dt_bias, D):
        import jax, jax.numpy as jnp
        import numpy as np
        import math
        D_MODEL = 128
        D_STATE = 128
        EXPAND = 2
        HEADDIM = 64
        NGROUPS = 1
        ROPE_FRACTION = 0.5
        A_FLOOR = 0.0001
        D_INNER = EXPAND * D_MODEL
        NHEADS = D_INNER // HEADDIM
        SPLIT = int(D_STATE * ROPE_FRACTION)
        R = SPLIT // 2
        D_IN_PROJ = 2 * D_INNER + 2 * D_STATE * NGROUPS + 3 * NHEADS + R
        BATCH = 1
        SEQLEN = 128

        def _mamba3_forward(u, w_in, w_out, dt_bias, D):
            b, l, _ = u.shape
            proj = u @ w_in.T
            sizes = [D_INNER, D_INNER, D_STATE * NGROUPS, D_STATE * NGROUPS, NHEADS, NHEADS, NHEADS, R]
            idx = np.cumsum(sizes)[:-1]
            z, x, B, C, dd_dt, dd_A, trap, angles = jnp.split(proj, idx, axis=-1)
            A = jnp.minimum(-jax.nn.softplus(dd_A), -A_FLOOR)
            dt = jax.nn.softplus(dd_dt + dt_bias)
            tr = jax.nn.sigmoid(trap)
            theta = jnp.cumsum(jnp.tanh(angles)[:, :, None, :] * dt[..., None] * jnp.pi, axis=1)
            x_h = x.reshape(b, l, NHEADS, HEADDIM)
            z_h = z.reshape(b, l, NHEADS, HEADDIM)
            B_h = B.reshape(b, l, NGROUPS, D_STATE)[:, :, 0, :]
            C_h = C.reshape(b, l, NGROUPS, D_STATE)[:, :, 0, :]

            def step(carry, inp):
                sr, si, px = carry
                dt_t, A_t, tr_t, th, bt, ct, xt = inp
                alpha = jnp.exp(A_t * dt_t)[:, :, None, None]
                beta = ((1.0 - tr_t) * dt_t)[:, :, None, None] * alpha
                gamma = (tr_t * dt_t)[:, :, None, None]
                base = bt[:, None, None, :] * (px[..., None] * beta + xt[..., None] * gamma)
                rc = jnp.cos(th)[:, :, None, :]
                rs = jnp.sin(th)[:, :, None, :]
                sr = sr * alpha + jnp.concatenate([base[..., :R] * rc, base[..., R:]], axis=-1)
                si = si * alpha + base[..., :R] * rs
                ctb = ct[:, None, None, :]
                y = jnp.sum((sr[..., :R] * rc + si * rs) * ctb[..., :R], axis=-1) + jnp.sum(sr[..., R:] * ctb[..., R:], axis=-1)
                return ((sr, si, xt), y)
            sr0 = jnp.zeros((b, NHEADS, HEADDIM, D_STATE), u.dtype)
            si0 = jnp.zeros((b, NHEADS, HEADDIM, R), u.dtype)
            px0 = jnp.zeros((b, NHEADS, HEADDIM), u.dtype)
            xs = (jnp.moveaxis(dt, 1, 0), jnp.moveaxis(A, 1, 0), jnp.moveaxis(tr, 1, 0), jnp.moveaxis(theta, 1, 0), jnp.moveaxis(B_h, 1, 0), jnp.moveaxis(C_h, 1, 0), jnp.moveaxis(x_h, 1, 0))
            _, ys = jax.lax.scan(step, (sr0, si0, px0), xs)
            y = jnp.moveaxis(ys, 0, 1) + D[None, None, :, None] * x_h
            out = y * jax.nn.silu(z_h)
            return out.reshape(b, l, D_INNER) @ w_out.T
        return _mamba3_forward(u, w_in, w_out, dt_bias, D)

    def _L0_xattn_ref(queries, keys, values, mask, Wq, bq, Wk, bk, Wv, bv, Wo, bo):
        import jax, jax.numpy as jnp
        import numpy as np
        B, S, D, H = (4, 256, 128, 16)
        HD = D // H
        b, sq, d = queries.shape

        def split_heads(x):
            return x.reshape(b, x.shape[1], H, HD).transpose(0, 2, 1, 3)
        q = split_heads(queries @ Wq + bq)
        k = split_heads(keys @ Wk + bk)
        v = split_heads(values @ Wv + bv)
        scores = jnp.einsum('bhqd,bhkd->bhqk', q, k) / jnp.sqrt(jnp.float32(HD))
        scores = jnp.where(mask, jnp.float32(-1000000000000000.0), scores)
        attn = jax.nn.softmax(scores, axis=-1)
        ctx = jnp.einsum('bhqk,bhkd->bhqd', attn, v)
        ctx = ctx.transpose(0, 2, 1, 3).reshape(b, sq, d)
        return ctx @ Wo + bo

    def _L0_ffn_ref(hidden_states, gate_w, gate_bias, Wg, Wu, Wd, Ws_g, Ws_u, Ws_d):
        import jax, jax.numpy as jnp
        import numpy as np
        E = 16
        K = 4
        NG = 4
        TG = 2
        SCALE = 2.5
        NORM_TOPK = True
        H = 128
        I = 64
        SH_I = I * 2
        B, S = (2, 256)
        x = hidden_states
        b, s, h = x.shape
        n = b * s
        xf = x.reshape(n, h)
        logits = xf @ gate_w.T
        scores = jax.nn.sigmoid(logits)
        sfc = scores + gate_bias
        epg = E // NG
        grp = sfc.reshape(n, NG, epg)
        g_scores = jax.lax.top_k(grp, 2)[0].sum(-1)
        _, gidx = jax.lax.top_k(g_scores, TG)
        gmask = jax.nn.one_hot(gidx, NG, dtype=sfc.dtype).sum(1)
        emask = jnp.repeat(gmask, epg, axis=1)
        masked = jnp.where(emask > 0, sfc, -jnp.inf)
        _, topk_idx = jax.lax.top_k(masked, K)
        topk_w = jnp.take_along_axis(scores, topk_idx, axis=1)
        if K > 1 and NORM_TOPK:
            topk_w = topk_w / (topk_w.sum(-1, keepdims=True) + 1e-20)
        topk_w = topk_w * SCALE
        cw = (jax.nn.one_hot(topk_idx, E, dtype=topk_w.dtype) * topk_w[..., None]).sum(1)
        hg = jnp.einsum('nh,eih->nei', xf, Wg)
        hu = jnp.einsum('nh,eih->nei', xf, Wu)
        act = jax.nn.silu(hg) * hu
        y = jnp.einsum('nei,ne,ehi->nh', act, cw, Wd)
        shared = jax.nn.silu(xf @ Ws_g.T) * (xf @ Ws_u.T) @ Ws_d.T
        y = y + shared
        return (x + y.reshape(b, s, h)).astype(hidden_states.dtype)
    x = _layernorm(x + _L0_attn_ref(x, L0_attn_w_in, L0_attn_w_out, L0_attn_dt_bias, L0_attn_D), axis=-1)
    x = _layernorm(x + _L0_xattn_ref(x, ctx_1024, ctx_1024, mask_Bx1xSxS2_bk1, L0_xattn_Wq, L0_xattn_bq, L0_xattn_Wk, L0_xattn_bk, L0_xattn_Wv, L0_xattn_bv, L0_xattn_Wo, L0_xattn_bo), axis=-1)
    x = _layernorm(x + _L0_ffn_ref(x, L0_ffn_gate_w, L0_ffn_gate_bias, L0_ffn_Wg, L0_ffn_Wu, L0_ffn_Wd, L0_ffn_Ws_g, L0_ffn_Ws_u, L0_ffn_Ws_d), axis=-1)
    return x

_drawn_inputs = setup_inputs


def setup_inputs(seed=0):
    import zlib

    import numpy as np

    out = dict(_drawn_inputs(seed))
    spreads = {'L0_attn_D': (1.0, 0.2),
     'L0_xattn_bq': (0.0, 0.1),
     'L0_xattn_bk': (0.0, 0.1),
     'L0_xattn_bv': (0.0, 0.1),
     'L0_xattn_bo': (0.0, 0.1),
     'L0_ffn_gate_bias': (0.0, 0.1)}
    factors = {}
    for name, (base, spread) in spreads.items():
        noise = np.random.default_rng([zlib.crc32(name.encode()), seed]).standard_normal(out[name].shape)
        drawn = base * np.exp(spread * noise) if base else spread * noise
        out[name] = jnp.asarray(drawn.astype(out[name].dtype))
    for name, factor in factors.items():
        out[name] = (out[name] * factor).astype(out[name].dtype)
    return out
```

```python
from contextlib import ExitStack

import concourse.bass as bass
from concourse import mybir

F32 = mybir.dt.float32
F32R = mybir.dt.float32r
BF16 = mybir.dt.bfloat16
U8 = mybir.dt.uint8
ALU = mybir.AluOpType
ACT = mybir.ActivationFunctionType
AX_X = mybir.AxisListType.X

P = 128
NSEQ = 32
GS = 4
NG = NSEQ // GS
GT = GS * P
D_INNER = 256
HEADS = 4
HD = D_INNER // HEADS
ROT = 32
PLAIN = P - ROT
SMALL = 3 * HEADS + ROT
O_Z, O_X, O_B, O_C, O_S = 0, 256, 512, 640, 768
A_FLOOR = 1e-4
LN_EPS = 1e-5
ROUND = 12582912.0
TWO_PI = 6.283185
NEG = -30000.0

XH = 16
XD = P // XH
MASKED = -1.0e15
EXPERTS = 16
EI = 64
CHUNKS = EXPERTS * EI // P
SCALE = 2.5


class Sem:

    def __init__(self, ctx, nc, name, n=1, by=1):
        self.sem = ctx.enter_context(nc.semaphore(name))
        self.n, self.by = n, by

    def prime(self, eng):
        eng.sem_inc(self.sem, 2 * self.n * self.by)

    def at(self, g, k=0):
        return (g * self.n + (2 * self.n + k + 1)) * self.by


class DmaSem:

    def __init__(self, ctx, nc, name, dmas=1):
        self.sem = [ctx.enter_context(nc.semaphore(f"{name}{k}")) for k in range(2)]
        self.step = 16 * dmas

    def prime(self, eng):
        for s in self.sem:
            eng.sem_inc(s, self.step)

    def at(self, g, par):
        return g * (self.step // 2) + self.step * (4 - par) // 2


def pairs(eng, group):
    with eng.Fori(0, NG // 2 - 1) as i:
        group(2 * i, 0, False)
        group(2 * i + 1, 1, False)
    group(NG - 2, 0, False)
    group(NG - 1, 1, True)


def bc(ap, shape):
    return ap.to_broadcast(shape)


def residual_dve(dve, g, bank, other, used, done, passed, res, stats, mv, times=1.0):
    dve.wait_ge(used.sem, used.at(g - 1, GS - 1))
    dve.scalar_tensor_tensor(res[:, :, :], other, times, bank[:, :].rearrange("p (b d) -> p b d", b=GS), ALU.mult, ALU.add)\
        .then_inc(done.sem, 1)
    dve.wait_ge(done.sem, done.at(g, 0))
    for b in range(GS):
        dve.bn_stats(stats[:, b, :], res[:, b, :]).then_inc(done.sem, 1)
    dve.wait_ge(done.sem, done.at(g, GS))
    dve.sem_inc(passed, 1)
    for b in range(GS):
        dve.bn_aggr(mv[:, b, :], stats[:, b, :]).then_inc(done.sem, 1)


def normalise_pool(pool, g, res_ready, used, done, mv, rstd, nmean, norm_c):
    pool.wait_ge(res_ready.sem, res_ready.at(g, 2 * GS))
    pool.wait_ge(used.sem, used.at(g - 1, GS - 1))
    pool.tensor_tensor(rstd[:, :], mv[:, :, 1], norm_c[:, 0, :], ALU.add).then_inc(done.sem, 1)
    pool.wait_ge(done.sem, done.at(g, 0))
    pool.tensor_tensor(nmean[:, :], mv[:, :, 0], norm_c[:, 1, :], ALU.mult).then_inc(done.sem, 1)
    pool.tensor_tensor(rstd[:, :], rstd[:, :], norm_c[:, 2, :], ALU.pow).then_inc(done.sem, 1)
    pool.wait_ge(done.sem, done.at(g, 2))
    pool.tensor_tensor(nmean[:, :], nmean[:, :], rstd[:, :], ALU.mult).then_inc(done.sem, 1)


def mixer(nc, t, d, psum, stop_at):
    with ExitStack() as ctx:
        def sb(name, shape, dt=F32):
            return ctx.enter_context(nc.sbuf_tensor(name, shape, dt))

        def sem(name, n=1, by=1):
            return Sem(ctx, nc, name, n, by)

        ident, ident32, norm_c = t["ident"], t["ident32"], t["norm_c"]
        w_in = sb("w_in", [P, O_S + SMALL])
        w_feat = sb("w_feat", [P, 2, 4, P], F32R)
        w_z = sb("w_z", [P, 2, D_INNER], F32R)
        w_x = sb("w_x", [P, 2, D_INNER], F32R)
        w_dx = sb("w_dx", [P, 2, D_INNER], F32R)
        w_dx32 = sb("w_dx32", [P, D_INNER])
        w_out = sb("w_out", [P, 2, P])
        dt_bias = sb("dt_bias", [P, 2 * HEADS])
        d_skip = sb("d_skip", [P, HEADS])
        upto = sb("upto", [P, P])
        after = sb("after", [P, P], F32R)
        acausal = sb("acausal", [P, P], BF16)
        phase = sb("phase", [P, 1])
        scratch = sb("scratch", [P, P])
        small = sb("small", [P, NSEQ, SMALL])
        soft = sb("soft", [P, NSEQ, 2 * HEADS])
        e8 = sb("e8", [P, NSEQ, 2 * HEADS])
        s8 = sb("s8", [P, NSEQ, 2 * HEADS])
        q8 = sb("q8", [P, NSEQ, 2 * HEADS])
        p8 = sb("p8", [P, NSEQ, 2 * HEADS])
        gate = sb("gate", [P, NSEQ, HEADS])
        ngate = sb("ngate", [P, NSEQ, HEADS])
        gamma = sb("gamma", [P, NSEQ, HEADS])
        beta = sb("beta", [P, NSEQ, HEADS])
        decay = sb("decay", [P, NSEQ, HEADS])
        alpha = sb("alpha", [P, NSEQ, HEADS])
        dec_hl = sb("dec_hl", [P, 2, NSEQ, HEADS])
        dec_r = sb("dec_r", [P, NSEQ, HEADS], F32R)
        half_dt = sb("half_dt", [P, NSEQ, HEADS])
        th = sb("th", [P, NSEQ, ROT])
        trig = sb("trig", [P, 2, NSEQ * P])
        rstd = sb("rstd_e", [P, GS])
        nmean = sb("nmean", [P, GS])

        w_loaded, const = sem("w_loaded", 1, 16), sem("const")
        wprep = sem("wprep")

        with ExitStack() as c1:
            xt = c1.enter_context(nc.sbuf_tensor("xt_small", [P, 2, GT], F32))
            s_xt = [c1.enter_context(nc.semaphore(f"xt_loaded{k}")) for k in range(2)]
            s_mm = c1.enter_context(nc.semaphore("small_mm"))
            s_ev = c1.enter_context(nc.semaphore("small_copied"))
            s_act = c1.enter_context(nc.semaphore("small_act"))
            s_dve = c1.enter_context(nc.semaphore("small_dve"))
            s_pool = c1.enter_context(nc.semaphore("mixer_consts"))
            s_w = c1.enter_context(nc.semaphore("mixer_weights"))
            s_win = c1.enter_context(nc.semaphore("w_in_loaded"))
            block = c1.enter_context(nc.Block())

            @block.sync
            def _(sp):
                sp.dma_start(w_in[:, :], d["w_inT"]).then_inc(s_win, 16)
                for g in range(NG):
                    if g >= 2:
                        sp.wait_ge(s_mm, g - 1)
                    sp.dma_start(xt[:, g % 2, :], d["xT"][:, g * GT:(g + 1) * GT]).then_inc(s_xt[g % 2], 16)

            @block.gpsimd
            def _(pool):
                pool.dma_start(dt_bias[:, 0:HEADS], d["dt_bias"].partition_broadcast(P)).then_inc(s_w, 16)
                pool.dma_start(d_skip[:, :], d["D"].partition_broadcast(P)).then_inc(s_w, 16)
                pool.dma_start(w_out[:, :, :], d["w_outT"].rearrange("(c k) n -> k c n", k=P)).then_inc(s_w, 16)
                pool.memset(scratch[:, :], 1.0).then_inc(s_pool, 1)
                pool.wait_ge(s_pool, 1)
                pool.affine_select(out=upto[:, :], in_=scratch[:, :], compare_op=ALU.is_ge, fill=0.0, base=0,
                                   pattern=[[1, P]], channel_multiplier=-1).then_inc(s_pool, 1)
                pool.affine_select(out=after[:, :], in_=scratch[:, :], compare_op=ALU.is_gt, fill=0.0, base=0,
                                   pattern=[[-1, P]], channel_multiplier=1).then_inc(s_pool, 1)
                pool.affine_select(out=ident[:, :], in_=scratch[:, :], compare_op=ALU.is_equal, fill=0.0, base=0,
                                   pattern=[[1, P]], channel_multiplier=-1).then_inc(s_pool, 1)
                pool.affine_select(out=ident32[:, :], in_=scratch[:, :], compare_op=ALU.is_equal, fill=0.0, base=0,
                                   pattern=[[1, P]], channel_multiplier=-1).then_inc(s_pool, 1)
                for k, value in enumerate((LN_EPS, -1.0, -0.5)):
                    pool.memset(norm_c[:, k, :], value).then_inc(s_pool, 1)
                pool.wait_ge(s_pool, 5)
                pool.memset(scratch[:, :], 0.0).then_inc(s_pool, 1)
                pool.wait_ge(s_pool, 9)
                pool.affine_select(out=acausal[:, :], in_=scratch[:, :], compare_op=ALU.is_ge, fill=NEG, base=0,
                                   pattern=[[1, P]], channel_multiplier=-1).then_inc(s_pool, 1)

            @block.tensor
            def _(pe):
                pe.wait_ge(s_win, 16)
                for g in range(NG):
                    pe.wait_ge(s_xt[g % 2], 16 * (g // 2 + 1))
                    if g >= 2:
                        pe.wait_ge(s_ev, g - 1)
                    for b in range(GS):
                        mm = pe.matmul(psum[g % 2][:, b * SMALL:(b + 1) * SMALL], xt[:, g % 2, b * P:(b + 1) * P],
                                       w_in[:, O_S:], start=True, stop=True)
                    mm.then_inc(s_mm, 1)

            @block.scalar
            def _(act):
                for g in range(NG):
                    act.wait_ge(s_mm, g + 1)
                    act.activation(small[:, g * GS:(g + 1) * GS, :], psum[g % 2][:, 0:GS * SMALL], ACT.Copy).then_inc(s_ev, 1)
                act.wait_ge(s_ev, NG)
                act.activation(th[:, :, :], small[:, :, 12:SMALL], ACT.Tanh).then_inc(s_act, 1)
                act.activation(ngate[:, :, :], small[:, :, 8:12], ACT.Exp, scale=-1.0).then_inc(s_act, 1)
                act.wait_ge(s_dve, 2)
                act.activation(e8[:, :, :], soft[:, :, :], ACT.Abs).then_inc(s_act, 1)
                act.wait_ge(s_act, 3)
                act.activation(e8[:, :, :], e8[:, :, :], ACT.Exp, scale=-1.0).then_inc(s_act, 1)
                act.wait_ge(s_dve, 21)
                act.activation(alpha[:, :, :], decay[:, :, :], ACT.Exp).then_inc(s_act, 1)

            @block.vector
            def _(dve):
                steps = [0]

                def link(ins):
                    steps[0] += 1
                    ins.then_inc(s_dve, 1)
                    dve.wait_ge(s_dve, steps[0])

                link(dve.memset(dt_bias[:, HEADS:], 0.0))
                for h in range(2):
                    dve.memset(phase[64 * h:64 * h + 32, :], 0.25)
                    dve.memset(phase[64 * h + 32:64 * h + 64, :], 0.0)
                dve.wait_ge(s_ev, NG)
                dve.wait_ge(s_w, 48)
                link(dve.tensor_tensor(soft[:, :, :], small[:, :, 0:8], bc(dt_bias[:, None, :], [P, NSEQ, 8]), ALU.add))
                dve.wait_ge(s_act, 4)
                link(dve.tensor_scalar(s8[:, :, :], e8[:, :, :], 2.0, None, ALU.add))
                link(dve.reciprocal(q8[:, :, :], s8[:, :, :]))
                link(dve.tensor_tensor(s8[:, :, :], e8[:, :, :], q8[:, :, :], ALU.mult))
                link(dve.tensor_tensor(p8[:, :, :], s8[:, :, :], s8[:, :, :], ALU.mult))
                link(dve.tensor_scalar(q8[:, :, :], p8[:, :, :], 1.0 / 17, None, ALU.mult))
                for k in range(7, 0, -1):
                    link(dve.scalar_tensor_tensor(q8[:, :, :], q8[:, :, :], 1.0 / (2 * k + 1), p8[:, :, :], ALU.add, ALU.mult))
                link(dve.scalar_tensor_tensor(q8[:, :, :], q8[:, :, :], 1.0, s8[:, :, :], ALU.add, ALU.mult))
                link(dve.tensor_scalar(p8[:, :, :], soft[:, :, :], 0.0, None, ALU.max))
                link(dve.scalar_tensor_tensor(soft[:, :, :], q8[:, :, :], 2.0, p8[:, :, :], ALU.mult, ALU.add))
                link(dve.tensor_scalar(decay[:, :, :], soft[:, :, 4:8], -1.0, -A_FLOOR, ALU.mult, ALU.min))
                link(dve.tensor_scalar(gate[:, :, :], ngate[:, :, :], 1.0, None, ALU.add))
                link(dve.tensor_scalar(half_dt[:, :, :], soft[:, :, 0:4], 0.5, None, ALU.mult))
                link(dve.tensor_tensor(decay[:, :, :], decay[:, :, :], soft[:, :, 0:4], ALU.mult))
                assert steps[0] == 21, steps
                link(dve.reciprocal(gate[:, :, :], gate[:, :, :]))
                link(dve.tensor_tensor(gamma[:, :, :], gate[:, :, :], soft[:, :, 0:4], ALU.mult))
                link(dve.tensor_scalar(ngate[:, :, :], gate[:, :, :], -1.0, 1.0, ALU.mult, ALU.add))
                link(dve.tensor_tensor(beta[:, :, :], ngate[:, :, :], soft[:, :, 0:4], ALU.mult))
                dve.wait_ge(s_act, 5)
                link(dve.tensor_tensor(beta[:, :, :], beta[:, :, :], alpha[:, :, :], ALU.mult))
                link(dve.tensor_copy(dec_r[:, :, :], decay[:, :, :]))
                link(dve.tensor_copy(dec_hl[:, 0, :, :], dec_r[:, :, :].bitcast(F32)))
                link(dve.tensor_tensor(dec_hl[:, 1, :, :], decay[:, :, :], dec_hl[:, 0, :, :], ALU.subtract))
                dve.wait_ge(s_win, 16)
                link(dve.tensor_tensor(w_dx32[:, :].rearrange("p (h e) -> p h e", h=HEADS),
                                       w_in[:, O_X:O_X + D_INNER].rearrange("p (h e) -> p h e", h=HEADS),
                                       bc(d_skip[:, :, None], [P, HEADS, HD]), ALU.mult))
                parts = [(w_feat[:, :, c, :].rearrange("p v (h r) -> p v h r", h=4), bc(w_in[:, None, o:o + ROT], [P, 4, ROT]))
                         for c, o in ((0, O_B), (1, O_C))]
                parts += [(w_feat[:, :, c, 0:PLAIN], w_in[:, o + ROT:o + P]) for c, o in ((2, O_B), (3, O_C))]
                parts += [(w_z[:, :, :], w_in[:, O_Z:O_Z + D_INNER]), (w_x[:, :, :], w_in[:, O_X:O_X + D_INNER]),
                          (w_dx[:, :, :], w_dx32[:, :])]
                for w, src in parts:
                    dve.tensor_copy(w[:, 0], src).then_inc(s_dve, 1)
                steps[0] += len(parts)
                dve.wait_ge(s_dve, steps[0])
                for w, src in parts:
                    dve.tensor_tensor(w[:, 1], src, w[:, 0].bitcast(F32), ALU.subtract).then_inc(s_dve, 1)

        if stop_at == "small":
            return

        with ExitStack() as c2:
            turns = c2.enter_context(nc.sbuf_tensor("turns", [P, 2, GS, HEADS, 2, ROT], F32))
            ang = c2.enter_context(nc.sbuf_tensor("ang", [P, 4, GT], F32))
            whole = c2.enter_context(nc.sbuf_tensor("whole", [P, 4, GT], F32))
            frac = c2.enter_context(nc.sbuf_tensor("frac", [P, 4, GT], F32))
            t_turns, t_mm = Sem(c2, nc, "turns_ready", 2), Sem(c2, nc, "theta_ready", 2)
            t_ang, t_whole = Sem(c2, nc, "ang_ready", 2), Sem(c2, nc, "whole_ready", 2)
            t_frac, t_trig = Sem(c2, nc, "frac_ready", 2), Sem(c2, nc, "trig_ready", 2)
            block = c2.enter_context(nc.Block())

            @block.vector
            def _(dve):
                for s in (t_turns, t_whole, t_frac):
                    s.prime(dve)

                def angles(g, par):
                    dve.wait_ge(t_mm.sem, t_mm.at(g - 2, 1))
                    for cs in range(2):
                        dve.tensor_tensor(turns[:, par, :, :, cs, :],
                                          bc(th[:, bass.ds(g * GS, GS), None, :], [P, GS, HEADS, ROT]),
                                          bc(half_dt[:, bass.ds(g * GS, GS), :, None], [P, GS, HEADS, ROT]),
                                          ALU.mult).then_inc(t_turns.sem, 1)

                def group(g, par, last):
                    for k in range(2):
                        j = 2 * par + k
                        dve.wait_ge(t_ang.sem, t_ang.at(g, k))
                        dve.wait_ge(t_frac.sem, t_frac.at(g - 2, k))
                        dve.tensor_scalar(whole[:, j, :], ang[:, j, :], ROUND, -ROUND, ALU.add, ALU.add).then_inc(t_whole.sem, 1)
                        dve.wait_ge(t_whole.sem, t_whole.at(g, k))
                        dve.wait_ge(t_trig.sem, t_trig.at(g - 2, k))
                        dve.tensor_tensor(frac[:, j, :], ang[:, j, :], whole[:, j, :], ALU.subtract).then_inc(t_frac.sem, 1)
                    if not last:
                        angles(g + 1, 1 - par)

                angles(0, 0)
                pairs(dve, group)

            @block.tensor
            def _(pe):
                t_mm.prime(pe)

                def group(g, par, last):
                    pe.wait_ge(t_turns.sem, t_turns.at(g, 1))
                    for k in range(2):
                        pe.wait_ge(t_ang.sem, t_ang.at(g - 2, k))
                        for b in range(GS):
                            mm = pe.matmul(psum[2 * par + k][:, b * P:(b + 1) * P],
                                           turns[:, par, b, 2 * k:2 * k + 2, :, :].rearrange("p h c r -> p (h c r)"),
                                           upto[:, :], start=True, stop=True)
                        mm.then_inc(t_mm.sem, 1)

                pairs(pe, group)

            @block.scalar
            def _(act):
                for s in (t_ang, t_trig):
                    s.prime(act)

                def group(g, par, last):
                    for k in range(2):
                        act.wait_ge(t_mm.sem, t_mm.at(g, k))
                        act.wait_ge(t_frac.sem, t_frac.at(g - 2, k))
                        act.activation(ang[:, 2 * par + k, :], psum[2 * par + k][:, :], ACT.Identity,
                                       bias=phase[:, 0:1]).then_inc(t_ang.sem, 1)
                    for k in range(2):
                        act.wait_ge(t_frac.sem, t_frac.at(g, k))
                        act.activation(trig[:, k, bass.ds(g * GT, GT)], frac[:, 2 * par + k, :], ACT.Sin,
                                       scale=TWO_PI).then_inc(t_trig.sem, 1)

                pairs(act, group)

        if stop_at == "trig":
            return

        xin = sb("xin", [P, 2, GS, P + 1])
        xhl = sb("xhl", [P, 2, 2, GS, P + 1], F32R)
        xres = sb("xres", [P, 2, GS, P])
        b_rot = sb("b_rot", [P, 2, 2, GT])
        c_rot = sb("c_rot", [P, 2, 2, GT])
        plain = sb("plain", [PLAIN, 2, 2, 2, GT], F32R)
        tz = sb("tz", [P, 2, 2, GT])
        ramp = sb("ramp", [P, 2, 2, HEADS, P], F32R)
        expo = sb("expo", [P, 2, HEADS, P])
        mix = sb("mix", [P, 2, HEADS, P])
        xg = sb("xg", [P, 2, D_INNER])
        w_tok = sb("w_tok", [P, 2, D_INNER])
        y = sb("y", [P, 2, GT])
        res = sb("res", [P, GS, P])
        stats = sb("stats", [P, GS, 6])
        mv = sb("mv", [P, GS, 2])
        x1 = t["x1"]

        s_xt, s_x = DmaSem(ctx, nc, "xT_in"), DmaSem(ctx, nc, "x_in")
        s_hi, s_lo = sem("x_hi"), sem("x_lo")
        s_feat = sem("feat_mm", 6)
        s_hiz = sem("feat_act", 4)
        s_prod = sem("feat_dve", 8)
        s_ramp = sem("ramp_ready", 8)
        s_dec = sem("decay_mm", GS)
        s_xx = sem("x_mm", GS)
        s_g = sem("g_mm", 2 * GS)
        s_exp = sem("expo_ready", GS)
        s_w = sem("w_ready", 3 * GS)
        s_mix = sem("mix_ready", GS)
        s_y = sem("y_mm", GS)
        s_yg = sem("y_gated", 2)
        s_o = sem("out_mm")
        s_res = sem("res_ready", 1 + 2 * GS)
        s_var = sem("rstd_ready", 4)
        s_x1 = sem("x1_ready", GS)
        s_zero = ctx.enter_context(nc.semaphore("x_zero_columns"))
        dve_passed = ctx.enter_context(nc.semaphore("mixer_dve_passed"))
        P0, P1, PX, PD, PG, PY0, PY1, PO = psum
        block = ctx.enter_context(nc.Block())

        @block.sync
        def _(sp):
            s_xt.prime(sp)
            s_x.prime(sp)

            def group(g, par, last):
                sp.wait_ge(s_lo.sem, s_lo.at(g - 2))
                sp.dma_start(xin[:, par, :, 1:], d["xT"].rearrange("p (b t) -> p b t", t=P)[:, bass.ds(g * GS, GS), :])\
                    .then_inc(s_xt.sem[par], 16)
                sp.wait_ge(s_res.sem, s_res.at(g - 2, 0))
                sp.dma_start(xres[:, par, :, :], d["x"].rearrange("(b t) d -> t b d", t=P)[:, bass.ds(g * GS, GS), :])\
                    .then_inc(s_x.sem[par], 16)

            pairs(sp, group)

        @block.scalar
        def _(act):
            for s in (s_hi, s_hiz, s_exp, s_x1):
                s.prime(act)

            def split(g, par):
                act.wait_ge(s_xt.sem[par], s_xt.at(g, par))
                act.wait_ge(s_y.sem, s_y.at(g - 2, 3))
                act.activation(xhl[:, par, 0, :, :], xin[:, par, :, :], ACT.Copy).then_inc(s_hi.sem, 1)

            def features(g, par):
                for k in range(2):
                    act.wait_ge(s_feat.sem, s_feat.at(g, 2 + k))
                    act.wait_ge(s_g.sem, s_g.at(g - 2, 7))
                    act.activation(plain[:, par, k, 0, :], (P0, P1)[k][0:PLAIN, :], ACT.Copy).then_inc(s_hiz.sem, 1)
                for k in range(2):
                    act.wait_ge(s_feat.sem, s_feat.at(g, 4 + k))
                    act.wait_ge(s_yg.sem, s_yg.at(g - 1, k))
                    act.activation(tz[:, 0, k, :], (P0, P1)[k][:, :], ACT.Tanh, scale=0.5).then_inc(s_hiz.sem, 1)

            def group(g, par, last):
                if not last:
                    split(g + 1, 1 - par)
                for b in range(GS):
                    act.wait_ge(s_dec.sem, s_dec.at(g, b))
                    act.wait_ge(s_mix.sem, s_mix.at(g, b - 2))
                    act.activation(expo[:, b % 2, :, :], PD[:, :], ACT.Exp).then_inc(s_exp.sem, 1)
                if not last:
                    features(g + 1, 1 - par)
                act.wait_ge(s_var.sem, s_var.at(g, 3))
                for b in range(GS):
                    act.activation(x1[:, bass.ds(g * GS + b, 1), :], res[:, b, :], ACT.Identity,
                                   bias=nmean[:, b:b + 1], scale=rstd[:, b:b + 1]).then_inc(s_x1.sem, 1)

            act.wait_ge(s_zero, 1)
            split(0, 0)
            features(0, 0)
            pairs(act, group)

        @block.gpsimd
        def _(pool):
            for s in (s_ramp, s_var):
                s.prime(pool)

            def group(g, par, last):
                for b in range(GS):
                    pool.wait_ge(s_dec.sem, s_dec.at(g, b - 2))
                    for v in range(2):
                        pool.tensor_tensor(ramp[:, b % 2, v, :, :], bc(upto[:, None, :], [P, HEADS, P]),
                                           bc(dec_hl[:, v, bass.ds(g * GS + b, 1), :].rearrange("p o h -> p (o h)")[:, :, None],
                                              [P, HEADS, P]), ALU.mult).then_inc(s_ramp.sem, 1)
                normalise_pool(pool, g, s_res, s_x1, s_var, mv, rstd, nmean, norm_c)

            pairs(pool, group)

        @block.vector
        def _(dve):
            dve.memset(xin[:, :, :, 0:1], 0.0).then_inc(s_zero, 1)
            for s in (s_lo, s_prod, s_w, s_mix, s_yg, s_res):
                s.prime(dve)

            def split(g, par):
                dve.wait_ge(s_hi.sem, s_hi.at(g))
                dve.tensor_tensor(xhl[:, par, 1, :, :], xin[:, par, :, :], xhl[:, par, 0, :, :].bitcast(F32), ALU.subtract)\
                    .then_inc(s_lo.sem, 1)

            def features(g, par):
                for c, rot in ((0, b_rot), (1, c_rot)):
                    dve.wait_ge(s_feat.sem, s_feat.at(g, c))
                    dve.wait_ge(s_g.sem, s_g.at(g - 2, 7))
                    for k in range(2):
                        dve.tensor_tensor(rot[:, par, k, :], (P0, P1)[c][:, :], trig[:, k, bass.ds(g * GT, GT)], ALU.mult)\
                            .then_inc(s_prod.sem, 1)
                for k in range(2):
                    dve.wait_ge(s_hiz.sem, s_hiz.at(g, k))
                    dve.tensor_tensor(plain[:, par, k, 1, :], (P0, P1)[k][0:PLAIN, :], plain[:, par, k, 0, :].bitcast(F32),
                                      ALU.subtract).then_inc(s_prod.sem, 1)
                for k in range(2):
                    dve.wait_ge(s_hiz.sem, s_hiz.at(g, 2 + k))
                    dve.wait_ge(s_yg.sem, s_yg.at(g - 1, k))
                    dve.scalar_tensor_tensor(tz[:, 1, k, :], tz[:, 0, k, :], 1.0, (P0, P1)[k][:, :], ALU.add, ALU.mult)\
                        .then_inc(s_prod.sem, 1)

            def inputs_of(g, b):
                dve.wait_ge(s_xx.sem, s_xx.at(g, b))
                heads = lambda ap: ap.rearrange("p (h e) -> p h e", h=HEADS)
                of = lambda co: bc(co[:, bass.ds(g * GS + b, 1), :].rearrange("p o h -> p (o h)")[:, :, None], [P, HEADS, HD])
                dve.wait_ge(s_w.sem, s_w.at(g, 3 * b - 1))
                dve.tensor_tensor(heads(xg[:, 0, :]), heads(PX[:, 0:D_INNER]), of(gamma), ALU.mult).then_inc(s_w.sem, 1)
                dve.tensor_tensor(heads(xg[:, 1, :]), heads(PX[:, D_INNER:]), of(beta), ALU.mult).then_inc(s_w.sem, 1)
                dve.wait_ge(s_w.sem, s_w.at(g, 3 * b + 1))
                dve.wait_ge(s_y.sem, s_y.at(g, b - 2))
                dve.tensor_tensor(w_tok[:, b % 2, :], xg[:, 0, :], xg[:, 1, :], ALU.add).then_inc(s_w.sem, 1)

            def group(g, par, last):
                if not last:
                    split(g + 1, 1 - par)
                for b in range(GS):
                    inputs_of(g, b)
                    dve.wait_ge(s_g.sem, s_g.at(g, 2 * b + 1))
                    dve.wait_ge(s_exp.sem, s_exp.at(g, b))
                    dve.wait_ge(s_y.sem, s_y.at(g, b - 2))
                    dve.tensor_tensor(mix[:, b % 2, :, :], PG[:, :].rearrange("p (h t) -> p h t", h=HEADS),
                                      expo[:, b % 2, :, :], ALU.mult).then_inc(s_mix.sem, 1)
                dve.wait_ge(s_y.sem, s_y.at(g, 3))
                dve.wait_ge(s_o.sem, s_o.at(g - 1))
                dve.wait_ge(s_prod.sem, s_prod.at(g, 7))
                for k in range(2):
                    dve.scalar_tensor_tensor(y[:, k, :], tz[:, 1, k, :], 0.5, (PY0, PY1)[k][:, :], ALU.mult, ALU.mult)\
                        .then_inc(s_yg.sem, 1)
                if not last:
                    features(g + 1, 1 - par)
                dve.wait_ge(s_o.sem, s_o.at(g))
                dve.wait_ge(s_x.sem[par], s_x.at(g, par))
                residual_dve(dve, g, PO, xres[:, par, :, :], s_x1, s_res, dve_passed, res, stats, mv)

            split(0, 0)
            features(0, 0)
            pairs(dve, group)

        @block.tensor
        def _(pe):
            for s in (s_feat, s_dec, s_xx, s_g, s_y, s_o):
                s.prime(pe)

            def features(g, par):
                pe.wait_ge(s_lo.sem, s_lo.at(g))
                freed = [None, None, (s_prod, 1), (s_prod, 3), (s_prod, 4), (s_prod, 5)]
                for c in range(6):
                    bank = (P0, P1)[c % 2]
                    if freed[c]:
                        pe.wait_ge(freed[c][0].sem, freed[c][0].at(g, freed[c][1]))
                    else:
                        pe.wait_ge(s_prod.sem, s_prod.at(g - 1, 6 + c))
                    m = (P, P, PLAIN, PLAIN, P, P)[c]
                    w = w_feat[:, :, c, 0:m] if c < 4 else w_z[:, :, (c - 4) * P:(c - 3) * P]
                    for n, (a, v) in enumerate(((0, 0), (0, 1), (1, 0))):
                        mm = pe.matmul(bank[0:m, :], w[:, a, :], xhl[:, par, v, :, 1:], start=(n == 0), stop=(n == 2))
                    mm.then_inc(s_feat.sem, 1)

            def front(g, par, b):
                pe.wait_ge(s_ramp.sem, s_ramp.at(g, 2 * b + 1))
                pe.wait_ge(s_exp.sem, s_exp.at(g, b - 1))
                for v in range(2):
                    pe.matmul(PD[:, :], after[:, :], ramp[:, b % 2, v, :, :], start=(v == 0), stop=False)
                pe.matmul(PD[:, :], ident[:, :], bc(acausal[:, None, :], [P, HEADS, P]), start=False, stop=True)\
                    .then_inc(s_dec.sem, 1)
                pe.wait_ge(s_w.sem, s_w.at(g, 3 * b - 2))
                tokens(par, b, 0)

            def tokens(par, b, shift):
                for n, (a, v) in enumerate(((0, 0), (0, 1), (1, 0))):
                    mm = pe.matmul(PX[:, shift * D_INNER:(shift + 1) * D_INNER], xhl[:, par, a, b, 1 - shift:P + 1 - shift],
                                   w_x[:, v, :], start=(n == 0), stop=(n == 2))
                return mm

            def scores(g, par, b):
                pe.wait_ge(s_mix.sem, s_mix.at(g, b - 1))
                tok = slice(b * P, (b + 1) * P)
                for n, (a, v) in enumerate(((0, 0), (0, 1), (1, 0))):
                    pe.matmul(PG[:, :], plain[:, par, 0, a, tok], bc(plain[:, par, 1, v, None, tok], [PLAIN, HEADS, P]),
                              start=(n == 0), stop=False, skip_group_check=True)
                for half in range(2):
                    rows = slice(64 * half, 64 * half + 64)
                    for k in range(2):
                        h = 2 * k + half
                        mm = pe.matmul(PG[:, h * P:(h + 1) * P], b_rot[rows, par, k, tok], c_rot[rows, par, k, tok],
                                       start=False, stop=True, skip_group_check=True)
                    mm.then_inc(s_g.sem, 1)
                    if half == 0:
                        tokens(par, b, 1).then_inc(s_xx.sem, 1)
                        pe.wait_ge(s_g.sem, s_g.at(g, 2 * b))

            def skip(g, par):
                for k in range(2):
                    pe.wait_ge(s_yg.sem, s_yg.at(g - 1, k))
                    for n, (a, v) in enumerate(((0, 0), (0, 1), (1, 0))):
                        pe.matmul((PY0, PY1)[k][:, :], w_dx[:, a, k * P:(k + 1) * P], xhl[:, par, v, :, 1:],
                                  start=(n == 0), stop=False, skip_group_check=True)

            def back(g, b):
                pe.wait_ge(s_mix.sem, s_mix.at(g, b))
                pe.wait_ge(s_w.sem, s_w.at(g, 3 * b + 2))
                for h in range(HEADS):
                    mm = pe.matmul((PY0, PY1)[h // 2][64 * (h % 2):64 * (h % 2) + 64, b * P:(b + 1) * P],
                                   w_tok[:, b % 2, h * HD:(h + 1) * HD], mix[:, b % 2, h, :],
                                   start=False, stop=True, skip_group_check=True)
                mm.then_inc(s_y.sem, 1)

            def group(g, par, last):
                pe.wait_ge(s_prod.sem, s_prod.at(g, 5))
                front(g, par, 0)
                scores(g, par, 0)
                skip(g, par)
                for b in range(1, GS):
                    front(g, par, b)
                    back(g, b - 1)
                    scores(g, par, b)
                back(g, GS - 1)
                if not last:
                    features(g + 1, 1 - par)
                pe.wait_ge(s_yg.sem, s_yg.at(g, 1))
                pe.wait_ge(s_res.sem, s_res.at(g - 1, 0))
                for b in range(GS):
                    for k in range(2):
                        mm = pe.matmul(PO[:, b * P:(b + 1) * P], y[:, k, b * P:(b + 1) * P], w_out[:, k, :],
                                       start=(k == 0), stop=(k == 1))
                mm.then_inc(s_o.sem, 1)

            features(0, 0)
            pairs(pe, group)


def attention(nc, t, d, psum):
    PAIRS = ((0, 0), (0, 1), (1, 0), (1, 1), (0, 2), (2, 0))
    NROW = len(PAIRS) * XD
    UNITS = 4
    DIAG = P + XD
    with ExitStack() as ctx:
        def sb(name, shape, dt=F32):
            return ctx.enter_context(nc.sbuf_tensor(name, shape, dt))

        def sem(name, n=1, by=1):
            return Sem(ctx, nc, name, n, by)

        def raw(name):
            return ctx.enter_context(nc.semaphore(name))

        wqk = sb("wqk", [P, 2, P])
        wqk_hl = sb("wqk_hl", [P, 2, 2, P], F32R)
        w_v, w_o = sb("w_v", [P, P]), sb("w_o", [P, P])
        bqk = sb("bqk", [P, 2])
        b_v, b_o = sb("b_v", [P, P]), sb("b_o", [P, P])
        neg_i = sb("neg_i", [P, P], BF16)
        zeros = sb("zeros", [P, P])
        ones_d = sb("ones_d", [P, UNITS * DIAG])
        cin = sb("cin", [P, 2, GT])
        c_hl = sb("c_hl", [P, 2, GT], F32R)
        mask8 = sb("mask8", [P, 2, GS, P], U8)
        mask = sb("mask", [P, 2, GS, P], BF16)
        xs = sb("xs", [P, 2, GS, P])
        xT_hl = sb("xT_hl", [P, 2, GT], F32R)
        q_part, k_part = sb("q_part", [P, 3, GT], BF16), sb("k_part", [P, 3, GT], BF16)
        rest = sb("rest", [P, 2, GT])
        q_stack, k_stack = sb("q_stack", [P, 2, 8, GT], BF16), sb("k_stack", [P, 2, 8, GT], BF16)
        v_d = sb("v_d", [P, 2, GS, UNITS * DIAG])
        nmax = sb("nmax", [P, GS, XH])
        nrest = sb("nrest", [P, GS, XH])
        npart = sb("npart", [P, GS, 2, 3, 8], BF16)
        nmT = sb("nmT", [48, GT], BF16)
        prob = sb("prob", [P, 2, UNITS, UNITS, P])
        recip = sb("recip", [P, 2, P])
        ctxT = sb("ctxT", [P, GS, P])
        xb = sb("xb", [P, GS, P])
        res = sb("res_b", [P, GS, P])
        stats, mv = sb("stats_b", [P, GS, 6]), sb("mv_b", [P, GS, 2])
        rstd, nmean = sb("rstd_b", [P, GS]), sb("nmean_b", [P, GS])
        x1, x2, ident, ident32, norm_c = (t[k] for k in ("x1", "x2", "ident", "ident32", "norm_c"))

        d_c, d_mask, d_xs = DmaSem(ctx, nc, "ctx_in"), DmaSem(ctx, nc, "mask_in"), DmaSem(ctx, nc, "x1_staged")
        d_k, d_q = DmaSem(ctx, nc, "k_stacked", 12), DmaSem(ctx, nc, "q_stacked", 12)
        d_m = [DmaSem(ctx, nc, f"max_stacked{h}_", 2) for h in range(2)]
        d_ks, d_qs = DmaSem(ctx, nc, "k_stored"), DmaSem(ctx, nc, "q_stored")
        d_ms = [DmaSem(ctx, nc, f"max_stored{h}_") for h in range(2)]
        k_dram = nc.dram_tensor("k_scratch", (2, P, 3, GT), BF16, kind="Internal").ap()
        q_dram = nc.dram_tensor("q_scratch", (2, P, 3, GT), BF16, kind="Internal").ap()
        m_dram = nc.dram_tensor("max_scratch", (2, 2, 48, 2 * P), BF16, kind="Internal").ap()
        a_c, a_mask, a_x = sem("ctx_hi"), sem("mask_ready"), sem("x1T_hi")
        a_k, a_q = sem("k_act", 2), sem("q_act", 2)
        a_exp, a_mt, a_out = sem("prob_ready", 4 * GS), sem("nmT_ready", 2), sem("x2_ready", GS)
        v_c, v_x, v_k, v_q = sem("ctx_lo"), sem("x1T_lo"), sem("k_dve", 2), sem("q_dve", 2)
        v_v, v_norm, v_max = sem("v_ready", GS), sem("ctx_norm", 2 * GS), sem("max_ready", 4 * GS)
        v_split, v_res = sem("max_parts", 8), sem("res_b_ready", 1 + 2 * GS)
        p_x, p_k, p_q, p_v = sem("x1T_mm"), sem("k_mm"), sem("q_mm"), sem("v_mm")
        p_s, p_t, p_u = sem("score_mm", 4 * GS), sem("scoreT_mm", 4 * GS), sem("pv_mm", GS)
        p_mt, p_o = sem("max_mm", 2), sem("out_b_mm")
        g_x, g_var = sem("x1_biased"), sem("rstd_b_ready", 4)
        g_init, v_init, d_w = raw("att_pool_init"), raw("att_dve_init"), raw("att_weights")
        sp_passed, dve_passed, pe_passed = raw("att_sp_passed"), raw("att_dve_passed"), raw("att_pe_passed")

        with nc.Block() as block:
            @block.sync
            def _(sp):
                for dst, src in ((wqk[:, 0, :], d["Wq"]), (wqk[:, 1, :], d["Wk"]), (w_v[:, :], d["Wv"]), (w_o[:, :], d["Wo"]),
                                 (bqk[:, 0:1], d["bq"].rearrange("(p o) -> p o", o=1)),
                                 (bqk[:, 1:2], d["bk"].rearrange("(p o) -> p o", o=1))):
                    sp.dma_start(dst, src).then_inc(d_w, 16)
                sp.dma_start(b_v[:, :], d["bv"].partition_broadcast(P)).then_inc(d_w, 16)
                sp.dma_start(b_o[:, :], d["bo"].partition_broadcast(P)).then_inc(d_w, 16)
                sp.wait_ge(d_w, 8 * 16)

            @block.gpsimd
            def _(pool):
                pool.memset(zeros[:, :], 0.0).then_inc(g_init, 1)
                pool.wait_ge(g_init, 1)
                pool.affine_select(out=neg_i[:, :], in_=zeros[:, :], compare_op=ALU.not_equal, fill=MASKED, base=0,
                                   pattern=[[1, P]], channel_multiplier=-1).then_inc(g_init, 1)

            @block.vector
            def _(dve):
                dve.memset(k_stack[:, :, :, :], 1.0)
                dve.memset(ones_d[:, :], 0.0).then_inc(v_init, 1)
                dve.memset(v_d[:, :, :, :], 0.0)
                dve.wait_ge(v_init, 1)
                dve.memset(ones_d[:, :].rearrange("p (i c) -> p i c", i=UNITS)[:, :, 0:P]
                           .rearrange("p i (c e) -> p i c e", e=4 * XD)[:, :, :, 0:XD], 1.0)
                dve.wait_ge(d_w, 8 * 16)
                dve.tensor_copy(wqk_hl[:, :, 0, :], wqk[:, :, :]).then_inc(v_init, 1)
                dve.wait_ge(v_init, 2)
                dve.tensor_tensor(wqk_hl[:, :, 1, :], wqk[:, :, :], wqk_hl[:, :, 0, :].bitcast(F32), ALU.subtract)

        TT0, TT1, SS0, SS1, U0, U1, PF, PO = psum
        block = ctx.enter_context(nc.Block())

        def unit_rows(u):
            return 64 * (u // 2), 4 * (u % 2)

        @block.sync
        def _(sp):
            for s in (d_c, d_mask, d_xs, d_k, d_q, *d_m, d_ks, d_qs, *d_ms):
                s.prime(sp)

            def loads(g, par):
                sp.wait_ge(p_v.sem, p_v.at(g - 2))
                sp.dma_start(cin[:, par, :], d["ctxT"][:, bass.ds(g * GT, GT)]).then_inc(d_c.sem[par], 16)
                sp.wait_ge(p_x.sem, p_x.at(g - 2))
                sp.dma_start(xs[:, par, :, :], x1[:, bass.ds(g * GS, GS), :]).then_inc(d_xs.sem[par], 16)
                sp.wait_ge(a_mask.sem, a_mask.at(g - 2))
                sp.dma_start(mask8[:, par, :, :].bitcast(mybir.dt.int32), d["mask"].rearrange("b q k -> q b k")[:, bass.ds(g * GS, GS), :])\
                    .then_inc(d_mask.sem[par], 16)

            def stack(g, par):
                for which, ready, part, via, stored, dst, done in (
                        (1, v_k, k_part, k_dram, d_ks, k_stack, d_k), (0, v_q, q_part, q_dram, d_qs, q_stack, d_q)):
                    sp.wait_ge(ready.sem, ready.at(g, 1))
                    sp.wait_ge(done.sem[par], done.at(g - 2, par))
                    sp.dma_start(via[par], part[:, :, :]).then_inc(stored.sem[par], 16)
                    sp.wait_ge(stored.sem[par], stored.at(g, par))
                    sp.wait_ge(p_t.sem, p_t.at(g - 2, 4 * GS - 1))
                    for j in range(2):
                        for r, pair in enumerate(PAIRS):
                            row = 64 * j + XD * r
                            sp.dma_start(dst[row:row + XD, par, :, :],
                                         via[par, 64 * j:64 * j + 64, pair[which], :].rearrange("(c e) t -> e c t", e=XD))\
                                .then_inc(done.sem[par], 16)

            def maxima(g, par, half):
                sp.wait_ge(a_mt.sem, a_mt.at(g, half))
                sp.sem_inc(sp_passed, 1)
                sp.wait_ge(d_m[half].sem[par], d_m[half].at(g - 2, par))
                tok = slice(half * 2 * P, half * 2 * P + 2 * P)
                sp.dma_start(m_dram[par, half], nmT[:, tok]).then_inc(d_ms[half].sem[par], 16)
                sp.wait_ge(d_ms[half].sem[par], d_ms[half].at(g, par))
                for j in range(2):
                    row = 64 * j + NROW
                    sp.dma_start(q_stack[row:row + 3, par, :, tok],
                                 m_dram[par, half, 24 * j:24 * j + 24, :].rearrange("(r c) t -> r c t", r=3))\
                        .then_inc(d_m[half].sem[par], 16)

            def group(g, par, last):
                if not last:
                    loads(g + 1, 1 - par)
                    stack(g + 1, 1 - par)
                    for half in range(2):
                        maxima(g + 1, 1 - par, half)

            loads(0, 0)
            stack(0, 0)
            for half in range(2):
                maxima(0, 0, half)
            pairs(sp, group)

        @block.gpsimd
        def _(pool):
            g_x.prime(pool)
            g_var.prime(pool)

            def group(g, par, last):
                pool.wait_ge(v_res.sem, v_res.at(g - 1, 0))
                pool.tensor_tensor(xb[:, :, :], x1[:, bass.ds(g * GS, GS), :], bc(b_o[:, None, :], [P, GS, P]), ALU.add)\
                    .then_inc(g_x.sem, 1)
                normalise_pool(pool, g, v_res, a_out, g_var, mv, rstd, nmean, norm_c)

            pairs(pool, group)

        @block.scalar
        def _(act):
            for s in (a_c, a_mask, a_x, a_k, a_q, a_exp, a_mt, a_out):
                s.prime(act)

            def inputs(g, par):
                act.wait_ge(d_c.sem[par], d_c.at(g, par))
                act.wait_ge(p_k.sem, p_k.at(g - 1))
                act.activation(c_hl[:, 0, :], cin[:, par, :], ACT.Copy).then_inc(a_c.sem, 1)
                act.wait_ge(d_mask.sem[par], d_mask.at(g, par))
                act.wait_ge(p_t.sem, p_t.at(g - 2, 4 * GS - 1))
                act.activation(mask[:, par, :, :], mask8[:, par, :, :], ACT.Copy).then_inc(a_mask.sem, 1)
                act.wait_ge(p_x.sem, p_x.at(g))
                act.wait_ge(p_q.sem, p_q.at(g - 1))
                act.activation(xT_hl[:, 0, :], PF[:, :], ACT.Copy).then_inc(a_x.sem, 1)

            def parts(g, par, which, mm, mine, theirs, part, stored):
                act.wait_ge(mm.sem, mm.at(g))
                act.wait_ge(stored.sem[1 - par], stored.at(g - 1, 1 - par))
                act.activation(part[:, 0, :], PF[:, :], ACT.Identity, bias=bqk[:, which:which + 1]).then_inc(mine.sem, 1)
                act.wait_ge(theirs.sem, theirs.at(g, 0))
                act.activation(part[:, 1, :], rest[:, which, :], ACT.Copy).then_inc(mine.sem, 1)

            def exps(g, b):
                for u in range(UNITS):
                    act.wait_ge(p_t.sem, p_t.at(g, 4 * b + u))
                    act.wait_ge(p_u.sem, p_u.at(g, b - 2))
                    act.activation(prob[:, b % 2, u, :, :], (TT0, TT1)[u % 2][:, :], ACT.Exp, scale=XD ** -0.5)\
                        .then_inc(a_exp.sem, 1)

            def maxT(g, par, half):
                act.wait_ge(p_mt.sem, p_mt.at(g, half))
                act.wait_ge(d_ms[half].sem[1 - par], d_ms[half].at(g - 1, 1 - par))
                tok = slice(half * 2 * P, half * 2 * P + 2 * P)
                act.activation(nmT[:, tok], PF[:, :].bitcast(BF16)[0:48, tok], ACT.Copy).then_inc(a_mt.sem, 1)

            def group(g, par, last):
                nxt = (g + 1, 1 - par)
                if not last:
                    inputs(*nxt)
                exps(g, 0)
                if not last:
                    parts(*nxt, 1, p_k, a_k, v_k, k_part, d_ks)
                exps(g, 1)
                if not last:
                    parts(*nxt, 0, p_q, a_q, v_q, q_part, d_qs)
                exps(g, 2)
                exps(g, 3)
                if not last:
                    maxT(*nxt, 0)
                    maxT(*nxt, 1)
                act.wait_ge(g_var.sem, g_var.at(g, 3))
                for b in range(GS):
                    act.activation(x2[:, bass.ds(g * GS + b, 1), :], res[:, b, :], ACT.Identity,
                                   bias=nmean[:, b:b + 1], scale=rstd[:, b:b + 1]).then_inc(a_out.sem, 1)

            inputs(0, 0)
            parts(0, 0, 1, p_k, a_k, v_k, k_part, d_ks)
            parts(0, 0, 0, p_q, a_q, v_q, q_part, d_qs)
            maxT(0, 0, 0)
            maxT(0, 0, 1)
            pairs(act, group)

        @block.vector
        def _(dve):
            for s in (v_c, v_x, v_k, v_q, v_v, v_norm, v_max, v_split, v_res):
                s.prime(dve)

            def inputs(g, par):
                dve.wait_ge(a_c.sem, a_c.at(g))
                dve.tensor_tensor(c_hl[:, 1, :], cin[:, par, :], c_hl[:, 0, :].bitcast(F32), ALU.subtract).then_inc(v_c.sem, 1)
                dve.wait_ge(a_x.sem, a_x.at(g))
                dve.tensor_tensor(xT_hl[:, 1, :], PF[:, :], xT_hl[:, 0, :].bitcast(F32), ALU.subtract).then_inc(v_x.sem, 1)

            def parts(g, which, theirs, mine, part):
                dve.wait_ge(theirs.sem, theirs.at(g, 0))
                dve.scalar_tensor_tensor(rest[:, which, :], PF[:, :], bqk[:, which:which + 1], part[:, 0, :],
                                         ALU.add, ALU.subtract).then_inc(mine.sem, 1)
                dve.wait_ge(theirs.sem, theirs.at(g, 1))
                dve.tensor_tensor(part[:, 2, :], rest[:, which, :], part[:, 1, :], ALU.subtract).then_inc(mine.sem, 1)

            def values(g, par):
                dve.wait_ge(p_v.sem, p_v.at(g))
                dve.wait_ge(p_u.sem, p_u.at(g - 2, GS - 1))
                for b in range(GS):
                    dst = v_d[:, par, b, :].rearrange("p (i c) -> p i c", i=UNITS)[:, :, 0:P]\
                        .rearrange("p i (c e) -> p i c e", e=4 * XD)[:, :, :, 0:XD]
                    dve.tensor_tensor(dst, PF[:, b * P:(b + 1) * P].rearrange("p (c i e) -> p i c e", c=4, i=4),
                                      b_v[:, :].rearrange("p (c i e) -> p i c e", c=4, i=4), ALU.add).then_inc(v_v.sem, 1)

            def maxima(g, b):
                for u in range(UNITS):
                    dve.wait_ge(p_s.sem, p_s.at(g, 4 * b + u))
                    dve.wait_ge(v_split.sem, v_split.at(g - 1, 7))
                    dve.tensor_reduce(nmax[:, b, 4 * u:4 * u + 4], (SS0, SS1)[u % 2][:, :].rearrange("p (i k) -> p i k", i=4),
                                      AX_X, ALU.max, negate=True).then_inc(v_max.sem, 1)

            def split_maxima(g, half):
                bs = slice(2 * half, 2 * half + 2)
                part = lambda r: npart[:, bs, :, r, :]
                of = lambda tile: tile[:, bs, :].rearrange("p b (j c) -> p b j c", j=2)
                dve.wait_ge(v_max.sem, v_max.at(g, 8 * half + 7))
                dve.wait_ge(p_mt.sem, p_mt.at(g - 1, half))
                dve.tensor_copy(part(0), of(nmax)).then_inc(v_split.sem, 1)
                dve.wait_ge(v_split.sem, v_split.at(g, 4 * half))
                dve.tensor_tensor(of(nrest), of(nmax), part(0), ALU.subtract).then_inc(v_split.sem, 1)
                dve.wait_ge(v_split.sem, v_split.at(g, 4 * half + 1))
                dve.tensor_copy(part(1), of(nrest)).then_inc(v_split.sem, 1)
                dve.wait_ge(v_split.sem, v_split.at(g, 4 * half + 2))
                dve.tensor_tensor(part(2), of(nrest), part(1), ALU.subtract).then_inc(v_split.sem, 1)

            def norm(g, b):
                bank = (U0, U1)[b % 2]
                dve.wait_ge(p_u.sem, p_u.at(g, b))
                dve.reciprocal(recip[:, b % 2, :], bank[:, P:2 * P]).then_inc(v_norm.sem, 1)
                dve.wait_ge(v_norm.sem, v_norm.at(g, 2 * b))
                dve.wait_ge(p_o.sem, p_o.at(g - 1))
                dve.tensor_tensor(ctxT[:, b, :], bank[:, 0:P], recip[:, b % 2, :], ALU.mult).then_inc(v_norm.sem, 1)

            def group(g, par, last):
                nxt = (g + 1, 1 - par)
                if not last:
                    inputs(*nxt)
                    parts(g + 1, 1, a_k, v_k, k_part)
                    parts(g + 1, 0, a_q, v_q, q_part)
                norm(g, 0)
                if not last:
                    values(*nxt)
                norm(g, 1)
                if not last:
                    maxima(g + 1, 0)
                    maxima(g + 1, 1)
                    split_maxima(g + 1, 0)
                norm(g, 2)
                if not last:
                    maxima(g + 1, 2)
                norm(g, 3)
                if not last:
                    maxima(g + 1, 3)
                    split_maxima(g + 1, 1)
                dve.wait_ge(p_o.sem, p_o.at(g))
                dve.wait_ge(g_x.sem, g_x.at(g))
                residual_dve(dve, g, PO, xb[:, :, :], a_out, v_res, dve_passed, res, stats, mv)

            inputs(0, 0)
            parts(0, 1, a_k, v_k, k_part)
            parts(0, 0, a_q, v_q, q_part)
            values(0, 0)
            for b in range(GS):
                maxima(0, b)
                if b % 2:
                    split_maxima(0, b // 2)
            pairs(dve, group)

        @block.tensor
        def _(pe):
            for s in (p_x, p_k, p_q, p_v, p_s, p_t, p_u, p_mt, p_o):
                s.prime(pe)

            def x1T(g, par):
                pe.wait_ge(d_xs.sem[par], d_xs.at(g, par))
                pe.wait_ge(a_mt.sem, a_mt.at(g - 1, 1))
                for b in range(GS):
                    mm = pe.transpose(PF[:, b * P:(b + 1) * P], xs[:, par, b, :], ident32[:, :])
                mm.then_inc(p_x.sem, 1)

            def project(g, which, src, ready, freed, done):
                pe.wait_ge(ready.sem, ready.at(g))
                pe.wait_ge(freed.sem, freed.at(g, 0))
                for n, (a, v) in enumerate(((0, 0), (0, 1), (1, 0))):
                    mm = pe.matmul(PF[:, :], wqk_hl[:, which, a, :], src[:, v, :], start=(n == 0), stop=(n == 2))
                mm.then_inc(done.sem, 1)

            def values(g, par):
                pe.wait_ge(v_q.sem, v_q.at(g, 0))
                for b in range(GS):
                    mm = pe.matmul(PF[:, b * P:(b + 1) * P], cin[:, par, b * P:(b + 1) * P], w_v[:, :], start=True, stop=True)
                mm.then_inc(p_v.sem, 1)

            def k_proj(g):
                project(g, 1, c_hl, v_c, v_x, p_k)

            def q_proj(g):
                project(g, 0, xT_hl, v_x, v_k, p_q)

            def scores(g, par, b):
                pe.wait_ge(d_k.sem[par], d_k.at(g, par))
                pe.wait_ge(d_q.sem[par], d_q.at(g, par))
                pe.wait_ge(a_mask.sem, a_mask.at(g))
                tok = slice(b * P, (b + 1) * P)
                for u in range(UNITS):
                    row, c0 = unit_rows(u)
                    bank = (SS0, SS1)[u % 2]
                    pe.wait_ge(v_max.sem, v_max.at(g, 4 * b + u - 2))
                    pe.matmul(bank[:, :], neg_i[:, :], bc(mask[:, par, b, None, :], [P, 4, P]), start=True, stop=False,
                              skip_group_check=True)
                    for i in range(4):
                        mm = pe.matmul(bank[:, i * P:(i + 1) * P], q_stack[row:row + NROW, par, c0 + i, tok],
                                       k_stack[row:row + NROW, par, c0 + i, tok], start=False, stop=True, skip_group_check=True)
                    mm.then_inc(p_s.sem, 1)

            def scoresT(g, par, b):
                pe.wait_ge(d_m[b // 2].sem[par], d_m[b // 2].at(g, par))
                tok = slice(b * P, (b + 1) * P)
                for u in range(UNITS):
                    row, c0 = unit_rows(u)
                    bank = (TT0, TT1)[u % 2]
                    pe.wait_ge(a_exp.sem, a_exp.at(g, 4 * b + u - 2))
                    pe.matmul(bank[:, :], mask[:, par, b, :], bc(neg_i[:, None, :], [P, 4, P]), start=True, stop=False,
                              skip_group_check=True)
                    for i in range(4):
                        mm = pe.matmul(bank[:, i * P:(i + 1) * P], k_stack[row:row + NROW + 3, par, c0 + i, tok],
                                       q_stack[row:row + NROW + 3, par, c0 + i, tok], start=False, stop=True,
                                       skip_group_check=True)
                    mm.then_inc(p_t.sem, 1)

            def weigh(g, par, b):
                bank = (U0, U1)[b % 2]
                pe.wait_ge(a_exp.sem, a_exp.at(g, 4 * b + 3))
                pe.wait_ge(v_v.sem, v_v.at(g, b))
                pe.wait_ge(v_norm.sem, v_norm.at(g, 2 * b - 3))
                for k, src in enumerate((v_d[:, par, b, :], ones_d[:, :])):
                    for i in range(4):
                        for u in range(UNITS):
                            mm = pe.matmul(bank[32 * u:32 * u + 32, k * P:(k + 1) * P], src[:, i * P + 32 * u:i * P + 32 * u + 32],
                                           prob[:, b % 2, u, i, :], start=(i == 0), stop=(i == 3), skip_group_check=True)
                mm.then_inc(p_u.sem, 1)

            def max_rows(g, half):
                pe.wait_ge(v_split.sem, v_split.at(g, 4 * half + 3))
                if half:
                    pe.wait_ge(a_mt.sem, a_mt.at(g, 0))
                else:
                    pe.wait_ge(v_v.sem, v_v.at(g, GS - 1))
                pe.sem_inc(pe_passed, 1)
                for b in range(2 * half, 2 * half + 2):
                    mm = pe.transpose(PF[:, :].bitcast(BF16)[0:48, b * P:(b + 1) * P],
                                      npart[:, b, :, :, :].rearrange("p j r c -> p (j r c)"), ident[:, :])
                mm.then_inc(p_mt.sem, 1)

            def output(g):
                pe.wait_ge(v_norm.sem, v_norm.at(g, 7))
                pe.wait_ge(v_res.sem, v_res.at(g - 1, 0))
                for b in range(GS):
                    mm = pe.matmul(PO[:, b * P:(b + 1) * P], ctxT[:, b, :], w_o[:, :], start=True, stop=True)
                mm.then_inc(p_o.sem, 1)

            def group(g, par, last):
                nxt = (g + 1, 1 - par)
                if not last:
                    x1T(*nxt)
                scoresT(g, par, 0)
                if not last:
                    k_proj(g + 1)
                scoresT(g, par, 1)
                if not last:
                    q_proj(g + 1)
                weigh(g, par, 0)
                if not last:
                    values(*nxt)
                scoresT(g, par, 2)
                weigh(g, par, 1)
                if not last:
                    scores(*nxt, 0)
                scoresT(g, par, 3)
                if not last:
                    scores(*nxt, 1)
                    max_rows(g + 1, 0)
                weigh(g, par, 2)
                if not last:
                    scores(*nxt, 2)
                weigh(g, par, 3)
                if not last:
                    scores(*nxt, 3)
                output(g)
                if not last:
                    max_rows(g + 1, 1)

            x1T(0, 0)
            k_proj(0)
            q_proj(0)
            values(0, 0)
            for b in range(GS):
                scores(0, 0, b)
                if b % 2:
                    max_rows(0, b // 2)
            pairs(pe, group)


def experts(nc, t, d, out, psum):
    NC = CHUNKS + 1
    SENTINEL, TAKEN = -3.0e38, 3.0e38
    with ExitStack() as ctx:
        def sb(name, shape, dt=F32):
            return ctx.enter_context(nc.sbuf_tensor(name, shape, dt))

        def sem(name, n=1, by=1):
            return Sem(ctx, nc, name, n, by)

        def raw(name):
            return ctx.enter_context(nc.semaphore(name))

        w_raw = sb("w_raw", [P, 2, NC, P])
        w_up = sb("w_up", [P, 2, 2, NC, P], F32R)
        w_down = sb("w_down", [P, NC, P])
        wg_raw = sb("wg_raw", [P, EXPERTS])
        w_gate = sb("w_gate", [P, 2, EXPERTS], F32R)
        bias = sb("bias", [P, EXPERTS])
        ones32 = sb("ones32", [32, CHUNKS, 2, EI])
        pick = sb("pick", [32, CHUNKS, 2, EI])
        spread = sb("spread", [32, CHUNKS, P], F32R)
        before = sb("before", [P, 4, 4])
        xs = sb("xs_c", [P, 2, GS, P])
        xT_hl = sb("xT_hl_c", [P, 2, 2, GT], F32R)
        th16 = sb("th16", [P, GS, EXPERTS])
        score = sb("score", [P, GS, EXPERTS])
        biased = sb("biased", [P, GS, EXPERTS])
        hi2, lo2, sum2 = (sb(n, [P, GS * 4, 2]) for n in ("hi2", "lo2", "sum2"))
        cross, gsum = sb("cross", [P, GS * 4]), sb("gsum", [P, GS, 4])
        above, tie = sb("above", [P, GS, 4, 4]), sb("tie", [P, GS, 4, 4])
        rank, penalty = sb("rank", [P, GS, 4]), sb("penalty", [P, GS, 4])
        open_ = sb("open_", [P, GS, EXPERTS + 4])
        top = sb("top", [P, GS, 8])
        marked = sb("marked", [P, GS, EXPERTS + 4])
        chosen = sb("chosen", [P, GS, EXPERTS])
        wsum = sb("wsum", [P, GS])
        cw = sb("cw", [P, GS, EXPERTS])
        cw_hl = sb("cw_hl", [P, GS, 2, EXPERTS], F32R)
        cwT = sb("cwT", [32, 2, GT], F32R)
        sg = sb("sg", [P, 2, GT])
        gu = sb("gu", [P, 2, GT])
        hid = sb("hid", [P, NC, GT])
        res = sb("res_c", [P, GS, P])
        normed = sb("normed", [P, 2, GS, P])
        stats, mv = sb("stats_c", [P, GS, 6]), sb("mv_c", [P, GS, 2])
        rstd, nmean = sb("rstd_c", [P, GS]), sb("nmean_c", [P, GS])
        x2, ident32, norm_c = t["x2"], t["ident32"], t["norm_c"]

        d_x, d_out = DmaSem(ctx, nc, "x2_staged"), DmaSem(ctx, nc, "out_stored")
        p_x, p_l, p_c = sem("x2T_mm"), sem("logit_mm"), sem("cwT_mm")
        p_g, p_u, p_w, p_d = sem("gate_mm", NC), sem("up_mm", NC), sem("weight_mm", CHUNKS), sem("down_mm", NC)
        a_x, a_l, a_c, a_s, a_o = sem("x2T_hi"), sem("logit_tanh"), sem("cwT_ready"), sem("silu_ready", NC), sem("out_ready", GS)
        v_x, v_sc, v_gu, v_hid = sem("x2T_lo"), sem("scores_ready", 2), sem("gu_ready", NC), sem("hid_ready", CHUNKS)
        v_sel, v_res = sem("select_dve", 18), sem("res_c_ready", 1 + 2 * GS)
        v_grp, g_var = sem("groups_ranked", 13), sem("rstd_c_ready", 4)
        d_w, v_init, g_init = raw("expert_weights"), raw("expert_dve_init"), raw("expert_pool_init")
        dve_passed = raw("expert_dve_passed")

        with nc.Block() as block:
            @block.sync
            def _(sp):
                for k, (e, sh) in enumerate((("WgT", "Ws_gT"), ("WuT", "Ws_uT"))):
                    sp.dma_start(w_raw[:, k, 0, :], d[sh]).then_inc(d_w, 16)
                    sp.dma_start(w_raw[:, k, 1:, :], d[e].rearrange("p (c n) -> p c n", n=P)).then_inc(d_w, 16)
                sp.dma_start(w_down[:, 0, :], d["Ws_dT"]).then_inc(d_w, 16)
                sp.dma_start(w_down[:, 1:, :], d["WdT"].rearrange("(c p) n -> p c n", p=P)).then_inc(d_w, 16)
                sp.dma_start(wg_raw[:, :], d["gate_wT"]).then_inc(d_w, 16)
                sp.dma_start(bias[:, :], d["gate_bias"].partition_broadcast(P)).then_inc(d_w, 16)
                sp.wait_ge(d_w, 8 * 16)

            @block.gpsimd
            def _(pool):
                pool.memset(ones32[:, :, :, :], 1.0).then_inc(g_init, 1)
                pool.memset(before[:, :, :], 1.0).then_inc(g_init, 1)
                pool.wait_ge(g_init, 2)
                pool.affine_select(out=pick[:, :, :, :], in_=ones32[:, :, :, :], compare_op=ALU.is_equal, fill=0.0, base=0,
                                   pattern=[[-2, CHUNKS], [-1, 2], [0, EI]], channel_multiplier=1).then_inc(g_init, 1)
                pool.wait_ge(g_init, 3)
                pool.affine_select(out=pick[:, :, :, :], in_=pick[:, :, :, :], compare_op=ALU.not_equal, fill=1.0, base=-EXPERTS,
                                   pattern=[[-2, CHUNKS], [-1, 2], [0, EI]], channel_multiplier=1).then_inc(g_init, 1)
                pool.affine_select(out=before[:, :, :], in_=before[:, :, :], compare_op=ALU.is_gt, fill=0.0, base=0,
                                   pattern=[[1, 4], [-1, 4]], channel_multiplier=0).then_inc(g_init, 1)

            @block.vector
            def _(dve):
                dve.memset(open_[:, :, EXPERTS:], SENTINEL)
                dve.memset(top[:, :, 4:], SENTINEL)
                dve.wait_ge(d_w, 8 * 16)
                for k in range(2):
                    dve.tensor_copy(w_up[:, k, 0], w_raw[:, k]).then_inc(v_init, 1)
                dve.tensor_copy(w_gate[:, 0, :], wg_raw[:, :]).then_inc(v_init, 1)
                dve.wait_ge(v_init, 3)
                for k in range(2):
                    dve.tensor_tensor(w_up[:, k, 1], w_raw[:, k], w_up[:, k, 0].bitcast(F32), ALU.subtract)
                dve.tensor_tensor(w_gate[:, 1, :], wg_raw[:, :], w_gate[:, 0, :].bitcast(F32), ALU.subtract)
                dve.wait_ge(g_init, 5)
                dve.tensor_copy(spread[:, :, :], pick[:, :, :, :].rearrange("p c e i -> p c (e i)"))

        GG, UU, WW, PF, PO = psum[0:2], psum[2:4], psum[4:6], psum[6], psum[7]
        block = ctx.enter_context(nc.Block())

        @block.sync
        def _(sp):
            d_x.prime(sp)
            d_out.prime(sp)

            def load(g, par):
                sp.wait_ge(v_res.sem, v_res.at(g - 2, 0))
                sp.dma_start(xs[:, par, :, :], x2[:, bass.ds(g * GS, GS), :]).then_inc(d_x.sem[par], 16)

            def group(g, par, last):
                if not last:
                    load(g + 1, 1 - par)
                sp.wait_ge(a_o.sem, a_o.at(g, GS - 1))
                sp.dma_start(out.rearrange("(b t) d -> t b d", t=P)[:, bass.ds(g * GS, GS), :], normed[:, par, :, :])\
                    .then_inc(d_out.sem[par], 16)

            load(0, 0)
            pairs(sp, group)
            for g in (NG - 2, NG - 1):
                sp.wait_ge(d_out.sem[g % 2], d_out.at(g, g % 2))

        @block.gpsimd
        def _(pool):
            g_var.prime(pool)

            def group(g, par, last):
                normalise_pool(pool, g, v_res, a_o, g_var, mv, rstd, nmean, norm_c)

            pairs(pool, group)

        @block.scalar
        def _(act):
            for s in (a_x, a_l, a_c, a_s, a_o):
                s.prime(act)

            def hi(g, par):
                act.wait_ge(p_x.sem, p_x.at(g))
                act.wait_ge(p_u.sem, p_u.at(g - 2, NC - 1))
                act.activation(xT_hl[:, par, 0, :], PF[:, :], ACT.Copy).then_inc(a_x.sem, 1)

            def logits(g):
                act.wait_ge(p_l.sem, p_l.at(g))
                act.wait_ge(v_sc.sem, v_sc.at(g - 1, 0))
                act.activation(th16[:, :, :], PF[:, 0:GS * EXPERTS], ACT.Tanh, scale=0.5).then_inc(a_l.sem, 1)

            def weights(g, par):
                act.wait_ge(p_c.sem, p_c.at(g))
                act.wait_ge(p_w.sem, p_w.at(g - 2, CHUNKS - 1))
                act.activation(cwT[:, par, :], PF[0:32, :], ACT.Copy).then_inc(a_c.sem, 1)

            def silu(g, par, c):
                k = (par + c) % 2
                act.wait_ge(p_g.sem, p_g.at(g, c))
                act.wait_ge(v_gu.sem, v_gu.at(g, c - 2))
                act.activation(sg[:, k, :], GG[k][:, :], ACT.Silu).then_inc(a_s.sem, 1)

            def group(g, par, last):
                nxt = (g + 1, 1 - par)
                for c in range(2, NC):
                    silu(g, par, c)
                    if not last and c == 2:
                        hi(*nxt)
                    if not last and c == 3:
                        logits(g + 1)
                    if not last and c == 7:
                        weights(*nxt)
                if not last:
                    silu(*nxt, 0)
                    silu(*nxt, 1)
                act.wait_ge(g_var.sem, g_var.at(g, 3))
                act.wait_ge(d_out.sem[par], d_out.at(g - 2, par))
                for b in range(GS):
                    act.activation(normed[:, par, b, :], res[:, b, :], ACT.Identity,
                                   bias=nmean[:, b:b + 1], scale=rstd[:, b:b + 1]).then_inc(a_o.sem, 1)

            hi(0, 0)
            logits(0)
            silu(0, 0, 0)
            weights(0, 0)
            silu(0, 0, 1)
            pairs(act, group)

        @block.vector
        def _(dve):
            for s in (v_x, v_sc, v_grp, v_gu, v_hid, v_sel, v_res):
                s.prime(dve)

            def lo(g, par):
                dve.wait_ge(a_x.sem, a_x.at(g))
                dve.tensor_tensor(xT_hl[:, par, 1, :], PF[:, :], xT_hl[:, par, 0, :].bitcast(F32), ALU.subtract).then_inc(v_x.sem, 1)

            def scores(g):
                dve.wait_ge(a_l.sem, a_l.at(g))
                dve.wait_ge(v_sel.sem, v_sel.at(g - 1, 11))
                dve.tensor_scalar(score[:, :, :], th16[:, :, :], 0.5, 0.5, ALU.mult, ALU.add).then_inc(v_sc.sem, 1)
                dve.wait_ge(v_sc.sem, v_sc.at(g, 0))
                dve.wait_ge(v_grp.sem, v_grp.at(g - 1, 1))
                dve.tensor_tensor(biased[:, :, :], score[:, :, :], bc(bias[:, None, :], [P, GS, EXPERTS]), ALU.add)\
                    .then_inc(v_sc.sem, 1)

            def groups_of(g):
                def step(k, ins):
                    ins.then_inc(v_grp.sem, 1)
                    dve.wait_ge(v_grp.sem, v_grp.at(g, k))

                dve.wait_ge(v_sc.sem, v_sc.at(g, 1))
                four = biased[:, :, :].rearrange("p b (q n e) -> p (b q) n e", q=4, n=2)
                step(0, dve.tensor_tensor(hi2[:, :, :], four[:, :, :, 0], four[:, :, :, 1], ALU.max))
                step(1, dve.tensor_tensor(lo2[:, :, :], four[:, :, :, 0], four[:, :, :, 1], ALU.min))
                step(2, dve.tensor_tensor(sum2[:, :, :], hi2[:, :, :], lo2[:, :, :], ALU.add))
                step(3, dve.tensor_tensor(cross[:, :], hi2[:, :, 0], hi2[:, :, 1], ALU.add))
                gs = gsum[:, :, :].rearrange("p b q -> p (b q)")
                step(4, dve.tensor_tensor(gs, sum2[:, :, 0], sum2[:, :, 1], ALU.max))
                step(5, dve.tensor_tensor(gs, gs, cross[:, :], ALU.max))
                mine, other = bc(gsum[:, :, :, None], [P, GS, 4, 4]), bc(gsum[:, :, None, :], [P, GS, 4, 4])
                step(6, dve.tensor_tensor(above[:, :, :, :], other, mine, ALU.is_gt))
                step(7, dve.tensor_tensor(tie[:, :, :, :], other, mine, ALU.is_ge))
                step(8, dve.tensor_tensor(tie[:, :, :, :], tie[:, :, :, :], bc(before[:, None, :, :], [P, GS, 4, 4]), ALU.mult))
                step(9, dve.tensor_tensor(above[:, :, :, :], above[:, :, :, :], tie[:, :, :, :], ALU.max))
                step(10, dve.tensor_tensor(tie[:, :, :, 0:2], above[:, :, :, 0:2], above[:, :, :, 2:4], ALU.add))
                step(11, dve.tensor_tensor(rank[:, :, :], tie[:, :, :, 0], tie[:, :, :, 1], ALU.add))
                dve.wait_ge(v_sel.sem, v_sel.at(g - 1, 0))
                step(12, dve.tensor_scalar(penalty[:, :, :], rank[:, :, :], 2.0, -1.0e30, ALU.is_ge, ALU.mult))

            def select(g):
                def step(k, ins):
                    ins.then_inc(v_sel.sem, 1)
                    dve.wait_ge(v_sel.sem, v_sel.at(g, k))

                dve.wait_ge(v_grp.sem, v_grp.at(g, 12))
                step(0, dve.tensor_tensor(open_[:, :, 0:EXPERTS].rearrange("p b (q e) -> p b q e", q=4),
                                          biased[:, :, :].rearrange("p b (q e) -> p b q e", q=4),
                                          bc(penalty[:, :, :, None], [P, GS, 4, 4]), ALU.add))
                dve.sem_inc(dve_passed, 1)
                for b in range(GS):
                    dve.max(top[:, b, :], open_[:, b, 0:EXPERTS]).then_inc(v_sel.sem, 1)
                dve.wait_ge(v_sel.sem, v_sel.at(g, 4))
                step(5, dve.memset(top[:, :, 4:], SENTINEL))
                dve.sem_inc(dve_passed, 1)
                for b in range(GS):
                    dve.match_replace(marked[:, b, :], top[:, b, :], open_[:, b, :], TAKEN).then_inc(v_sel.sem, 1)
                dve.wait_ge(v_sel.sem, v_sel.at(g, 9))
                step(10, dve.tensor_scalar(chosen[:, :, :], marked[:, :, 0:EXPERTS], TAKEN, None, ALU.is_ge))
                step(11, dve.tensor_tensor(chosen[:, :, :], chosen[:, :, :], score[:, :, :], ALU.mult))
                step(12, dve.tensor_reduce(wsum[:, :], chosen[:, :, :], AX_X, ALU.add))
                step(13, dve.tensor_scalar(wsum[:, :], wsum[:, :], 1e-20, None, ALU.add))
                step(14, dve.reciprocal(wsum[:, :], wsum[:, :]))
                step(15, dve.scalar_tensor_tensor(cw[:, :, :], chosen[:, :, :], SCALE, bc(wsum[:, :, None], [P, GS, EXPERTS]),
                                                  ALU.mult, ALU.mult))
                dve.wait_ge(p_c.sem, p_c.at(g - 1))
                step(16, dve.tensor_copy(cw_hl[:, :, 0, :], cw[:, :, :]))
                step(17, dve.tensor_tensor(cw_hl[:, :, 1, :], cw[:, :, :], cw_hl[:, :, 0, :].bitcast(F32), ALU.subtract))

            def hidden(g, par, c):
                k = (par + c) % 2
                dve.wait_ge(a_s.sem, a_s.at(g, c))
                dve.wait_ge(p_u.sem, p_u.at(g, c))
                dve.wait_ge(p_d.sem, p_d.at(g - 1, c))
                if c:
                    dve.wait_ge(v_hid.sem, v_hid.at(g, max(c - 3, -1)))
                dst = hid[:, 0, :] if c == 0 else gu[:, k, :]
                dve.tensor_tensor(dst, sg[:, k, :], UU[k][:, :], ALU.mult).then_inc(v_gu.sem, 1)
                if c:
                    dve.wait_ge(v_gu.sem, v_gu.at(g, c))
                    dve.wait_ge(p_w.sem, p_w.at(g, c - 1))
                    dve.tensor_tensor(hid[:, c, :], gu[:, k, :], WW[(c - 1) % 2][:, :], ALU.mult).then_inc(v_hid.sem, 1)

            def group(g, par, last):
                nxt = (g + 1, 1 - par)
                for c in range(2, NC):
                    hidden(g, par, c)
                    if not last and c == 2:
                        lo(*nxt)
                    if not last and c == 3:
                        scores(g + 1)
                    if not last and c == 4:
                        groups_of(g + 1)
                    if not last and c == 5:
                        select(g + 1)
                if not last:
                    hidden(*nxt, 0)
                    hidden(*nxt, 1)
                dve.wait_ge(p_d.sem, p_d.at(g, NC - 1))
                residual_dve(dve, g, PO, xs[:, par, :, :], a_o, v_res, dve_passed, res, stats, mv, times=2.0)

            lo(0, 0)
            scores(0)
            hidden(0, 0, 0)
            groups_of(0)
            select(0)
            hidden(0, 0, 1)
            pairs(dve, group)

        @block.tensor
        def _(pe):
            for s in (p_x, p_l, p_c, p_g, p_u, p_w, p_d):
                s.prime(pe)

            def x2T(g, par):
                pe.wait_ge(d_x.sem[par], d_x.at(g, par))
                pe.wait_ge(a_c.sem, a_c.at(g - 1))
                for b in range(GS):
                    mm = pe.transpose(PF[:, b * P:(b + 1) * P], xs[:, par, b, :], ident32[:, :])
                mm.then_inc(p_x.sem, 1)

            def logits(g, par):
                pe.wait_ge(v_x.sem, v_x.at(g))
                for b in range(GS):
                    for n, (a, v) in enumerate(((0, 0), (0, 1), (1, 0))):
                        mm = pe.matmul(PF[:, b * EXPERTS:(b + 1) * EXPERTS], xT_hl[:, par, a, b * P:(b + 1) * P], w_gate[:, v, :],
                                       start=(n == 0), stop=(n == 2))
                mm.then_inc(p_l.sem, 1)

            def weights(g):
                pe.wait_ge(v_sel.sem, v_sel.at(g, 17))
                pe.wait_ge(a_l.sem, a_l.at(g))
                for b in range(GS):
                    mm = pe.transpose(PF[0:32, b * P:(b + 1) * P],
                                      cw_hl[:, b, :, :].rearrange("p v e -> p (v e)").bitcast(F32), ident32[:, :])
                mm.then_inc(p_c.sem, 1)

            def up(g, par, c):
                k = (par + c) % 2
                for which, bank, freed, done in ((0, GG[k], a_s, p_g), (1, UU[k], v_gu, p_u)):
                    pe.wait_ge(freed.sem, freed.at(g, c - 2))
                    for n, (a, v) in enumerate(((0, 0), (0, 1), (1, 0))):
                        mm = pe.matmul(bank[:, :], w_up[:, which, a, c, :], xT_hl[:, par, v, :], start=(n == 0), stop=(n == 2))
                    mm.then_inc(done.sem, 1)
                if c:
                    pe.wait_ge(a_c.sem, a_c.at(g))
                    pe.wait_ge(v_hid.sem, v_hid.at(g, c - 3))
                    pe.matmul(WW[(c - 1) % 2][:, :], spread[:, c - 1, :], cwT[:, par, :], start=True, stop=True)\
                        .then_inc(p_w.sem, 1)

            def down(g, c):
                if c == 0:
                    pe.wait_ge(v_gu.sem, v_gu.at(g, 0))
                    pe.wait_ge(v_res.sem, v_res.at(g - 1, 0))
                else:
                    pe.wait_ge(v_hid.sem, v_hid.at(g, c - 1))
                for b in range(GS):
                    mm = pe.matmul(PO[:, b * P:(b + 1) * P], hid[:, c, b * P:(b + 1) * P], w_down[:, c, :],
                                   start=(c == 0 and b == 0), stop=(c == NC - 1), skip_group_check=True)
                mm.then_inc(p_d.sem, 1)

            def group(g, par, last):
                nxt = (g + 1, 1 - par)
                for c in range(2, NC):
                    up(g, par, c)
                    down(g, c - 2)
                    if not last and c == 2:
                        x2T(*nxt)
                    if not last and c == 3:
                        logits(*nxt)
                    if not last and c == 7:
                        weights(g + 1)
                if not last:
                    up(*nxt, 0)
                down(g, NC - 2)
                if not last:
                    up(*nxt, 1)
                down(g, NC - 1)

            x2T(0, 0)
            logits(0, 0)
            up(0, 0, 0)
            weights(0)
            up(0, 0, 1)
            pairs(pe, group)


def build(nc, d, out, stop_at=None):
    with ExitStack() as ctx:
        psum = [ctx.enter_context(nc.psum_tensor(f"bank{k}", [P, 512], F32)) for k in range(8)]
        t = {k: ctx.enter_context(nc.sbuf_tensor(k, [P, NSEQ, P], F32)) for k in ("x1", "x2")}
        t["ident"] = ctx.enter_context(nc.sbuf_tensor("ident", [P, P], BF16))
        t["ident32"] = ctx.enter_context(nc.sbuf_tensor("ident32", [P, P], F32))
        t["norm_c"] = ctx.enter_context(nc.sbuf_tensor("norm_c", [P, 3, GS], F32))
        mixer(nc, t, d, psum, stop_at)
        if stop_at in ("small", "trig", "mixer"):
            return
        attention(nc, t, d, psum)
        experts(nc, t, d, out, psum)


_DRAM = {
    "x": "x", "xT": "x", "ctxT": "ctx_1024", "mask": "mask_Bx1xSxS2_bk1", "w_inT": "L0_attn_w_in", "w_outT": "L0_attn_w_out",
    "dt_bias": "L0_attn_dt_bias", "D": "L0_attn_D", "Wq": "L0_xattn_Wq", "bq": "L0_xattn_bq", "Wk": "L0_xattn_Wk",
    "bk": "L0_xattn_bk", "Wv": "L0_xattn_Wv", "bv": "L0_xattn_bv", "Wo": "L0_xattn_Wo", "bo": "L0_xattn_bo",
    "gate_wT": "L0_ffn_gate_w", "gate_bias": "L0_ffn_gate_bias", "WgT": "L0_ffn_Wg", "WuT": "L0_ffn_Wu", "WdT": "L0_ffn_Wd",
    "Ws_gT": "L0_ffn_Ws_g", "Ws_uT": "L0_ffn_Ws_u", "Ws_dT": "L0_ffn_Ws_d",
}


def lay_out(inputs):
    import numpy as np
    a = {k: np.asarray(inputs[v]) for k, v in _DRAM.items()}
    a["x"] = a["x"].reshape(-1, P)
    a["xT"] = a["xT"].reshape(-1, P).T
    a["ctxT"] = a["ctxT"].reshape(-1, P).T
    a["mask"] = np.ascontiguousarray(a["mask"]).reshape(NSEQ, P, P).view(np.int32)
    for k in ("w_inT", "w_outT", "gate_wT", "Ws_gT", "Ws_uT", "Ws_dT"):
        a[k] = a[k].T
    a["WgT"] = a["WgT"].reshape(EXPERTS * EI, P).T
    a["WuT"] = a["WuT"].reshape(EXPERTS * EI, P).T
    a["WdT"] = a["WdT"].transpose(0, 2, 1).reshape(EXPERTS * EI, P)
    return {k: np.ascontiguousarray(v) for k, v in a.items()}


def kernel(**inputs):
    import concourse.bacc as bacc
    from concourse.bass_utils import run_bass_kernel_spmd

    nc = bacc.Bacc("TRN2", target_bir_lowering=False, num_devices=1)
    arrays = lay_out(inputs)
    d = {k: nc.dram_tensor(k + "_in", a.shape, mybir.dt.from_np(a.dtype), kind="ExternalInput").ap() for k, a in arrays.items()}
    out = nc.dram_tensor("out", (NSEQ * P, P), F32, kind="ExternalOutput").ap()
    build(nc, d, out)
    r = run_bass_kernel_spmd(nc, [{k + "_in": a for k, a in arrays.items()}], core_ids=[0])
    return r.results[0]["out"].reshape(NSEQ, P, P)
```

```python
from contextlib import ExitStack

import concourse.bass as bass
from concourse import mybir

F32 = mybir.dt.float32
F32R = mybir.dt.float32r
BF16 = mybir.dt.bfloat16
U8 = mybir.dt.uint8
ALU = mybir.AluOpType
ACT = mybir.ActivationFunctionType
AX_X = mybir.AxisListType.X

P = 128
NSEQ = 32
GS = 4
NG = NSEQ // GS
GT = GS * P
D_INNER = 256
HEADS = 4
HD = D_INNER // HEADS
ROT = 32
PLAIN = P - ROT
SMALL = 3 * HEADS + ROT
O_Z, O_X, O_B, O_C, O_S = 0, 256, 512, 640, 768
A_FLOOR = 1e-4
LN_EPS = 1e-5
ROUND = 12582912.0
TWO_PI = 6.283185
NEG = -30000.0

XH = 16
XD = P // XH
MASKED = -1.0e15
EXPERTS = 16
EI = 64
CHUNKS = EXPERTS * EI // P
SCALE = 2.5


class Sem:

    def __init__(self, ctx, nc, name, n=1, by=1):
        self.sem = ctx.enter_context(nc.semaphore(name))
        self.n, self.by = n, by

    def prime(self, eng):
        eng.sem_inc(self.sem, 2 * self.n * self.by)

    def at(self, g, k=0):
        return (g * self.n + (2 * self.n + k + 1)) * self.by


class DmaSem:

    def __init__(self, ctx, nc, name, dmas=1):
        self.sem = [ctx.enter_context(nc.semaphore(f"{name}{k}")) for k in range(2)]
        self.step = 16 * dmas

    def prime(self, eng):
        for s in self.sem:
            eng.sem_inc(s, self.step)

    def at(self, g, par):
        return g * (self.step // 2) + self.step * (4 - par) // 2


def pairs(eng, group):
    with eng.Fori(0, NG // 2 - 1) as i:
        group(2 * i, 0, 2)
        group(2 * i + 1, 1, 2)
    group(NG - 2, 0, 1)
    group(NG - 1, 1, 0)


def bc(ap, shape):
    return ap.to_broadcast(shape)


def residual_dve(dve, g, bank, other, normed, done, passed, res, stats, mv, times=1.0):
    dve.wait_ge(normed.sem, normed.at(g - 1, 3))
    dve.scalar_tensor_tensor(res[:, :, :], other, times, bank[:, :].rearrange("p (b d) -> p b d", b=GS), ALU.mult, ALU.add)\
        .then_inc(done.sem, 1)
    dve.wait_ge(done.sem, done.at(g, 0))
    for b in range(GS):
        dve.bn_stats(stats[:, b, :], res[:, b, :]).then_inc(done.sem, 1)
    dve.wait_ge(done.sem, done.at(g, GS))
    dve.sem_inc(passed, 1)
    for b in range(GS):
        dve.bn_aggr(mv[:, b, :], stats[:, b, :]).then_inc(done.sem, 1)


def normalise_pool(pool, g, res_ready, done, res, mv, rstd, norm_c, out, out_free=None):
    pool.wait_ge(res_ready.sem, res_ready.at(g, 2 * GS))
    pool.tensor_tensor(rstd[:, :], mv[:, :, 1], norm_c[:, 0, :], ALU.add).then_inc(done.sem, 1)
    pool.tensor_tensor(res[:, :, :], res[:, :, :], bc(mv[:, :, 0:1], [P, GS, P]), ALU.subtract).then_inc(done.sem, 1)
    pool.wait_ge(done.sem, done.at(g, 1))
    pool.tensor_tensor(rstd[:, :], rstd[:, :], norm_c[:, 1, :], ALU.pow).then_inc(done.sem, 1)
    if out_free:
        pool.wait_ge(*out_free)
    pool.wait_ge(done.sem, done.at(g, 2))
    pool.tensor_tensor(out, res[:, :, :], bc(rstd[:, :, None], [P, GS, P]), ALU.mult).then_inc(done.sem, 1)


def mixer(nc, t, d, psum, stop_at):
    with ExitStack() as ctx:
        def sb(name, shape, dt=F32):
            return ctx.enter_context(nc.sbuf_tensor(name, shape, dt))

        def sem(name, n=1, by=1):
            return Sem(ctx, nc, name, n, by)

        ident, ident32, norm_c = t["ident"], t["ident32"], t["norm_c"]
        xT = t["x2"]
        w_in = sb("w_in", [P, O_S + SMALL])
        w_feat = sb("w_feat", [P, 2, 4, P], F32R)
        w_z = sb("w_z", [P, 2, D_INNER], F32R)
        w_x = sb("w_x", [P, 2, D_INNER], F32R)
        w_dx = sb("w_dx", [P, 2, D_INNER], F32R)
        w_dx32 = sb("w_dx32", [P, D_INNER])
        w_out = sb("w_out", [P, 2, P])
        dt_bias = sb("dt_bias", [P, 2 * HEADS])
        d_skip = sb("d_skip", [P, HEADS])
        upto = sb("upto", [P, P])
        after = sb("after", [P, P], F32R)
        acausal = sb("acausal", [P, P], BF16)
        phase = sb("phase", [P, 1])
        scratch = sb("scratch", [P, P])
        small = sb("small", [P, NSEQ, SMALL])
        soft = sb("soft", [P, NSEQ, 2 * HEADS])
        minus1 = sb("minus1", [P, 1])
        e8 = sb("e8", [P, NSEQ, 2 * HEADS])
        s8 = sb("s8", [P, NSEQ, 2 * HEADS])
        q8 = sb("q8", [P, NSEQ, 2 * HEADS])
        p8 = sb("p8", [P, NSEQ, 2 * HEADS])
        gate = sb("gate", [P, NSEQ, HEADS])
        ngate = sb("ngate", [P, NSEQ, HEADS])
        gamma = sb("gamma", [P, NSEQ, HEADS])
        beta = sb("beta", [P, NSEQ, HEADS])
        decay = sb("decay", [P, NSEQ, HEADS])
        alpha = sb("alpha", [P, NSEQ, HEADS])
        dec_hl = sb("dec_hl", [P, 2, NSEQ, HEADS])
        dec_r = sb("dec_r", [P, NSEQ, HEADS], F32R)
        half_dt = sb("half_dt", [P, NSEQ, HEADS])
        th = sb("th", [P, NSEQ, ROT])
        trig = sb("trig", [P, 2, NSEQ * P])
        rstd = sb("rstd_e", [P, GS])

        w_loaded, const = sem("w_loaded", 1, 16), sem("const")
        wprep = sem("wprep")

        with ExitStack() as c1:
            BIASED = 17
            s_xt = [c1.enter_context(nc.semaphore(f"xt_loaded{g}")) for g in range(NG)]
            s_mm = c1.enter_context(nc.semaphore("small_mm"))
            s_ev = c1.enter_context(nc.semaphore("small_copied"))
            s_act = c1.enter_context(nc.semaphore("small_act"))
            s_dve = c1.enter_context(nc.semaphore("small_dve"))
            s_pool = c1.enter_context(nc.semaphore("mixer_consts"))
            s_w = c1.enter_context(nc.semaphore("mixer_weights"))
            s_win = c1.enter_context(nc.semaphore("w_in_loaded"))
            block = c1.enter_context(nc.Block())

            @block.sync
            def _(sp):
                sp.dma_start(w_in[:, :], d["w_inT"]).then_inc(s_win, 16)
                for g in range(NG):
                    sp.dma_start(xT[:, g * GS:(g + 1) * GS, :], d["xT"][:, g * GT:(g + 1) * GT]
                                 .rearrange("p (b t) -> p b t", t=P)).then_inc(s_xt[g], 16)

            @block.gpsimd
            def _(pool):
                pool.dma_start(dt_bias[:, 0:HEADS], d["dt_bias"].partition_broadcast(P)).then_inc(s_w, 16)
                pool.dma_start(d_skip[:, :], d["D"].partition_broadcast(P)).then_inc(s_w, 16)
                pool.dma_start(w_out[:, :, :], d["w_outT"].rearrange("(c k) n -> k c n", k=P)).then_inc(s_w, 16)
                pool.memset(scratch[:, :], 1.0).then_inc(s_pool, 1)
                pool.wait_ge(s_pool, 1)
                pool.affine_select(out=upto[:, :], in_=scratch[:, :], compare_op=ALU.is_ge, fill=0.0, base=0,
                                   pattern=[[1, P]], channel_multiplier=-1).then_inc(s_pool, 1)
                pool.affine_select(out=after[:, :], in_=scratch[:, :], compare_op=ALU.is_gt, fill=0.0, base=0,
                                   pattern=[[-1, P]], channel_multiplier=1).then_inc(s_pool, 1)
                pool.affine_select(out=ident[:, :], in_=scratch[:, :], compare_op=ALU.is_equal, fill=0.0, base=0,
                                   pattern=[[1, P]], channel_multiplier=-1).then_inc(s_pool, 1)
                pool.affine_select(out=ident32[:, :], in_=scratch[:, :], compare_op=ALU.is_equal, fill=0.0, base=0,
                                   pattern=[[1, P]], channel_multiplier=-1).then_inc(s_pool, 1)
                pool.memset(minus1[:, :], -1.0)
                for k, value in enumerate((LN_EPS, -0.5)):
                    pool.memset(norm_c[:, k, :], value).then_inc(s_pool, 1)
                pool.wait_ge(s_pool, 5)
                pool.memset(scratch[:, :], 0.0).then_inc(s_pool, 1)
                pool.wait_ge(s_pool, 8)
                pool.affine_select(out=acausal[:, :], in_=scratch[:, :], compare_op=ALU.is_ge, fill=NEG, base=0,
                                   pattern=[[1, P]], channel_multiplier=-1).then_inc(s_pool, 1)

            @block.tensor
            def _(pe):
                pe.wait_ge(s_win, 16)
                for g in range(NG):
                    pe.wait_ge(s_xt[g], 16)
                    if g >= 2:
                        pe.wait_ge(s_ev, g - 1)
                    for b in range(GS):
                        mm = pe.matmul(psum[g % 2][:, b * SMALL:(b + 1) * SMALL], xT[:, g * GS + b, :],
                                       w_in[:, O_S:], start=True, stop=True)
                    mm.then_inc(s_mm, 1)

            @block.scalar
            def _(act):
                for g in range(NG):
                    act.wait_ge(s_mm, g + 1)
                    act.activation(small[:, g * GS:(g + 1) * GS, :], psum[g % 2][:, 0:GS * SMALL], ACT.Copy).then_inc(s_ev, 1)
                act.wait_ge(s_ev, NG)
                act.activation(th[:, :, :], small[:, :, 12:SMALL], ACT.Tanh).then_inc(s_act, 1)
                act.activation(ngate[:, :, :], small[:, :, 8:12], ACT.Exp, scale=-1.0).then_inc(s_act, 1)
                act.wait_ge(s_dve, BIASED)
                act.activation(e8[:, :, :], soft[:, :, :], ACT.Abs).then_inc(s_act, 1)
                act.wait_ge(s_act, 3)
                act.activation(e8[:, :, :], e8[:, :, :], ACT.Exp, scale=-1.0).then_inc(s_act, 1)

            @block.vector
            def _(dve):
                steps = [0]

                def link(ins):
                    steps[0] += 1
                    ins.then_inc(s_dve, 1)
                    dve.wait_ge(s_dve, steps[0])

                for h in range(2):
                    dve.memset(phase[64 * h:64 * h + 32, :], 0.25)
                    dve.memset(phase[64 * h + 32:64 * h + 64, :], 0.0)
                link(dve.memset(dt_bias[:, HEADS:], 0.0))
                dve.wait_ge(s_win, 16)
                dve.wait_ge(s_w, 48)
                link(dve.tensor_tensor(w_dx32[:, :].rearrange("p (h e) -> p h e", h=HEADS),
                                       w_in[:, O_X:O_X + D_INNER].rearrange("p (h e) -> p h e", h=HEADS),
                                       bc(d_skip[:, :, None], [P, HEADS, HD]), ALU.mult))
                parts = [(w_feat[:, :, c, :].rearrange("p v (h r) -> p v h r", h=4), bc(w_in[:, None, o:o + ROT], [P, 4, ROT]))
                         for c, o in ((0, O_B), (1, O_C))]
                parts += [(w_feat[:, :, c, 0:PLAIN], w_in[:, o + ROT:o + P]) for c, o in ((2, O_B), (3, O_C))]
                parts += [(w_z[:, :, :], w_in[:, O_Z:O_Z + D_INNER]), (w_x[:, :, :], w_in[:, O_X:O_X + D_INNER]),
                          (w_dx[:, :, :], w_dx32[:, :])]
                for w, src in parts:
                    dve.tensor_copy(w[:, 0], src).then_inc(s_dve, 1)
                steps[0] += len(parts)
                dve.wait_ge(s_dve, steps[0])
                for w, src in parts:
                    dve.tensor_tensor(w[:, 1], src, w[:, 0].bitcast(F32), ALU.subtract).then_inc(s_dve, 1)
                steps[0] += len(parts)
                dve.wait_ge(s_ev, NG)
                link(dve.tensor_tensor(soft[:, :, :], small[:, :, 0:8], bc(dt_bias[:, None, :], [P, NSEQ, 8]), ALU.add))
                assert steps[0] == BIASED, steps
                dve.wait_ge(s_act, 4)
                link(dve.tensor_scalar(s8[:, :, :], e8[:, :, :], 2.0, None, ALU.add))
                link(dve.reciprocal(q8[:, :, :], s8[:, :, :]))
                link(dve.tensor_tensor(s8[:, :, :], e8[:, :, :], q8[:, :, :], ALU.mult))
                link(dve.tensor_tensor(p8[:, :, :], s8[:, :, :], s8[:, :, :], ALU.mult))
                link(dve.tensor_scalar(q8[:, :, :], p8[:, :, :], 1.0 / 17, None, ALU.mult))
                for k in range(7, 0, -1):
                    link(dve.scalar_tensor_tensor(q8[:, :, :], q8[:, :, :], 1.0 / (2 * k + 1), p8[:, :, :], ALU.add, ALU.mult))
                link(dve.scalar_tensor_tensor(q8[:, :, :], q8[:, :, :], 1.0, s8[:, :, :], ALU.add, ALU.mult))
                link(dve.tensor_scalar(p8[:, :, :], soft[:, :, :], 0.0, None, ALU.max))
                link(dve.scalar_tensor_tensor(soft[:, :, :], q8[:, :, :], 2.0, p8[:, :, :], ALU.mult, ALU.add))
                dve.tensor_scalar(decay[:, :, :], soft[:, :, 4:8], -1.0, -A_FLOOR, ALU.mult, ALU.min)
                dve.tensor_scalar(half_dt[:, :, :], soft[:, :, 0:4], 0.5, None, ALU.mult)

        if stop_at == "small":
            return

        with ExitStack() as c2:
            turns = c2.enter_context(nc.sbuf_tensor("turns", [P, 2, GS, HEADS, 2, ROT], F32))
            ang = c2.enter_context(nc.sbuf_tensor("ang", [P, 4, GT], F32))
            whole = c2.enter_context(nc.sbuf_tensor("whole", [P, 4, GT], F32))
            frac = c2.enter_context(nc.sbuf_tensor("frac", [P, 4, GT], F32))
            t_turns, t_mm = Sem(c2, nc, "turns_ready", 2), Sem(c2, nc, "theta_ready", 2)
            t_ang, t_whole = Sem(c2, nc, "ang_ready", 2), Sem(c2, nc, "whole_ready", 2)
            t_frac, t_trig = Sem(c2, nc, "frac_ready", 2), Sem(c2, nc, "trig_ready", 2)
            s_coef = c2.enter_context(nc.semaphore("coefficients_pool"))
            s_alpha = c2.enter_context(nc.semaphore("alpha_ready"))
            block = c2.enter_context(nc.Block())

            @block.gpsimd
            def _(pool):
                dt = soft[:, :, 0:4]
                pool.tensor_tensor(decay[:, :, :], decay[:, :, :], dt, ALU.mult).then_inc(s_coef, 1)
                pool.tensor_scalar(gate[:, :, :], ngate[:, :, :], 1.0, None, ALU.add).then_inc(s_coef, 1)
                pool.wait_ge(s_coef, 2)
                pool.tensor_tensor(gate[:, :, :], gate[:, :, :], bc(minus1[:, :, None], [P, NSEQ, HEADS]), ALU.pow).then_inc(s_coef, 1)
                pool.tensor_copy(dec_r[:, :, :], decay[:, :, :]).then_inc(s_coef, 1)
                pool.wait_ge(s_coef, 4)
                pool.tensor_tensor(gamma[:, :, :], gate[:, :, :], dt, ALU.mult).then_inc(s_coef, 1)
                pool.tensor_copy(dec_hl[:, 0, :, :], dec_r[:, :, :].bitcast(F32)).then_inc(s_coef, 1)
                pool.wait_ge(s_coef, 6)
                pool.tensor_tensor(ngate[:, :, :], dt, gamma[:, :, :], ALU.subtract).then_inc(s_coef, 1)
                pool.tensor_tensor(dec_hl[:, 1, :, :], decay[:, :, :], dec_hl[:, 0, :, :], ALU.subtract).then_inc(s_coef, 1)
                pool.wait_ge(s_coef, 8)
                pool.wait_ge(s_alpha, 1)
                pool.tensor_tensor(beta[:, :, :], ngate[:, :, :], alpha[:, :, :], ALU.mult)

            @block.vector
            def _(dve):
                for s in (t_turns, t_whole, t_frac):
                    s.prime(dve)

                def angles(g, par):
                    dve.wait_ge(t_mm.sem, t_mm.at(g - 2, 1))
                    for cs in range(2):
                        dve.tensor_tensor(turns[:, par, :, :, cs, :],
                                          bc(th[:, bass.ds(g * GS, GS), None, :], [P, GS, HEADS, ROT]),
                                          bc(half_dt[:, bass.ds(g * GS, GS), :, None], [P, GS, HEADS, ROT]),
                                          ALU.mult).then_inc(t_turns.sem, 1)

                def group(g, par, left):
                    if left:
                        angles(g + 1, 1 - par)
                    for k in range(2):
                        j = 2 * par + k
                        dve.wait_ge(t_ang.sem, t_ang.at(g, k))
                        dve.wait_ge(t_frac.sem, t_frac.at(g - 2, k))
                        dve.tensor_scalar(whole[:, j, :], ang[:, j, :], ROUND, -ROUND, ALU.add, ALU.add).then_inc(t_whole.sem, 1)
                        dve.wait_ge(t_whole.sem, t_whole.at(g, k))
                        dve.wait_ge(t_trig.sem, t_trig.at(g - 2, k))
                        dve.tensor_tensor(frac[:, j, :], ang[:, j, :], whole[:, j, :], ALU.subtract).then_inc(t_frac.sem, 1)

                angles(0, 0)
                pairs(dve, group)

            @block.tensor
            def _(pe):
                t_mm.prime(pe)

                def group(g, par, left):
                    pe.wait_ge(t_turns.sem, t_turns.at(g, 1))
                    for k in range(2):
                        pe.wait_ge(t_ang.sem, t_ang.at(g - 2, k))
                        for b in range(GS):
                            mm = pe.matmul(psum[2 * par + k][:, b * P:(b + 1) * P],
                                           turns[:, par, b, 2 * k:2 * k + 2, :, :].rearrange("p h c r -> p (h c r)"),
                                           upto[:, :], start=True, stop=True)
                        mm.then_inc(t_mm.sem, 1)

                pairs(pe, group)

            @block.scalar
            def _(act):
                for s in (t_ang, t_trig):
                    s.prime(act)

                def copied(g, par, k):
                    act.wait_ge(t_mm.sem, t_mm.at(g, k))
                    act.wait_ge(t_frac.sem, t_frac.at(g - 2, k))
                    act.activation(ang[:, 2 * par + k, :], psum[2 * par + k][:, :], ACT.Identity,
                                   bias=phase[:, 0:1]).then_inc(t_ang.sem, 1)

                def group(g, par, left):
                    for k in range(2):
                        if left:
                            copied(g + 1, 1 - par, k)
                        act.wait_ge(t_frac.sem, t_frac.at(g, k))
                        act.activation(trig[:, k, bass.ds(g * GT, GT)], frac[:, 2 * par + k, :], ACT.Sin,
                                       scale=TWO_PI).then_inc(t_trig.sem, 1)

                act.wait_ge(s_coef, 1)
                act.activation(alpha[:, :, :], decay[:, :, :], ACT.Exp).then_inc(s_alpha, 1)
                copied(0, 0, 0)
                copied(0, 0, 1)
                pairs(act, group)

        if stop_at == "trig":
            return

        xhl = sb("xhl", [P, 2, 2, GS, P + 1], F32R)
        xres = sb("xres", [P, 2, GS, P])
        b_rot = sb("b_rot", [P, 2, 2, GT])
        c_rot = sb("c_rot", [P, 2, 2, GT])
        plain = sb("plain", [PLAIN, 2, 2, 2, GT], F32R)
        tz = sb("tz", [P, 2, 2, GT])
        ramp = sb("ramp", [P, 2, 2, HEADS, P], F32R)
        expo = sb("expo", [P, 2, HEADS, P])
        mix = sb("mix", [P, 2, HEADS, P])
        xg = sb("xg", [P, 2, D_INNER])
        w_tok = sb("w_tok", [P, 2, D_INNER])
        y = sb("y", [P, 2, GT])
        res = sb("res", [P, GS, P])
        stats = sb("stats", [P, GS, 6])
        mv = sb("mv", [P, GS, 2])
        x1 = t["x1"]

        s_x = DmaSem(ctx, nc, "x_in")
        s_hi, s_lo = sem("x_hi"), sem("x_lo")
        s_feat = sem("feat_mm", 6)
        s_hiz = sem("feat_act", 4)
        s_prod = sem("feat_dve", 8)
        s_ramp = sem("ramp_ready", 8)
        s_dec = sem("decay_mm", GS)
        s_xx = sem("x_mm", GS)
        s_g = sem("g_mm", 2 * GS)
        s_exp = sem("expo_ready", GS)
        s_w = sem("w_ready", 3 * GS)
        s_mix = sem("mix_ready", GS)
        s_y = sem("y_mm", GS)
        s_yg = sem("y_gated", 2)
        s_o = sem("out_mm")
        s_res = sem("res_ready", 1 + 2 * GS)
        s_x1 = sem("x1_ready", 4)
        s_zero = ctx.enter_context(nc.semaphore("x_zero_columns"))
        act_passed = ctx.enter_context(nc.semaphore("mixer_act_passed"))
        dve_passed = ctx.enter_context(nc.semaphore("mixer_dve_passed"))
        P0, P1, PX, PD, PG, PY0, PY1, PO = psum
        block = ctx.enter_context(nc.Block())

        @block.sync
        def _(sp):
            s_x.prime(sp)

            def group(g, par, left):
                sp.wait_ge(s_res.sem, s_res.at(g - 2, 0))
                sp.dma_start(xres[:, par, :, :], d["x"].rearrange("(b t) d -> t b d", t=P)[:, bass.ds(g * GS, GS), :])\
                    .then_inc(s_x.sem[par], 16)

            pairs(sp, group)

        @block.scalar
        def _(act):
            for s in (s_hi, s_hiz, s_exp):
                s.prime(act)

            def split(g, par):
                act.wait_ge(s_y.sem, s_y.at(g - 2, 3))
                act.sem_inc(act_passed, 1)
                act.activation(xhl[:, par, 0, :, 1:], xT[:, bass.ds(g * GS, GS), :], ACT.Copy).then_inc(s_hi.sem, 1)

            def plain_hi(g, par):
                for k in range(2):
                    act.wait_ge(s_feat.sem, s_feat.at(g, 2 + k))
                    act.wait_ge(s_g.sem, s_g.at(g - 2, 7))
                    act.activation(plain[:, par, k, 0, :], (P0, P1)[k][0:PLAIN, :], ACT.Copy).then_inc(s_hiz.sem, 1)

            def gates(g):
                for k in range(2):
                    act.wait_ge(s_feat.sem, s_feat.at(g, 4 + k))
                    act.wait_ge(s_yg.sem, s_yg.at(g - 1, k))
                    act.activation(tz[:, 0, k, :], (P0, P1)[k][:, :], ACT.Tanh, scale=0.5).then_inc(s_hiz.sem, 1)

            def group(g, par, left):
                if left:
                    split(g + 1, 1 - par)
                for b in range(GS):
                    act.wait_ge(s_dec.sem, s_dec.at(g, b))
                    act.wait_ge(s_mix.sem, s_mix.at(g, b - 2))
                    act.activation(expo[:, b % 2, :, :], PD[:, :], ACT.Exp).then_inc(s_exp.sem, 1)
                    if left and b == 2:
                        plain_hi(g + 1, 1 - par)
                if left:
                    gates(g + 1)

            split(0, 0)
            plain_hi(0, 0)
            gates(0)
            pairs(act, group)

        @block.gpsimd
        def _(pool):
            for s in (s_ramp, s_x1):
                s.prime(pool)

            def ramps(g, bs):
                for b in bs:
                    pool.wait_ge(s_dec.sem, s_dec.at(g, b - 2))
                    for v in range(2):
                        pool.tensor_tensor(ramp[:, b % 2, v, :, :], bc(upto[:, None, :], [P, HEADS, P]),
                                           bc(dec_hl[:, v, bass.ds(g * GS + b, 1), :].rearrange("p o h -> p (o h)")[:, :, None],
                                              [P, HEADS, P]), ALU.mult).then_inc(s_ramp.sem, 1)

            def group(g, par, left):
                ramps(g, (2, 3))
                if left:
                    ramps(g + 1, (0, 1))
                normalise_pool(pool, g, s_res, s_x1, res, mv, rstd, norm_c, x1[:, bass.ds(g * GS, GS), :])

            ramps(0, (0, 1))
            pairs(pool, group)

        @block.vector
        def _(dve):
            dve.memset(xhl[:, :, :, :, 0:1].bitcast(F32), 0.0).then_inc(s_zero, 1)
            for s in (s_lo, s_prod, s_w, s_mix, s_yg, s_res):
                s.prime(dve)

            def split(g, par):
                dve.wait_ge(s_hi.sem, s_hi.at(g))
                dve.tensor_tensor(xhl[:, par, 1, :, 1:], xT[:, bass.ds(g * GS, GS), :], xhl[:, par, 0, :, 1:].bitcast(F32),
                                  ALU.subtract)\
                    .then_inc(s_lo.sem, 1)

            def rotate(g, par):
                for c, rot in ((0, b_rot), (1, c_rot)):
                    dve.wait_ge(s_feat.sem, s_feat.at(g, c))
                    dve.wait_ge(s_g.sem, s_g.at(g - 2, 7))
                    for k in range(2):
                        dve.tensor_tensor(rot[:, par, k, :], (P0, P1)[c][:, :], trig[:, k, bass.ds(g * GT, GT)], ALU.mult)\
                            .then_inc(s_prod.sem, 1)

            def plain_lo(g, par):
                for k in range(2):
                    dve.wait_ge(s_hiz.sem, s_hiz.at(g, k))
                    dve.tensor_tensor(plain[:, par, k, 1, :], (P0, P1)[k][0:PLAIN, :], plain[:, par, k, 0, :].bitcast(F32),
                                      ALU.subtract).then_inc(s_prod.sem, 1)

            def gates(g):
                for k in range(2):
                    dve.wait_ge(s_hiz.sem, s_hiz.at(g, 2 + k))
                    dve.wait_ge(s_yg.sem, s_yg.at(g - 1, k))
                    dve.scalar_tensor_tensor(tz[:, 1, k, :], tz[:, 0, k, :], 1.0, (P0, P1)[k][:, :], ALU.add, ALU.mult)\
                        .then_inc(s_prod.sem, 1)

            def inputs_of(g, b):
                dve.wait_ge(s_xx.sem, s_xx.at(g, b))
                heads = lambda ap: ap.rearrange("p (h e) -> p h e", h=HEADS)
                of = lambda co: bc(co[:, bass.ds(g * GS + b, 1), :].rearrange("p o h -> p (o h)")[:, :, None], [P, HEADS, HD])
                dve.wait_ge(s_w.sem, s_w.at(g, 3 * b - 1))
                dve.tensor_tensor(heads(xg[:, 0, :]), heads(PX[:, 0:D_INNER]), of(gamma), ALU.mult).then_inc(s_w.sem, 1)
                dve.tensor_tensor(heads(xg[:, 1, :]), heads(PX[:, D_INNER:]), of(beta), ALU.mult).then_inc(s_w.sem, 1)
                dve.wait_ge(s_w.sem, s_w.at(g, 3 * b + 1))
                dve.wait_ge(s_y.sem, s_y.at(g, b - 2))
                dve.tensor_tensor(w_tok[:, b % 2, :], xg[:, 0, :], xg[:, 1, :], ALU.add).then_inc(s_w.sem, 1)

            def group(g, par, left):
                if left:
                    split(g + 1, 1 - par)
                for b in range(GS):
                    inputs_of(g, b)
                    dve.wait_ge(s_g.sem, s_g.at(g, 2 * b + 1))
                    dve.wait_ge(s_exp.sem, s_exp.at(g, b))
                    dve.wait_ge(s_y.sem, s_y.at(g, b - 2))
                    dve.tensor_tensor(mix[:, b % 2, :, :], PG[:, :].rearrange("p (h t) -> p h t", h=HEADS),
                                      expo[:, b % 2, :, :], ALU.mult).then_inc(s_mix.sem, 1)
                    if left and b == 1:
                        rotate(g + 1, 1 - par)
                    if left and b == 2:
                        plain_lo(g + 1, 1 - par)
                dve.wait_ge(s_y.sem, s_y.at(g, 3))
                dve.wait_ge(s_o.sem, s_o.at(g - 1))
                dve.wait_ge(s_prod.sem, s_prod.at(g, 7))
                for k in range(2):
                    dve.scalar_tensor_tensor(y[:, k, :], tz[:, 1, k, :], 0.5, (PY0, PY1)[k][:, :], ALU.mult, ALU.mult)\
                        .then_inc(s_yg.sem, 1)
                if left:
                    gates(g + 1)
                dve.wait_ge(s_o.sem, s_o.at(g))
                dve.wait_ge(s_x.sem[par], s_x.at(g, par))
                residual_dve(dve, g, PO, xres[:, par, :, :], s_x1, s_res, dve_passed, res, stats, mv)

            split(0, 0)
            rotate(0, 0)
            plain_lo(0, 0)
            gates(0)
            pairs(dve, group)

        @block.tensor
        def _(pe):
            for s in (s_feat, s_dec, s_xx, s_g, s_y, s_o):
                s.prime(pe)

            def features(g, par, cs):
                pe.wait_ge(s_lo.sem, s_lo.at(g))
                freed = [None, None, (s_prod, 1), (s_prod, 3), (s_prod, 4), (s_prod, 5)]
                for c in cs:
                    bank = (P0, P1)[c % 2]
                    if freed[c]:
                        pe.wait_ge(freed[c][0].sem, freed[c][0].at(g, freed[c][1]))
                    else:
                        pe.wait_ge(s_prod.sem, s_prod.at(g - 1, 6 + c))
                    m = (P, P, PLAIN, PLAIN, P, P)[c]
                    w = w_feat[:, :, c, 0:m] if c < 4 else w_z[:, :, (c - 4) * P:(c - 3) * P]
                    for n, (a, v) in enumerate(((0, 0), (0, 1), (1, 0))):
                        mm = pe.matmul(bank[0:m, :], w[:, a, :], xhl[:, par, v, :, 1:], start=(n == 0), stop=(n == 2))
                    mm.then_inc(s_feat.sem, 1)

            def front(g, par, b):
                pe.wait_ge(s_ramp.sem, s_ramp.at(g, 2 * b + 1))
                pe.wait_ge(s_exp.sem, s_exp.at(g, b - 1))
                for v in range(2):
                    pe.matmul(PD[:, :], after[:, :], ramp[:, b % 2, v, :, :], start=(v == 0), stop=False)
                pe.matmul(PD[:, :], ident[:, :], bc(acausal[:, None, :], [P, HEADS, P]), start=False, stop=True)\
                    .then_inc(s_dec.sem, 1)
                pe.wait_ge(s_w.sem, s_w.at(g, 3 * b - 2))
                tokens(par, b, 0)

            def tokens(par, b, shift):
                for n, (a, v) in enumerate(((0, 0), (0, 1), (1, 0))):
                    mm = pe.matmul(PX[:, shift * D_INNER:(shift + 1) * D_INNER], xhl[:, par, a, b, 1 - shift:P + 1 - shift],
                                   w_x[:, v, :], start=(n == 0), stop=(n == 2))
                return mm

            def scores(g, par, b):
                pe.wait_ge(s_mix.sem, s_mix.at(g, b - 1))
                tok = slice(b * P, (b + 1) * P)
                for n, (a, v) in enumerate(((0, 0), (0, 1), (1, 0))):
                    pe.matmul(PG[:, :], plain[:, par, 0, a, tok], bc(plain[:, par, 1, v, None, tok], [PLAIN, HEADS, P]),
                              start=(n == 0), stop=False, skip_group_check=True)
                for half in range(2):
                    rows = slice(64 * half, 64 * half + 64)
                    for k in range(2):
                        h = 2 * k + half
                        mm = pe.matmul(PG[:, h * P:(h + 1) * P], b_rot[rows, par, k, tok], c_rot[rows, par, k, tok],
                                       start=False, stop=True, skip_group_check=True)
                    mm.then_inc(s_g.sem, 1)
                    if half == 0:
                        tokens(par, b, 1).then_inc(s_xx.sem, 1)
                        pe.wait_ge(s_g.sem, s_g.at(g, 2 * b))

            def skip(g, par):
                for k in range(2):
                    pe.wait_ge(s_yg.sem, s_yg.at(g - 1, k))
                    for n, (a, v) in enumerate(((0, 0), (0, 1), (1, 0))):
                        pe.matmul((PY0, PY1)[k][:, :], w_dx[:, a, k * P:(k + 1) * P], xhl[:, par, v, :, 1:],
                                  start=(n == 0), stop=False, skip_group_check=True)

            def back(g, b):
                pe.wait_ge(s_mix.sem, s_mix.at(g, b))
                pe.wait_ge(s_w.sem, s_w.at(g, 3 * b + 2))
                for h in range(HEADS):
                    mm = pe.matmul((PY0, PY1)[h // 2][64 * (h % 2):64 * (h % 2) + 64, b * P:(b + 1) * P],
                                   w_tok[:, b % 2, h * HD:(h + 1) * HD], mix[:, b % 2, h, :],
                                   start=False, stop=True, skip_group_check=True)
                mm.then_inc(s_y.sem, 1)

            def group(g, par, left):
                pe.wait_ge(s_prod.sem, s_prod.at(g, 5))
                front(g, par, 0)
                scores(g, par, 0)
                skip(g, par)
                for b in range(1, GS):
                    front(g, par, b)
                    back(g, b - 1)
                    scores(g, par, b)
                    if left and b < 3:
                        features(g + 1, 1 - par, (2 * b - 2, 2 * b - 1))
                back(g, GS - 1)
                if left:
                    features(g + 1, 1 - par, (4, 5))
                pe.wait_ge(s_yg.sem, s_yg.at(g, 1))
                pe.wait_ge(s_res.sem, s_res.at(g - 1, 0))
                for b in range(GS):
                    for k in range(2):
                        mm = pe.matmul(PO[:, b * P:(b + 1) * P], y[:, k, b * P:(b + 1) * P], w_out[:, k, :],
                                       start=(k == 0), stop=(k == 1))
                mm.then_inc(s_o.sem, 1)

            pe.wait_ge(s_zero, 1)
            features(0, 0, range(6))
            pairs(pe, group)


def attention(nc, t, d, psum):
    PAIRS = ((0, 3, 0), (3, 2, 1), (5, 1, 2))
    NP = 6
    NROW = NP * XD
    UNITS = 4
    DIAG = P + XD
    with ExitStack() as ctx:
        def sb(name, shape, dt=F32):
            return ctx.enter_context(nc.sbuf_tensor(name, shape, dt))

        def sem(name, n=1, by=1):
            return Sem(ctx, nc, name, n, by)

        def raw(name):
            return ctx.enter_context(nc.semaphore(name))

        wqk = sb("wqk", [P, 2, P])
        wqk_hl = sb("wqk_hl", [P, 2, 2, P], F32R)
        w_v, w_o = sb("w_v", [P, P]), sb("w_o", [P, P])
        bqk = sb("bqk", [P, 2])
        b_v, b_o = sb("b_v", [P, P]), sb("b_o", [P, P])
        neg_i = sb("neg_i", [P, P], BF16)
        zeros = sb("zeros", [P, P])
        ones_d = sb("ones_d", [P, UNITS * DIAG])
        cin = sb("cin", [P, 2, GT])
        c_hl = sb("c_hl", [P, 2, GT], F32R)
        mask8 = sb("mask8", [P, 2, GS, P], U8)
        mask = sb("mask", [P, 2, GS, P], BF16)
        xs = sb("xs", [P, 2, GS, P])
        xT_hl = sb("xT_hl", [P, 2, GT], F32R)
        q_part, k_part = sb("q_part", [P, 3, GT], BF16), sb("k_part", [P, 3, GT], BF16)
        rest = sb("rest", [P, 2, GT])
        q_stack, k_stack = sb("q_stack", [P, 2, 8, GT], BF16), sb("k_stack", [P, 2, 8, GT], BF16)
        v_d = sb("v_d", [P, 2, GS, UNITS * DIAG])
        nmax = sb("nmax", [P, GS, XH])
        nrest = sb("nrest", [P, GS, XH])
        npart = sb("npart", [P, GS, 2, 3, 8], BF16)
        nmT = sb("nmT", [48, GT], BF16)
        prob = sb("prob", [P, 2, UNITS, UNITS, P])
        recip = sb("recip", [P, 2, P])
        ctxT = sb("ctxT", [P, GS, P])
        xb = sb("xb", [P, GS, P])
        res = sb("res_b", [P, GS, P])
        stats, mv = sb("stats_b", [P, GS, 6]), sb("mv_b", [P, GS, 2])
        rstd = sb("rstd_b", [P, GS])
        x1, x2, ident, ident32, norm_c = (t[k] for k in ("x1", "x2", "ident", "ident32", "norm_c"))

        d_c, d_mask, d_xs = DmaSem(ctx, nc, "ctx_in"), DmaSem(ctx, nc, "mask_in"), DmaSem(ctx, nc, "x1_staged")
        d_k, d_q, d_m = ([DmaSem(ctx, nc, f"{x}_stacked{h}_", 2) for h in range(2)] for x in ("k", "q", "max"))
        d_ks, d_qs = DmaSem(ctx, nc, "k_stored", 3), DmaSem(ctx, nc, "q_stored", 3)
        d_ms = [DmaSem(ctx, nc, f"max_stored{h}_") for h in range(2)]
        k_dram = nc.dram_tensor("k_scratch", (2, NP, P, GT), BF16, kind="Internal").ap()
        q_dram = nc.dram_tensor("q_scratch", (2, NP, P, GT), BF16, kind="Internal").ap()
        m_dram = nc.dram_tensor("max_scratch", (2, 2, 48, 2 * P), BF16, kind="Internal").ap()
        a_c, a_mask, a_x = sem("ctx_hi"), sem("mask_ready"), sem("x1T_hi")
        a_k, a_q = sem("k_act", 2), sem("q_act", 2)
        a_exp, a_mt = sem("prob_ready", 4 * GS), sem("nmT_ready", 2)
        v_c, v_x, v_k, v_q = sem("ctx_lo"), sem("x1T_lo"), sem("k_dve", 2), sem("q_dve", 2)
        v_v, v_norm, v_max = sem("v_ready", GS), sem("ctx_norm", 2 * GS), sem("max_ready", 4 * GS)
        v_split, v_res = sem("max_parts", 8), sem("res_b_ready", 1 + 2 * GS)
        p_x, p_k, p_q, p_v = sem("x1T_mm"), sem("k_mm"), sem("q_mm"), sem("v_mm")
        p_s, p_t, p_u = sem("score_mm", 4 * GS), sem("scoreT_mm", 4 * GS), sem("pv_mm", GS)
        p_mt, p_o = sem("max_mm", 2), sem("out_b_mm")
        g_x, g_out = sem("x1_biased"), sem("x2_ready", 4)
        g_init, v_init, d_w = raw("att_pool_init"), raw("att_dve_init"), raw("att_weights")
        sp_passed, dve_passed, pe_passed = raw("att_sp_passed"), raw("att_dve_passed"), raw("att_pe_passed")

        with nc.Block() as block:
            @block.sync
            def _(sp):
                for dst, src in ((wqk[:, 0, :], d["Wq"]), (wqk[:, 1, :], d["Wk"]), (w_v[:, :], d["Wv"]), (w_o[:, :], d["Wo"]),
                                 (bqk[:, 0:1], d["bq"].rearrange("(p o) -> p o", o=1)),
                                 (bqk[:, 1:2], d["bk"].rearrange("(p o) -> p o", o=1))):
                    sp.dma_start(dst, src).then_inc(d_w, 16)
                sp.dma_start(b_v[:, :], d["bv"].partition_broadcast(P)).then_inc(d_w, 16)
                sp.dma_start(b_o[:, :], d["bo"].partition_broadcast(P)).then_inc(d_w, 16)
                sp.wait_ge(d_w, 8 * 16)

            @block.gpsimd
            def _(pool):
                pool.memset(zeros[:, :], 0.0).then_inc(g_init, 1)
                pool.wait_ge(g_init, 1)
                pool.affine_select(out=neg_i[:, :], in_=zeros[:, :], compare_op=ALU.not_equal, fill=MASKED, base=0,
                                   pattern=[[1, P]], channel_multiplier=-1).then_inc(g_init, 1)

            @block.vector
            def _(dve):
                dve.memset(k_stack[:, :, :, :], 1.0)
                dve.memset(ones_d[:, :], 0.0).then_inc(v_init, 1)
                dve.memset(v_d[:, :, :, :], 0.0)
                dve.wait_ge(v_init, 1)
                dve.memset(ones_d[:, :].rearrange("p (i c) -> p i c", i=UNITS)[:, :, 0:P]
                           .rearrange("p i (c e) -> p i c e", e=4 * XD)[:, :, :, 0:XD], 1.0)
                dve.wait_ge(d_w, 8 * 16)
                dve.tensor_copy(wqk_hl[:, :, 0, :], wqk[:, :, :]).then_inc(v_init, 1)
                dve.wait_ge(v_init, 2)
                dve.tensor_tensor(wqk_hl[:, :, 1, :], wqk[:, :, :], wqk_hl[:, :, 0, :].bitcast(F32), ALU.subtract)

        TT0, TT1, SS0, SS1, U0, U1, PF, PO = psum
        block = ctx.enter_context(nc.Block())

        def unit_rows(u):
            return 64 * (u // 2), 4 * (u % 2)

        @block.sync
        def _(sp):
            for s in (d_c, d_mask, d_xs, *d_k, *d_q, *d_m, d_ks, d_qs, *d_ms):
                s.prime(sp)

            def loads(g, par):
                sp.wait_ge(p_v.sem, p_v.at(g - 2))
                sp.dma_start(cin[:, par, :], d["ctxT"][:, bass.ds(g * GT, GT)]).then_inc(d_c.sem[par], 16)
                sp.wait_ge(p_x.sem, p_x.at(g - 2))
                sp.dma_start(xs[:, par, :, :], x1[:, bass.ds(g * GS, GS), :]).then_inc(d_xs.sem[par], 16)
                sp.wait_ge(a_mask.sem, a_mask.at(g - 2))
                sp.dma_start(mask8[:, par, :, :].bitcast(mybir.dt.int32), d["mask"].rearrange("b q k -> q b k")[:, bass.ds(g * GS, GS), :])\
                    .then_inc(d_mask.sem[par], 16)

            def store(g, par, ready, part, via, stored, done, keys):
                sp.wait_ge(ready.sem, ready.at(g, 1))
                sp.wait_ge(done[0].sem[par], done[0].at(g - 2, par))
                sp.wait_ge(done[1].sem[par], done[1].at(g - 2, par))
                for r, n, a in PAIRS:
                    src = part[:, 0:n, :] if keys else bc(part[:, a, None, :], [P, n, GT])
                    sp.dma_start(via[par, r:r + n].rearrange("r p t -> p r t"), src).then_inc(stored.sem[par], 16)

            def stack(g, par, half, via, stored, dst, done):
                sp.wait_ge(stored.sem[par], stored.at(g, par))
                sp.sem_inc(sp_passed, 1)
                sp.wait_ge(p_t.sem, p_t.at(g - 2, 8 * half + 7))
                tok = slice(half * 2 * P, half * 2 * P + 2 * P)
                rows = via[par].rearrange("r (e j c) t -> j (r e) c t", e=XD, j=2)
                for j in range(2):
                    sp.dma_start(dst[64 * j:64 * j + NROW, par, :, tok], rows[j][:, :, tok]).then_inc(done[half].sem[par], 16)

            def store_max(g, par, half):
                sp.wait_ge(a_mt.sem, a_mt.at(g, half))
                sp.sem_inc(sp_passed, 1)
                sp.wait_ge(d_m[half].sem[par], d_m[half].at(g - 2, par))
                tok = slice(half * 2 * P, half * 2 * P + 2 * P)
                sp.dma_start(m_dram[par, half], nmT[:, tok]).then_inc(d_ms[half].sem[par], 16)

            def stack_max(g, par, half):
                sp.wait_ge(d_ms[half].sem[par], d_ms[half].at(g, par))
                tok = slice(half * 2 * P, half * 2 * P + 2 * P)
                for j in range(2):
                    row = 64 * j + NROW
                    sp.dma_start(q_stack[row:row + 3, par, :, tok],
                                 m_dram[par, half, 24 * j:24 * j + 24, :].rearrange("(r c) t -> r c t", r=3))\
                        .then_inc(d_m[half].sem[par], 16)

            def store_k(g, par):
                store(g, par, v_k, k_part, k_dram, d_ks, d_k, True)

            def store_q(g, par):
                store(g, par, v_q, q_part, q_dram, d_qs, d_q, False)

            def stacks(g, par, half):
                stack(g, par, half, k_dram, d_ks, k_stack, d_k)
                stack(g, par, half, q_dram, d_qs, q_stack, d_q)

            def group(g, par, left):
                if left == 2:
                    loads(g + 2, par)
                stack_max(g, par, 1)
                if left == 2:
                    store_k(g + 2, par)
                    store_q(g + 2, par)
                if left:
                    store_max(g + 1, 1 - par, 0)
                if left == 2:
                    stacks(g + 2, par, 0)
                if left:
                    stack_max(g + 1, 1 - par, 0)
                if left == 2:
                    stacks(g + 2, par, 1)
                if left:
                    store_max(g + 1, 1 - par, 1)

            for g in range(2):
                loads(g, g)
            for g in range(2):
                store_k(g, g)
                store_q(g, g)
                stacks(g, g, 0)
                stacks(g, g, 1)
            store_max(0, 0, 0)
            stack_max(0, 0, 0)
            store_max(0, 0, 1)
            pairs(sp, group)

        @block.gpsimd
        def _(pool):
            g_x.prime(pool)
            g_out.prime(pool)

            def group(g, par, left):
                pool.wait_ge(v_res.sem, v_res.at(g - 1, 0))
                pool.tensor_tensor(xb[:, :, :], x1[:, bass.ds(g * GS, GS), :], bc(b_o[:, None, :], [P, GS, P]), ALU.add)\
                    .then_inc(g_x.sem, 1)
                normalise_pool(pool, g, v_res, g_out, res, mv, rstd, norm_c, x2[:, bass.ds(g * GS, GS), :])

            pairs(pool, group)

        @block.scalar
        def _(act):
            for s in (a_c, a_mask, a_x, a_k, a_q, a_exp, a_mt):
                s.prime(act)

            def inputs(g, par):
                act.wait_ge(d_c.sem[par], d_c.at(g, par))
                act.wait_ge(p_k.sem, p_k.at(g - 1))
                act.activation(c_hl[:, 0, :], cin[:, par, :], ACT.Copy).then_inc(a_c.sem, 1)
                act.wait_ge(p_x.sem, p_x.at(g))
                act.wait_ge(p_q.sem, p_q.at(g - 1))
                act.activation(xT_hl[:, 0, :], PF[:, :], ACT.Copy).then_inc(a_x.sem, 1)

            def masks(g, par):
                act.wait_ge(d_mask.sem[par], d_mask.at(g, par))
                act.wait_ge(p_t.sem, p_t.at(g - 2, 4 * GS - 1))
                act.activation(mask[:, par, :, :], mask8[:, par, :, :], ACT.Copy).then_inc(a_mask.sem, 1)

            def parts(g, par, which, mm, mine, theirs, part, stored):
                act.wait_ge(mm.sem, mm.at(g))
                act.wait_ge(stored.sem[1 - par], stored.at(g - 1, 1 - par))
                act.activation(part[:, 0, :], PF[:, :], ACT.Identity, bias=bqk[:, which:which + 1]).then_inc(mine.sem, 1)
                act.wait_ge(theirs.sem, theirs.at(g, 0))
                act.activation(part[:, 1, :], rest[:, which, :], ACT.Copy).then_inc(mine.sem, 1)

            def exps(g, b):
                for u in range(UNITS):
                    act.wait_ge(p_t.sem, p_t.at(g, 4 * b + u))
                    act.wait_ge(p_u.sem, p_u.at(g, b - 2))
                    act.activation(prob[:, b % 2, u, :, :], (TT0, TT1)[u % 2][:, :], ACT.Exp, scale=XD ** -0.5)\
                        .then_inc(a_exp.sem, 1)

            def maxT(g, par, half):
                act.wait_ge(p_mt.sem, p_mt.at(g, half))
                act.wait_ge(d_ms[half].sem[1 - par], d_ms[half].at(g - 1, 1 - par))
                tok = slice(half * 2 * P, half * 2 * P + 2 * P)
                act.activation(nmT[:, tok], PF[:, :].bitcast(BF16)[0:48, tok], ACT.Copy).then_inc(a_mt.sem, 1)

            def k_parts(g, par):
                parts(g, par, 1, p_k, a_k, v_k, k_part, d_ks)

            def q_parts(g, par):
                parts(g, par, 0, p_q, a_q, v_q, q_part, d_qs)

            def group(g, par, left):
                exps(g, 0)
                if left == 2:
                    inputs(g + 2, par)
                exps(g, 1)
                if left == 2:
                    k_parts(g + 2, par)
                exps(g, 2)
                if left == 2:
                    q_parts(g + 2, par)
                if left:
                    maxT(g + 1, 1 - par, 0)
                exps(g, 3)
                if left == 2:
                    masks(g + 2, par)
                if left:
                    maxT(g + 1, 1 - par, 1)

            for g in range(2):
                inputs(g, g)
                k_parts(g, g)
                q_parts(g, g)
                masks(g, g)
            maxT(0, 0, 0)
            maxT(0, 0, 1)
            pairs(act, group)

        @block.vector
        def _(dve):
            for s in (v_c, v_x, v_k, v_q, v_v, v_norm, v_max, v_split, v_res):
                s.prime(dve)

            def inputs(g, par):
                dve.wait_ge(a_c.sem, a_c.at(g))
                dve.tensor_tensor(c_hl[:, 1, :], cin[:, par, :], c_hl[:, 0, :].bitcast(F32), ALU.subtract).then_inc(v_c.sem, 1)
                dve.wait_ge(a_x.sem, a_x.at(g))
                dve.tensor_tensor(xT_hl[:, 1, :], PF[:, :], xT_hl[:, 0, :].bitcast(F32), ALU.subtract).then_inc(v_x.sem, 1)

            def parts(g, which, theirs, mine, part):
                dve.wait_ge(theirs.sem, theirs.at(g, 0))
                dve.scalar_tensor_tensor(rest[:, which, :], PF[:, :], bqk[:, which:which + 1], part[:, 0, :],
                                         ALU.add, ALU.subtract).then_inc(mine.sem, 1)
                dve.wait_ge(theirs.sem, theirs.at(g, 1))
                dve.tensor_tensor(part[:, 2, :], rest[:, which, :], part[:, 1, :], ALU.subtract).then_inc(mine.sem, 1)

            def values(g, par):
                dve.wait_ge(p_v.sem, p_v.at(g))
                dve.wait_ge(p_u.sem, p_u.at(g - 2, GS - 1))
                for b in range(GS):
                    dst = v_d[:, par, b, :].rearrange("p (i c) -> p i c", i=UNITS)[:, :, 0:P]\
                        .rearrange("p i (c e) -> p i c e", e=4 * XD)[:, :, :, 0:XD]
                    dve.tensor_tensor(dst, PF[:, b * P:(b + 1) * P].rearrange("p (c i e) -> p i c e", c=4, i=4),
                                      b_v[:, :].rearrange("p (c i e) -> p i c e", c=4, i=4), ALU.add).then_inc(v_v.sem, 1)

            def maxima(g, b):
                for u in range(UNITS):
                    dve.wait_ge(p_s.sem, p_s.at(g, 4 * b + u))
                    dve.wait_ge(v_split.sem, v_split.at(g - 1, 7))
                    dve.tensor_reduce(nmax[:, b, 4 * u:4 * u + 4], (SS0, SS1)[u % 2][:, :].rearrange("p (i k) -> p i k", i=4),
                                      AX_X, ALU.max, negate=True).then_inc(v_max.sem, 1)

            def split_maxima(g, half):
                bs = slice(2 * half, 2 * half + 2)
                part = lambda r: npart[:, bs, :, r, :]
                of = lambda tile: tile[:, bs, :].rearrange("p b (j c) -> p b j c", j=2)
                dve.wait_ge(v_max.sem, v_max.at(g, 8 * half + 7))
                dve.wait_ge(p_mt.sem, p_mt.at(g - 1, half))
                dve.tensor_copy(part(0), of(nmax)).then_inc(v_split.sem, 1)
                dve.wait_ge(v_split.sem, v_split.at(g, 4 * half))
                dve.tensor_tensor(of(nrest), of(nmax), part(0), ALU.subtract).then_inc(v_split.sem, 1)
                dve.wait_ge(v_split.sem, v_split.at(g, 4 * half + 1))
                dve.tensor_copy(part(1), of(nrest)).then_inc(v_split.sem, 1)
                dve.wait_ge(v_split.sem, v_split.at(g, 4 * half + 2))
                dve.tensor_tensor(part(2), of(nrest), part(1), ALU.subtract).then_inc(v_split.sem, 1)

            def norm(g, b):
                bank = (U0, U1)[b % 2]
                dve.wait_ge(p_u.sem, p_u.at(g, b))
                dve.reciprocal(recip[:, b % 2, :], bank[:, P:2 * P]).then_inc(v_norm.sem, 1)
                dve.wait_ge(v_norm.sem, v_norm.at(g, 2 * b))
                dve.wait_ge(p_o.sem, p_o.at(g - 1))
                dve.tensor_tensor(ctxT[:, b, :], bank[:, 0:P], recip[:, b % 2, :], ALU.mult).then_inc(v_norm.sem, 1)

            def k_parts(g):
                parts(g, 1, a_k, v_k, k_part)

            def q_parts(g):
                parts(g, 0, a_q, v_q, q_part)

            def group(g, par, left):
                if left:
                    maxima(g + 1, 0)
                if left == 2:
                    inputs(g + 2, par)
                if left:
                    maxima(g + 1, 1)
                    split_maxima(g + 1, 0)
                if left == 2:
                    k_parts(g + 2)
                norm(g, 0)
                if left:
                    maxima(g + 1, 2)
                if left == 2:
                    q_parts(g + 2)
                norm(g, 1)
                if left:
                    maxima(g + 1, 3)
                    split_maxima(g + 1, 1)
                norm(g, 2)
                norm(g, 3)
                if left == 2:
                    values(g + 2, par)
                dve.wait_ge(p_o.sem, p_o.at(g))
                dve.wait_ge(g_x.sem, g_x.at(g))
                residual_dve(dve, g, PO, xb[:, :, :], g_out, v_res, dve_passed, res, stats, mv)

            for g in range(2):
                inputs(g, g)
                k_parts(g)
                q_parts(g)
                values(g, g)
            for b in range(GS):
                maxima(0, b)
                if b % 2:
                    split_maxima(0, b // 2)
            pairs(dve, group)

        @block.tensor
        def _(pe):
            for s in (p_x, p_k, p_q, p_v, p_s, p_t, p_u, p_mt, p_o):
                s.prime(pe)

            def x1T(g, par):
                pe.wait_ge(d_xs.sem[par], d_xs.at(g, par))
                pe.wait_ge(a_mt.sem, a_mt.at(g - 2, 1))
                pe.wait_ge(v_v.sem, v_v.at(g - 1, GS - 1))
                for b in range(GS):
                    mm = pe.transpose(PF[:, b * P:(b + 1) * P], xs[:, par, b, :], ident32[:, :])
                mm.then_inc(p_x.sem, 1)

            def project(g, which, src, ready, freed, done):
                pe.wait_ge(ready.sem, ready.at(g))
                pe.wait_ge(freed.sem, freed.at(g, 0))
                for n, (a, v) in enumerate(((0, 0), (0, 1), (1, 0))):
                    mm = pe.matmul(PF[:, :], wqk_hl[:, which, a, :], src[:, v, :], start=(n == 0), stop=(n == 2))
                mm.then_inc(done.sem, 1)

            def values(g, par, freed):
                pe.wait_ge(*freed)
                for b in range(GS):
                    mm = pe.matmul(PF[:, b * P:(b + 1) * P], cin[:, par, b * P:(b + 1) * P], w_v[:, :], start=True, stop=True)
                mm.then_inc(p_v.sem, 1)

            def k_proj(g):
                project(g, 1, c_hl, v_c, v_x, p_k)

            def q_proj(g):
                project(g, 0, xT_hl, v_x, v_k, p_q)

            def stacked(g, par, half):
                pe.wait_ge(d_k[half].sem[par], d_k[half].at(g, par))
                pe.wait_ge(d_q[half].sem[par], d_q[half].at(g, par))
                pe.wait_ge(a_mask.sem, a_mask.at(g))

            def scores(g, par, b, u):
                tok = slice(b * P, (b + 1) * P)
                row, c0 = unit_rows(u)
                bank = (SS0, SS1)[u % 2]
                pe.wait_ge(v_max.sem, v_max.at(g, 4 * b + u - 2))
                pe.matmul(bank[:, :], neg_i[:, :], bc(mask[:, par, b, None, :], [P, 4, P]), start=True, stop=False,
                          skip_group_check=True)
                for i in range(4):
                    mm = pe.matmul(bank[:, i * P:(i + 1) * P], q_stack[row:row + NROW, par, c0 + i, tok],
                                   k_stack[row:row + NROW, par, c0 + i, tok], start=False, stop=True, skip_group_check=True)
                mm.then_inc(p_s.sem, 1)

            def scoresT(g, par, b, u):
                tok = slice(b * P, (b + 1) * P)
                row, c0 = unit_rows(u)
                bank = (TT0, TT1)[u % 2]
                pe.wait_ge(a_exp.sem, a_exp.at(g, 4 * b + u - 2))
                pe.matmul(bank[:, :], mask[:, par, b, :], bc(neg_i[:, None, :], [P, 4, P]), start=True, stop=False,
                          skip_group_check=True)
                for i in range(4):
                    mm = pe.matmul(bank[:, i * P:(i + 1) * P], k_stack[row:row + NROW + 3, par, c0 + i, tok],
                                   q_stack[row:row + NROW + 3, par, c0 + i, tok], start=False, stop=True,
                                   skip_group_check=True)
                mm.then_inc(p_t.sem, 1)

            def both(g, par, b, left):
                pe.wait_ge(d_m[b // 2].sem[par], d_m[b // 2].at(g, par))
                for u in range(UNITS):
                    scoresT(g, par, b, u)
                    if left:
                        if b % 2 == 0 and u == 0:
                            stacked(g + 1, 1 - par, b // 2)
                        scores(g + 1, 1 - par, b, u)

            def weigh(g, par, b):
                bank = (U0, U1)[b % 2]
                pe.wait_ge(a_exp.sem, a_exp.at(g, 4 * b + 3))
                pe.wait_ge(v_v.sem, v_v.at(g, b))
                pe.wait_ge(v_norm.sem, v_norm.at(g, 2 * b - 3))
                for k, src in enumerate((v_d[:, par, b, :], ones_d[:, :])):
                    for i in range(4):
                        for u in range(UNITS):
                            mm = pe.matmul(bank[32 * u:32 * u + 32, k * P:(k + 1) * P], src[:, i * P + 32 * u:i * P + 32 * u + 32],
                                           prob[:, b % 2, u, i, :], start=(i == 0), stop=(i == 3), skip_group_check=True)
                mm.then_inc(p_u.sem, 1)

            def max_rows(g, half, freed):
                pe.wait_ge(v_split.sem, v_split.at(g, 4 * half + 3))
                pe.wait_ge(*freed)
                pe.sem_inc(pe_passed, 1)
                for b in range(2 * half, 2 * half + 2):
                    mm = pe.transpose(PF[:, :].bitcast(BF16)[0:48, b * P:(b + 1) * P],
                                      npart[:, b, :, :, :].rearrange("p j r c -> p (j r c)"), ident[:, :])
                mm.then_inc(p_mt.sem, 1)

            def output(g):
                pe.wait_ge(v_norm.sem, v_norm.at(g, 7))
                pe.wait_ge(v_res.sem, v_res.at(g - 1, 0))
                for b in range(GS):
                    mm = pe.matmul(PO[:, b * P:(b + 1) * P], ctxT[:, b, :], w_o[:, :], start=True, stop=True)
                mm.then_inc(p_o.sem, 1)

            def group(g, par, left):
                both(g, par, 0, left)
                if left == 2:
                    x1T(g + 2, par)
                both(g, par, 1, left)
                if left == 2:
                    k_proj(g + 2)
                weigh(g, par, 0)
                both(g, par, 2, left)
                if left == 2:
                    q_proj(g + 2)
                weigh(g, par, 1)
                if left:
                    max_rows(g + 1, 0, (v_q.sem, v_q.at(g + 2, 0)) if left == 2 else (v_v.sem, v_v.at(g + 1, GS - 1)))
                both(g, par, 3, left)
                weigh(g, par, 2)
                if left:
                    max_rows(g + 1, 1, (a_mt.sem, a_mt.at(g + 1, 0)))
                weigh(g, par, 3)
                if left == 2:
                    values(g + 2, par, (a_mt.sem, a_mt.at(g + 1, 1)))
                output(g)

            for g in range(2):
                x1T(g, g)
                k_proj(g)
                q_proj(g)
                values(g, g, (v_q.sem, v_q.at(g, 0)))
            for b in range(GS):
                if b % 2 == 0:
                    stacked(0, 0, b // 2)
                for u in range(UNITS):
                    scores(0, 0, b, u)
                if b == 1:
                    max_rows(0, 0, (v_v.sem, v_v.at(1, GS - 1)))
                if b == 3:
                    max_rows(0, 1, (a_mt.sem, a_mt.at(0, 0)))
            pairs(pe, group)


def experts(nc, t, d, out, psum):
    NC = CHUNKS + 1
    SENTINEL, TAKEN = -3.0e38, 3.0e38
    with ExitStack() as ctx:
        def sb(name, shape, dt=F32):
            return ctx.enter_context(nc.sbuf_tensor(name, shape, dt))

        def sem(name, n=1, by=1):
            return Sem(ctx, nc, name, n, by)

        def raw(name):
            return ctx.enter_context(nc.semaphore(name))

        w_raw = sb("w_raw", [P, 2, NC, P])
        w_up = sb("w_up", [P, 2, 2, NC, P], F32R)
        w_down = sb("w_down", [P, NC, P])
        wg_raw = sb("wg_raw", [P, EXPERTS])
        w_gate = sb("w_gate", [P, 2, EXPERTS], F32R)
        bias = sb("bias", [P, EXPERTS])
        ones32 = sb("ones32", [32, CHUNKS, 2, EI])
        pick = sb("pick", [32, CHUNKS, 2, EI])
        spread = sb("spread", [32, CHUNKS, P], F32R)
        before = sb("before", [P, 4, 4])
        xs = sb("xs_c", [P, 2, GS, P])
        xT_hl = sb("xT_hl_c", [P, 2, 2, GT], F32R)
        th16 = sb("th16", [P, GS, EXPERTS])
        score = sb("score", [P, GS, EXPERTS])
        biased = sb("biased", [P, GS, EXPERTS])
        hi2, lo2, sum2 = (sb(n, [P, GS * 4, 2]) for n in ("hi2", "lo2", "sum2"))
        cross, gsum = sb("cross", [P, GS * 4]), sb("gsum", [P, GS, 4])
        above, tie = sb("above", [P, GS, 4, 4]), sb("tie", [P, GS, 4, 4])
        rank, penalty = sb("rank", [P, GS, 4]), sb("penalty", [P, GS, 4])
        open_ = sb("open_", [P, GS, EXPERTS + 4])
        top = sb("top", [P, GS, 8])
        marked = sb("marked", [P, GS, EXPERTS + 4])
        chosen = sb("chosen", [P, GS, EXPERTS])
        wsum = sb("wsum", [P, GS])
        cw = sb("cw", [P, GS, EXPERTS])
        cw_hl = sb("cw_hl", [P, GS, 2, EXPERTS], F32R)
        cwT = sb("cwT", [32, 2, GT], F32R)
        sg = sb("sg", [P, 2, GT])
        gu = sb("gu", [P, 2, GT])
        hid = sb("hid", [P, NC, GT])
        res = sb("res_c", [P, GS, P])
        normed = sb("normed", [P, 2, GS, P])
        stats, mv = sb("stats_c", [P, GS, 6]), sb("mv_c", [P, GS, 2])
        rstd = sb("rstd_c", [P, GS])
        x2, ident32, norm_c = t["x2"], t["ident32"], t["norm_c"]

        d_x, d_out = DmaSem(ctx, nc, "x2_staged"), DmaSem(ctx, nc, "out_stored")
        p_x, p_l, p_c = sem("x2T_mm"), sem("logit_mm"), sem("cwT_mm")
        p_g, p_u, p_w, p_d = sem("gate_mm", NC), sem("up_mm", NC), sem("weight_mm", CHUNKS), sem("down_mm", NC)
        a_x, a_l, a_c, a_s = sem("x2T_hi"), sem("logit_tanh"), sem("cwT_ready"), sem("silu_ready", NC)
        v_x, v_sc, v_gu, v_hid = sem("x2T_lo"), sem("scores_ready", 2), sem("gu_ready", NC), sem("hid_ready", CHUNKS)
        v_sel, v_res = sem("select_dve", 18), sem("res_c_ready", 1 + 2 * GS)
        v_grp, g_out = sem("groups_ranked", 13), sem("out_ready", 4)
        d_w, v_init, g_init = raw("expert_weights"), raw("expert_dve_init"), raw("expert_pool_init")
        dve_passed = raw("expert_dve_passed")

        with nc.Block() as block:
            @block.sync
            def _(sp):
                for k, (e, sh) in enumerate((("WgT", "Ws_gT"), ("WuT", "Ws_uT"))):
                    sp.dma_start(w_raw[:, k, 0, :], d[sh]).then_inc(d_w, 16)
                    sp.dma_start(w_raw[:, k, 1:, :], d[e].rearrange("p (c n) -> p c n", n=P)).then_inc(d_w, 16)
                sp.dma_start(w_down[:, 0, :], d["Ws_dT"]).then_inc(d_w, 16)
                sp.dma_start(w_down[:, 1:, :], d["WdT"].rearrange("(c p) n -> p c n", p=P)).then_inc(d_w, 16)
                sp.dma_start(wg_raw[:, :], d["gate_wT"]).then_inc(d_w, 16)
                sp.dma_start(bias[:, :], d["gate_bias"].partition_broadcast(P)).then_inc(d_w, 16)
                sp.wait_ge(d_w, 8 * 16)

            @block.gpsimd
            def _(pool):
                pool.memset(ones32[:, :, :, :], 1.0).then_inc(g_init, 1)
                pool.memset(before[:, :, :], 1.0).then_inc(g_init, 1)
                pool.wait_ge(g_init, 2)
                pool.affine_select(out=pick[:, :, :, :], in_=ones32[:, :, :, :], compare_op=ALU.is_equal, fill=0.0, base=0,
                                   pattern=[[-2, CHUNKS], [-1, 2], [0, EI]], channel_multiplier=1).then_inc(g_init, 1)
                pool.wait_ge(g_init, 3)
                pool.affine_select(out=pick[:, :, :, :], in_=pick[:, :, :, :], compare_op=ALU.not_equal, fill=1.0, base=-EXPERTS,
                                   pattern=[[-2, CHUNKS], [-1, 2], [0, EI]], channel_multiplier=1).then_inc(g_init, 1)
                pool.affine_select(out=before[:, :, :], in_=before[:, :, :], compare_op=ALU.is_gt, fill=0.0, base=0,
                                   pattern=[[1, 4], [-1, 4]], channel_multiplier=0).then_inc(g_init, 1)

            @block.vector
            def _(dve):
                dve.memset(open_[:, :, EXPERTS:], SENTINEL)
                dve.memset(top[:, :, 4:], SENTINEL)
                dve.wait_ge(d_w, 8 * 16)
                for k in range(2):
                    dve.tensor_copy(w_up[:, k, 0], w_raw[:, k]).then_inc(v_init, 1)
                dve.tensor_copy(w_gate[:, 0, :], wg_raw[:, :]).then_inc(v_init, 1)
                dve.wait_ge(v_init, 3)
                for k in range(2):
                    dve.tensor_tensor(w_up[:, k, 1], w_raw[:, k], w_up[:, k, 0].bitcast(F32), ALU.subtract)
                dve.tensor_tensor(w_gate[:, 1, :], wg_raw[:, :], w_gate[:, 0, :].bitcast(F32), ALU.subtract)
                dve.wait_ge(g_init, 5)
                dve.tensor_copy(spread[:, :, :], pick[:, :, :, :].rearrange("p c e i -> p c (e i)"))

        GG, UU, WW, PF, PO = psum[0:2], psum[2:4], psum[4:6], psum[6], psum[7]
        block = ctx.enter_context(nc.Block())

        @block.sync
        def _(sp):
            d_x.prime(sp)
            d_out.prime(sp)

            def load(g, par):
                sp.wait_ge(p_x.sem, p_x.at(g - 2))
                sp.dma_start(xs[:, par, :, :], x2[:, bass.ds(g * GS, GS), :]).then_inc(d_x.sem[par], 16)

            def group(g, par, left):
                if left == 2:
                    load(g + 2, par)
                sp.wait_ge(g_out.sem, g_out.at(g, 3))
                sp.dma_start(out.rearrange("(b t) d -> t b d", t=P)[:, bass.ds(g * GS, GS), :], normed[:, par, :, :])\
                    .then_inc(d_out.sem[par], 16)

            load(0, 0)
            load(1, 1)
            pairs(sp, group)
            for g in (NG - 2, NG - 1):
                sp.wait_ge(d_out.sem[g % 2], d_out.at(g, g % 2))

        @block.gpsimd
        def _(pool):
            g_out.prime(pool)

            def group(g, par, left):
                normalise_pool(pool, g, v_res, g_out, res, mv, rstd, norm_c, normed[:, par, :, :],
                               (d_out.sem[par], d_out.at(g - 2, par)))

            pairs(pool, group)

        @block.scalar
        def _(act):
            for s in (a_x, a_l, a_c, a_s):
                s.prime(act)

            def hi(g, par):
                act.wait_ge(p_x.sem, p_x.at(g))
                act.wait_ge(p_u.sem, p_u.at(g - 2, NC - 1))
                act.activation(xT_hl[:, par, 0, :], PF[:, :], ACT.Copy).then_inc(a_x.sem, 1)

            def logits(g):
                act.wait_ge(p_l.sem, p_l.at(g))
                act.wait_ge(v_sc.sem, v_sc.at(g - 1, 0))
                act.activation(th16[:, :, :], PF[:, 0:GS * EXPERTS], ACT.Tanh, scale=0.5).then_inc(a_l.sem, 1)

            def weights(g, par):
                act.wait_ge(p_c.sem, p_c.at(g))
                act.wait_ge(p_w.sem, p_w.at(g - 2, CHUNKS - 1))
                act.activation(cwT[:, par, :], PF[0:32, :], ACT.Copy).then_inc(a_c.sem, 1)

            def silu(g, par, c):
                k = (par + c) % 2
                act.wait_ge(p_g.sem, p_g.at(g, c))
                act.wait_ge(v_gu.sem, v_gu.at(g, c - 2))
                act.activation(sg[:, k, :], GG[k][:, :], ACT.Silu).then_inc(a_s.sem, 1)

            def group(g, par, left):
                nxt = (g + 1, 1 - par)
                for c in range(2, NC):
                    silu(g, par, c)
                    if left and c == 2:
                        hi(*nxt)
                    if left and c == 3:
                        logits(g + 1)
                if left:
                    silu(*nxt, 0)
                    weights(*nxt)
                    silu(*nxt, 1)

            hi(0, 0)
            logits(0)
            silu(0, 0, 0)
            weights(0, 0)
            silu(0, 0, 1)
            pairs(act, group)

        @block.vector
        def _(dve):
            for s in (v_x, v_sc, v_grp, v_gu, v_hid, v_sel, v_res):
                s.prime(dve)

            def lo(g, par):
                dve.wait_ge(a_x.sem, a_x.at(g))
                dve.tensor_tensor(xT_hl[:, par, 1, :], PF[:, :], xT_hl[:, par, 0, :].bitcast(F32), ALU.subtract).then_inc(v_x.sem, 1)

            def scores(g):
                dve.wait_ge(a_l.sem, a_l.at(g))
                dve.wait_ge(v_sel.sem, v_sel.at(g - 1, 11))
                dve.tensor_scalar(score[:, :, :], th16[:, :, :], 0.5, 0.5, ALU.mult, ALU.add).then_inc(v_sc.sem, 1)
                dve.wait_ge(v_sc.sem, v_sc.at(g, 0))
                dve.wait_ge(v_grp.sem, v_grp.at(g - 1, 1))
                dve.tensor_tensor(biased[:, :, :], score[:, :, :], bc(bias[:, None, :], [P, GS, EXPERTS]), ALU.add)\
                    .then_inc(v_sc.sem, 1)

            def groups_of(g):
                def step(k, ins):
                    ins.then_inc(v_grp.sem, 1)
                    dve.wait_ge(v_grp.sem, v_grp.at(g, k))

                dve.wait_ge(v_sc.sem, v_sc.at(g, 1))
                four = biased[:, :, :].rearrange("p b (q n e) -> p (b q) n e", q=4, n=2)
                step(0, dve.tensor_tensor(hi2[:, :, :], four[:, :, :, 0], four[:, :, :, 1], ALU.max))
                step(1, dve.tensor_tensor(lo2[:, :, :], four[:, :, :, 0], four[:, :, :, 1], ALU.min))
                step(2, dve.tensor_tensor(sum2[:, :, :], hi2[:, :, :], lo2[:, :, :], ALU.add))
                step(3, dve.tensor_tensor(cross[:, :], hi2[:, :, 0], hi2[:, :, 1], ALU.add))
                gs = gsum[:, :, :].rearrange("p b q -> p (b q)")
                step(4, dve.tensor_tensor(gs, sum2[:, :, 0], sum2[:, :, 1], ALU.max))
                step(5, dve.tensor_tensor(gs, gs, cross[:, :], ALU.max))
                mine, other = bc(gsum[:, :, :, None], [P, GS, 4, 4]), bc(gsum[:, :, None, :], [P, GS, 4, 4])
                step(6, dve.tensor_tensor(above[:, :, :, :], other, mine, ALU.is_gt))
                step(7, dve.tensor_tensor(tie[:, :, :, :], other, mine, ALU.is_ge))
                step(8, dve.tensor_tensor(tie[:, :, :, :], tie[:, :, :, :], bc(before[:, None, :, :], [P, GS, 4, 4]), ALU.mult))
                step(9, dve.tensor_tensor(above[:, :, :, :], above[:, :, :, :], tie[:, :, :, :], ALU.max))
                step(10, dve.tensor_tensor(tie[:, :, :, 0:2], above[:, :, :, 0:2], above[:, :, :, 2:4], ALU.add))
                step(11, dve.tensor_tensor(rank[:, :, :], tie[:, :, :, 0], tie[:, :, :, 1], ALU.add))
                dve.wait_ge(v_sel.sem, v_sel.at(g - 1, 0))
                step(12, dve.tensor_scalar(penalty[:, :, :], rank[:, :, :], 2.0, -1.0e30, ALU.is_ge, ALU.mult))

            def select(g):
                def step(k, ins):
                    ins.then_inc(v_sel.sem, 1)
                    dve.wait_ge(v_sel.sem, v_sel.at(g, k))

                dve.wait_ge(v_grp.sem, v_grp.at(g, 12))
                step(0, dve.tensor_tensor(open_[:, :, 0:EXPERTS].rearrange("p b (q e) -> p b q e", q=4),
                                          biased[:, :, :].rearrange("p b (q e) -> p b q e", q=4),
                                          bc(penalty[:, :, :, None], [P, GS, 4, 4]), ALU.add))
                dve.sem_inc(dve_passed, 1)
                for b in range(GS):
                    dve.max(top[:, b, :], open_[:, b, 0:EXPERTS]).then_inc(v_sel.sem, 1)
                dve.wait_ge(v_sel.sem, v_sel.at(g, 4))
                step(5, dve.memset(top[:, :, 4:], SENTINEL))
                dve.sem_inc(dve_passed, 1)
                for b in range(GS):
                    dve.match_replace(marked[:, b, :], top[:, b, :], open_[:, b, :], TAKEN).then_inc(v_sel.sem, 1)
                dve.wait_ge(v_sel.sem, v_sel.at(g, 9))

            def share(g):
                def step(k, ins):
                    ins.then_inc(v_sel.sem, 1)
                    dve.wait_ge(v_sel.sem, v_sel.at(g, k))

                step(10, dve.tensor_scalar(chosen[:, :, :], marked[:, :, 0:EXPERTS], TAKEN, None, ALU.is_ge))
                step(11, dve.tensor_tensor(chosen[:, :, :], chosen[:, :, :], score[:, :, :], ALU.mult))
                step(12, dve.tensor_reduce(wsum[:, :], chosen[:, :, :], AX_X, ALU.add))
                step(13, dve.tensor_scalar(wsum[:, :], wsum[:, :], 1e-20, None, ALU.add))
                step(14, dve.reciprocal(wsum[:, :], wsum[:, :]))
                step(15, dve.scalar_tensor_tensor(cw[:, :, :], chosen[:, :, :], SCALE, bc(wsum[:, :, None], [P, GS, EXPERTS]),
                                                  ALU.mult, ALU.mult))
                dve.wait_ge(p_c.sem, p_c.at(g - 1))
                step(16, dve.tensor_copy(cw_hl[:, :, 0, :], cw[:, :, :]))
                step(17, dve.tensor_tensor(cw_hl[:, :, 1, :], cw[:, :, :], cw_hl[:, :, 0, :].bitcast(F32), ALU.subtract))

            def hidden(g, par, c):
                k = (par + c) % 2
                dve.wait_ge(a_s.sem, a_s.at(g, c))
                dve.wait_ge(p_u.sem, p_u.at(g, c))
                dve.wait_ge(p_d.sem, p_d.at(g - 1, c))
                if c:
                    dve.wait_ge(v_hid.sem, v_hid.at(g, max(c - 3, -1)))
                dst = hid[:, 0, :] if c == 0 else gu[:, k, :]
                dve.tensor_tensor(dst, sg[:, k, :], UU[k][:, :], ALU.mult).then_inc(v_gu.sem, 1)
                if c:
                    dve.wait_ge(v_gu.sem, v_gu.at(g, c))
                    dve.wait_ge(p_w.sem, p_w.at(g, c - 1))
                    dve.tensor_tensor(hid[:, c, :], gu[:, k, :], WW[(c - 1) % 2][:, :], ALU.mult).then_inc(v_hid.sem, 1)

            def group(g, par, left):
                nxt = (g + 1, 1 - par)
                for c in range(2, NC):
                    hidden(g, par, c)
                    if left and c == 2:
                        lo(*nxt)
                    if left and c == 3:
                        scores(g + 1)
                    if left and c == 4:
                        groups_of(g + 1)
                    if left and c == 5:
                        select(g + 1)
                    if left and c == 6:
                        share(g + 1)
                if left:
                    hidden(*nxt, 0)
                    hidden(*nxt, 1)
                dve.wait_ge(p_d.sem, p_d.at(g, NC - 1))
                residual_dve(dve, g, PO, x2[:, bass.ds(g * GS, GS), :], g_out, v_res, dve_passed, res, stats, mv, times=2.0)

            lo(0, 0)
            scores(0)
            hidden(0, 0, 0)
            groups_of(0)
            select(0)
            share(0)
            hidden(0, 0, 1)
            pairs(dve, group)

        @block.tensor
        def _(pe):
            for s in (p_x, p_l, p_c, p_g, p_u, p_w, p_d):
                s.prime(pe)

            def x2T(g, par):
                pe.wait_ge(d_x.sem[par], d_x.at(g, par))
                pe.wait_ge(a_c.sem, a_c.at(g - 1))
                for b in range(GS):
                    mm = pe.transpose(PF[:, b * P:(b + 1) * P], xs[:, par, b, :], ident32[:, :])
                mm.then_inc(p_x.sem, 1)

            def logits(g, par):
                pe.wait_ge(v_x.sem, v_x.at(g))
                for b in range(GS):
                    for n, (a, v) in enumerate(((0, 0), (0, 1), (1, 0))):
                        mm = pe.matmul(PF[:, b * EXPERTS:(b + 1) * EXPERTS], xT_hl[:, par, a, b * P:(b + 1) * P], w_gate[:, v, :],
                                       start=(n == 0), stop=(n == 2))
                mm.then_inc(p_l.sem, 1)

            def weights(g):
                pe.wait_ge(v_sel.sem, v_sel.at(g, 17))
                pe.wait_ge(a_l.sem, a_l.at(g))
                for b in range(GS):
                    mm = pe.transpose(PF[0:32, b * P:(b + 1) * P],
                                      cw_hl[:, b, :, :].rearrange("p v e -> p (v e)").bitcast(F32), ident32[:, :])
                mm.then_inc(p_c.sem, 1)

            def up(g, par, c):
                k = (par + c) % 2
                for which, bank, freed, done in ((0, GG[k], a_s, p_g), (1, UU[k], v_gu, p_u)):
                    pe.wait_ge(freed.sem, freed.at(g, c - 2))
                    for n, (a, v) in enumerate(((0, 0), (0, 1), (1, 0))):
                        mm = pe.matmul(bank[:, :], w_up[:, which, a, c, :], xT_hl[:, par, v, :], start=(n == 0), stop=(n == 2))
                    mm.then_inc(done.sem, 1)
                if c:
                    pe.wait_ge(a_c.sem, a_c.at(g))
                    pe.wait_ge(v_hid.sem, v_hid.at(g, c - 3))
                    pe.matmul(WW[(c - 1) % 2][:, :], spread[:, c - 1, :], cwT[:, par, :], start=True, stop=True)\
                        .then_inc(p_w.sem, 1)

            def down(g, c):
                if c == 0:
                    pe.wait_ge(v_gu.sem, v_gu.at(g, 0))
                    pe.wait_ge(v_res.sem, v_res.at(g - 1, 0))
                else:
                    pe.wait_ge(v_hid.sem, v_hid.at(g, c - 1))
                for b in range(GS):
                    mm = pe.matmul(PO[:, b * P:(b + 1) * P], hid[:, c, b * P:(b + 1) * P], w_down[:, c, :],
                                   start=(c == 0 and b == 0), stop=(c == NC - 1), skip_group_check=True)
                mm.then_inc(p_d.sem, 1)

            def group(g, par, left):
                nxt = (g + 1, 1 - par)
                for c in range(2, NC):
                    up(g, par, c)
                    down(g, c - 2)
                    if left and c == 2:
                        x2T(*nxt)
                    if left and c == 3:
                        logits(*nxt)
                if left:
                    up(*nxt, 0)
                    weights(g + 1)
                down(g, NC - 2)
                if left:
                    up(*nxt, 1)
                down(g, NC - 1)

            x2T(0, 0)
            logits(0, 0)
            up(0, 0, 0)
            weights(0)
            up(0, 0, 1)
            pairs(pe, group)


def build(nc, d, out, stop_at=None):
    with ExitStack() as ctx:
        psum = [ctx.enter_context(nc.psum_tensor(f"bank{k}", [P, 512], F32)) for k in range(8)]
        t = {k: ctx.enter_context(nc.sbuf_tensor(k, [P, NSEQ, P], F32)) for k in ("x1", "x2")}
        t["ident"] = ctx.enter_context(nc.sbuf_tensor("ident", [P, P], BF16))
        t["ident32"] = ctx.enter_context(nc.sbuf_tensor("ident32", [P, P], F32))
        t["norm_c"] = ctx.enter_context(nc.sbuf_tensor("norm_c", [P, 2, GS], F32))
        mixer(nc, t, d, psum, stop_at)
        if stop_at in ("small", "trig", "mixer"):
            return
        attention(nc, t, d, psum)
        experts(nc, t, d, out, psum)


_DRAM = {
    "x": "x", "xT": "x", "ctxT": "ctx_1024", "mask": "mask_Bx1xSxS2_bk1", "w_inT": "L0_attn_w_in", "w_outT": "L0_attn_w_out",
    "dt_bias": "L0_attn_dt_bias", "D": "L0_attn_D", "Wq": "L0_xattn_Wq", "bq": "L0_xattn_bq", "Wk": "L0_xattn_Wk",
    "bk": "L0_xattn_bk", "Wv": "L0_xattn_Wv", "bv": "L0_xattn_bv", "Wo": "L0_xattn_Wo", "bo": "L0_xattn_bo",
    "gate_wT": "L0_ffn_gate_w", "gate_bias": "L0_ffn_gate_bias", "WgT": "L0_ffn_Wg", "WuT": "L0_ffn_Wu", "WdT": "L0_ffn_Wd",
    "Ws_gT": "L0_ffn_Ws_g", "Ws_uT": "L0_ffn_Ws_u", "Ws_dT": "L0_ffn_Ws_d",
}


def lay_out(inputs):
    import numpy as np
    a = {k: np.asarray(inputs[v]) for k, v in _DRAM.items()}
    a["x"] = a["x"].reshape(-1, P)
    a["xT"] = a["xT"].reshape(-1, P).T
    a["ctxT"] = a["ctxT"].reshape(-1, P).T
    a["mask"] = np.ascontiguousarray(a["mask"]).reshape(NSEQ, P, P).view(np.int32)
    for k in ("Wq", "bq", "Wk", "bk"):
        a[k] = a[k].reshape(-1, XH, XD).swapaxes(-1, -2).reshape(a[k].shape)
    for k in ("w_inT", "w_outT", "gate_wT", "Ws_gT", "Ws_uT", "Ws_dT"):
        a[k] = a[k].T
    a["WgT"] = a["WgT"].reshape(EXPERTS * EI, P).T
    a["WuT"] = a["WuT"].reshape(EXPERTS * EI, P).T
    a["WdT"] = a["WdT"].transpose(0, 2, 1).reshape(EXPERTS * EI, P)
    return {k: np.ascontiguousarray(v) for k, v in a.items()}


def kernel(**inputs):
    import concourse.bacc as bacc
    from concourse.bass_utils import run_bass_kernel_spmd

    nc = bacc.Bacc("TRN2", target_bir_lowering=False, num_devices=1)
    arrays = lay_out(inputs)
    d = {k: nc.dram_tensor(k + "_in", a.shape, mybir.dt.from_np(a.dtype), kind="ExternalInput").ap() for k, a in arrays.items()}
    out = nc.dram_tensor("out", (NSEQ * P, P), F32, kind="ExternalOutput").ap()
    build(nc, d, out)
    r = run_bass_kernel_spmd(nc, [{k + "_in": a for k, a in arrays.items()}], core_ids=[0])
    return r.results[0]["out"].reshape(NSEQ, P, P)
```

```python
from contextlib import ExitStack

import concourse.bass as bass
from concourse import mybir

F32 = mybir.dt.float32
F32R = mybir.dt.float32r
BF16 = mybir.dt.bfloat16
U8 = mybir.dt.uint8
ALU = mybir.AluOpType
ACT = mybir.ActivationFunctionType
AX_X = mybir.AxisListType.X

P = 128
NSEQ = 32
GS = 4
NG = NSEQ // GS
GT = GS * P
D_INNER = 256
HEADS = 4
HD = D_INNER // HEADS
ROT = 32
PLAIN = P - ROT
SMALL = 3 * HEADS + ROT
O_Z, O_X, O_B, O_C, O_S = 0, 256, 512, 640, 768
A_FLOOR = 1e-4
LN_EPS = 1e-5
ROUND = 12582912.0
TWO_PI = 6.283185
SINES_AFTER = 1
NEG = -30000.0

XH = 16
XD = P // XH
SENTINEL, TAKEN = -3.0e38, 3.0e38
SPREAD, PREPARED = 6, 12
TWO_ONES = 1 + 0x3F80 / 2**23
MASKED = -1.0e15
EXPERTS = 16
EI = 64
CHUNKS = EXPERTS * EI // P
NC = CHUNKS + 1
SCALE = 2.5


class Sem:

    def __init__(self, ctx, nc, name, n=1, by=1):
        self.sem = ctx.enter_context(nc.semaphore(name))
        self.n, self.by = n, by

    def prime(self, eng):
        eng.sem_inc(self.sem, 2 * self.n * self.by)

    def at(self, g, k=0):
        return (g * self.n + (2 * self.n + k + 1)) * self.by


class DmaSem:

    def __init__(self, ctx, nc, name, dmas=1):
        self.sem = [ctx.enter_context(nc.semaphore(f"{name}{k}")) for k in range(2)]
        self.step = 16 * dmas

    def prime(self, eng):
        for s in self.sem:
            eng.sem_inc(s, self.step)

    def at(self, g, par):
        return g * (self.step // 2) + self.step * (4 - par) // 2


def pairs(eng, group):
    with eng.Fori(0, NG // 2 - 1) as i:
        group(2 * i, 0, 2)
        group(2 * i + 1, 1, 2)
    group(NG - 2, 0, 1)
    group(NG - 1, 1, 0)


def bc(ap, shape):
    return ap.to_broadcast(shape)


def residual_dve(dve, g, bank, other, normed, done, passed, res, stats, mv, times=1.0):
    dve.wait_ge(normed.sem, normed.at(g - 1, 3))
    dve.scalar_tensor_tensor(res[:, :, :], other, times, bank[:, :].rearrange("p (b d) -> p b d", b=GS), ALU.mult, ALU.add)\
        .then_inc(done.sem, 1)
    dve.wait_ge(done.sem, done.at(g, 0))
    for b in range(GS):
        dve.bn_stats(stats[:, b, :], res[:, b, :]).then_inc(done.sem, 1)
    dve.wait_ge(done.sem, done.at(g, GS))
    dve.sem_inc(passed, 1)
    for b in range(GS):
        dve.bn_aggr(mv[:, b, :], stats[:, b, :]).then_inc(done.sem, 1)


def normalise_pool(pool, g, res_ready, done, res, mv, rstd, norm_c, out, out_free=None):
    pool.wait_ge(res_ready.sem, res_ready.at(g, 2 * GS))
    pool.tensor_tensor(rstd[:, :], mv[:, :, 1], norm_c[:, 0, :], ALU.add).then_inc(done.sem, 1)
    pool.tensor_tensor(res[:, :, :], res[:, :, :], bc(mv[:, :, 0:1], [P, GS, P]), ALU.subtract).then_inc(done.sem, 1)
    pool.wait_ge(done.sem, done.at(g, 1))
    pool.tensor_tensor(rstd[:, :], rstd[:, :], norm_c[:, 1, :], ALU.pow).then_inc(done.sem, 1)
    if out_free:
        pool.wait_ge(*out_free)
    pool.wait_ge(done.sem, done.at(g, 2))
    pool.tensor_tensor(out, res[:, :, :], bc(rstd[:, :, None], [P, GS, P]), ALU.mult).then_inc(done.sem, 1)


PAIRS = ((0, 3, 0), (3, 2, 1), (5, 1, 2))
NP = 6


class Projections:
    pass


def projection_tensors(ctx, nc, t):
    def sb(name, shape, dt=F32):
        return ctx.enter_context(nc.sbuf_tensor(name, shape, dt))

    def sem(name, n=1):
        return Sem(ctx, nc, name, n)

    a = Projections()
    a.wqk_hl = sb("wqk_hl", [P, 2, 2, P], F32R)
    a.bqk = sb("bqk", [P, 2])
    a.cin = sb("cin", [P, 2, GT])
    a.c_hl, a.xT_hl = sb("c_hl", [P, 2, GT], F32R), sb("xT_hl", [P, 2, GT], F32R)
    a.part = sb("q_part", [P, 3, GT], BF16), sb("k_part", [P, 3, GT], BF16)
    a.rest = sb("rest", [P, 2, GT])
    a.dram = [nc.dram_tensor(n, (2, NP, P, GT), BF16, kind="Internal").ap() for n in ("q_scratch", "k_scratch")]
    a.d_c, a.a_c, a.v_c = DmaSem(ctx, nc, "ctx_in"), sem("ctx_hi"), sem("ctx_lo")
    a.p_x, a.a_x, a.v_x = sem("x1T_mm"), sem("x1T_hi"), sem("x1T_lo")
    a.mm = sem("q_mm"), sem("k_mm")
    a.act, a.dve = (sem("q_act", 2), sem("k_act", 2)), (sem("q_dve", 2), sem("k_dve", 2))
    a.stored = DmaSem(ctx, nc, "q_stored", 3), DmaSem(ctx, nc, "k_stored", 3)
    a.stacked = [[DmaSem(ctx, nc, f"{x}_stacked{h}_", 2) for h in range(2)] for x in ("q", "k")]
    return a


def inputs_hi(act, a, g, par, bank):
    act.wait_ge(a.d_c.sem[par], a.d_c.at(g, par))
    act.wait_ge(a.mm[1].sem, a.mm[1].at(g - 1))
    act.activation(a.c_hl[:, 0, :], a.cin[:, par, :], ACT.Copy).then_inc(a.a_c.sem, 1)
    act.wait_ge(a.p_x.sem, a.p_x.at(g))
    act.wait_ge(a.mm[0].sem, a.mm[0].at(g - 1))
    act.activation(a.xT_hl[:, 0, :], bank[:, :], ACT.Copy).then_inc(a.a_x.sem, 1)


def inputs_lo(dve, a, g, par, bank):
    dve.wait_ge(a.a_c.sem, a.a_c.at(g))
    dve.tensor_tensor(a.c_hl[:, 1, :], a.cin[:, par, :], a.c_hl[:, 0, :].bitcast(F32), ALU.subtract).then_inc(a.v_c.sem, 1)
    dve.wait_ge(a.a_x.sem, a.a_x.at(g))
    dve.tensor_tensor(a.xT_hl[:, 1, :], bank[:, :], a.xT_hl[:, 0, :].bitcast(F32), ALU.subtract).then_inc(a.v_x.sem, 1)


def parts_act(act, a, g, par, which, bank):
    act.wait_ge(a.mm[which].sem, a.mm[which].at(g))
    act.wait_ge(a.stored[which].sem[1 - par], a.stored[which].at(g - 1, 1 - par))
    act.activation(a.part[which][:, 0, :], bank[:, :], ACT.Identity, bias=a.bqk[:, which:which + 1]).then_inc(a.act[which].sem, 1)
    act.wait_ge(a.dve[which].sem, a.dve[which].at(g, 0))
    act.activation(a.part[which][:, 1, :], a.rest[:, which, :], ACT.Copy).then_inc(a.act[which].sem, 1)


def parts_dve(dve, a, g, which, bank):
    dve.wait_ge(a.act[which].sem, a.act[which].at(g, 0))
    dve.scalar_tensor_tensor(a.rest[:, which, :], bank[:, :], a.bqk[:, which:which + 1], a.part[which][:, 0, :],
                             ALU.add, ALU.subtract).then_inc(a.dve[which].sem, 1)
    dve.wait_ge(a.act[which].sem, a.act[which].at(g, 1))
    dve.tensor_tensor(a.part[which][:, 2, :], a.rest[:, which, :], a.part[which][:, 1, :], ALU.subtract)\
        .then_inc(a.dve[which].sem, 1)


def transpose_x1(pe, a, t, src, bank):
    for b in range(GS):
        mm = pe.transpose(bank[:, b * P:(b + 1) * P], src[:, b, :], t["ident32"][:, :])
    mm.then_inc(a.p_x.sem, 1)


def project(pe, a, g, which, bank):
    src, ready = ((a.xT_hl, a.v_x), (a.c_hl, a.v_c))[which]
    pe.wait_ge(ready.sem, ready.at(g))
    for n, (w, v) in enumerate(((0, 0), (0, 1), (1, 0))):
        mm = pe.matmul(bank[:, :], a.wqk_hl[:, which, w, :], src[:, v, :], start=(n == 0), stop=(n == 2))
    mm.then_inc(a.mm[which].sem, 1)


def store_parts(sp, a, g, par, which):
    sp.wait_ge(a.dve[which].sem, a.dve[which].at(g, 1))
    for done in a.stacked[which]:
        sp.wait_ge(done.sem[par], done.at(g - 2, par))
    for r, n, p in PAIRS:
        src = a.part[which][:, 0:n, :] if which else bc(a.part[which][:, p, None, :], [P, n, GT])
        sp.dma_start(a.dram[which][par, r:r + n].rearrange("r p t -> p r t"), src).then_inc(a.stored[which].sem[par], 16)


def mixer(nc, t, d, psum, a, stop_at):
    with ExitStack() as ctx:
        def sb(name, shape, dt=F32):
            return ctx.enter_context(nc.sbuf_tensor(name, shape, dt))

        def sem(name, n=1, by=1):
            return Sem(ctx, nc, name, n, by)

        ident, ident32, norm_c = t["ident"], t["ident32"], t["norm_c"]
        xT = t["x2"]
        w_in = sb("w_in", [P, O_S + SMALL])
        w_feat = sb("w_feat", [P, 2, 4, P], F32R)
        w_z = sb("w_z", [P, 2, D_INNER], F32R)
        w_x = sb("w_x", [P, 2, D_INNER], F32R)
        w_dx = sb("w_dx", [P, 2, D_INNER], F32R)
        w_dx32 = sb("w_dx32", [P, D_INNER])
        w_out = sb("w_out", [P, 2, P])
        dt_bias = sb("dt_bias", [P, 2 * HEADS])
        d_skip = sb("d_skip", [P, HEADS])
        upto = sb("upto", [P, P])
        after = sb("after", [P, P], F32R)
        acausal = sb("acausal", [P, P], BF16)
        phase = sb("phase", [P, 1])
        scratch = sb("scratch", [P, P])
        soft = sb("soft", [P, NSEQ, 2 * HEADS])
        gate = sb("gate", [P, NSEQ, HEADS])
        ngate = sb("ngate", [P, NSEQ, HEADS])
        gamma = sb("gamma", [P, NSEQ, HEADS])
        beta = sb("beta", [P, NSEQ, HEADS])
        decay = sb("decay", [P, NSEQ, HEADS])
        alpha = sb("alpha", [P, NSEQ, HEADS])
        dec_hl = sb("dec_hl", [P, 2, NSEQ, HEADS])
        dec_r = sb("dec_r", [P, NSEQ, HEADS], F32R)
        half_dt = sb("half_dt", [P, NSEQ, HEADS])
        th = sb("th", [P, NSEQ, ROT])

        w_loaded, const = sem("w_loaded", 1, 16), sem("const")
        wprep = sem("wprep")

        with ExitStack() as c1:
            small = c1.enter_context(nc.sbuf_tensor("small", [P, NSEQ, SMALL], F32))
            e8 = c1.enter_context(nc.sbuf_tensor("e8", [P, NSEQ, 2 * HEADS], F32))
            s8 = c1.enter_context(nc.sbuf_tensor("s8", [P, NSEQ, 2 * HEADS], F32))
            q8 = c1.enter_context(nc.sbuf_tensor("q8", [P, NSEQ, 2 * HEADS], F32))
            p8 = c1.enter_context(nc.sbuf_tensor("p8", [P, NSEQ, 2 * HEADS], F32))
            wqk = c1.enter_context(nc.sbuf_tensor("wqk", [P, 2, P], F32))
            s_att = c1.enter_context(nc.semaphore("att_weights"))
            HALVES = (slice(0, NSEQ // 2), slice(NSEQ // 2, NSEQ))
            BIASED = (18, 34)
            s_xt = [c1.enter_context(nc.semaphore(f"xt_loaded{g}")) for g in range(NG)]
            s_mm = c1.enter_context(nc.semaphore("small_mm"))
            s_ev = c1.enter_context(nc.semaphore("small_copied"))
            s_act = c1.enter_context(nc.semaphore("small_act"))
            s_dve = c1.enter_context(nc.semaphore("small_dve"))
            s_pool = c1.enter_context(nc.semaphore("mixer_consts"))
            s_w = c1.enter_context(nc.semaphore("mixer_weights"))
            s_win = c1.enter_context(nc.semaphore("w_in_loaded"))
            block = c1.enter_context(nc.Block())

            @block.sync
            def _(sp):
                sp.dma_start(w_in[:, :], d["w_inT"]).then_inc(s_win, 16)
                for g in range(NG):
                    sp.dma_start(xT[:, g * GS:(g + 1) * GS, :], d["xT"][:, g * GT:(g + 1) * GT]
                                 .rearrange("p (b t) -> p b t", t=P)).then_inc(s_xt[g], 16)
                for dst, src in ((wqk[:, 0, :], d["Wq"]), (wqk[:, 1, :], d["Wk"]), (t["w_v"][:, :], d["Wv"]), (t["w_o"][:, :], d["Wo"]),
                                 (a.bqk[:, 0:1], d["bq"].rearrange("(p o) -> p o", o=1)),
                                 (a.bqk[:, 1:2], d["bk"].rearrange("(p o) -> p o", o=1)),
                                 (t["b_v"][:, :], d["bv"].partition_broadcast(P)), (t["b_o"][:, :], d["bo"].partition_broadcast(P))):
                    sp.dma_start(dst, src).then_inc(s_att, 16)
                sp.dma_start(a.cin[:, :, :], d["ctxT"][:, 0:2 * GT].rearrange("p (g t) -> p g t", t=GT)).then_inc(s_att, 16)
                sp.wait_ge(s_att, 9 * 16)

            @block.gpsimd
            def _(pool):
                pool.dma_start(dt_bias[:, 0:HEADS], d["dt_bias"].partition_broadcast(P)).then_inc(s_w, 16)
                pool.dma_start(d_skip[:, :], d["D"].partition_broadcast(P)).then_inc(s_w, 16)
                pool.dma_start(w_out[:, :, :], d["w_outT"].rearrange("(c k) n -> k c n", k=P)).then_inc(s_w, 16)
                pool.memset(scratch[:, :], 1.0).then_inc(s_pool, 1)
                pool.wait_ge(s_pool, 1)
                pool.affine_select(out=upto[:, :], in_=scratch[:, :], compare_op=ALU.is_ge, fill=0.0, base=0,
                                   pattern=[[1, P]], channel_multiplier=-1).then_inc(s_pool, 1)
                pool.affine_select(out=after[:, :], in_=scratch[:, :], compare_op=ALU.is_gt, fill=0.0, base=0,
                                   pattern=[[-1, P]], channel_multiplier=1).then_inc(s_pool, 1)
                pool.affine_select(out=ident[:, :], in_=scratch[:, :], compare_op=ALU.is_equal, fill=0.0, base=0,
                                   pattern=[[1, P]], channel_multiplier=-1).then_inc(s_pool, 1)
                pool.affine_select(out=ident32[:, :], in_=scratch[:, :], compare_op=ALU.is_equal, fill=0.0, base=0,
                                   pattern=[[1, P]], channel_multiplier=-1).then_inc(s_pool, 1)
                for k, value in enumerate((LN_EPS, -0.5)):
                    pool.memset(norm_c[:, k, :], value).then_inc(s_pool, 1)
                pool.wait_ge(s_pool, 5)
                pool.memset(scratch[:, :], 0.0).then_inc(s_pool, 1)
                pool.wait_ge(s_pool, 8)
                pool.affine_select(out=acausal[:, :], in_=scratch[:, :], compare_op=ALU.is_ge, fill=NEG, base=0,
                                   pattern=[[1, P]], channel_multiplier=-1).then_inc(s_pool, 1)

            @block.tensor
            def _(pe):
                pe.wait_ge(s_win, 16)
                for g in range(NG):
                    pe.wait_ge(s_xt[g], 16)
                    if g >= 2:
                        pe.wait_ge(s_ev, g - 1)
                    for b in range(GS):
                        mm = pe.matmul(psum[g % 2][:, b * SMALL:(b + 1) * SMALL], xT[:, g * GS + b, :],
                                       w_in[:, O_S:], start=True, stop=True)
                    mm.then_inc(s_mm, 1)

            @block.scalar
            def _(act):
                for half, seqs in enumerate(HALVES):
                    for g in range(half * NG // 2, (half + 1) * NG // 2):
                        act.wait_ge(s_mm, g + 1)
                        act.activation(small[:, g * GS:(g + 1) * GS, :], psum[g % 2][:, 0:GS * SMALL], ACT.Copy).then_inc(s_ev, 1)
                    act.wait_ge(s_ev, (half + 1) * NG // 2)
                    act.activation(th[:, seqs, :], small[:, seqs, 12:SMALL], ACT.Tanh).then_inc(s_act, 1)
                    act.activation(ngate[:, seqs, :], small[:, seqs, 8:12], ACT.Exp, scale=-1.0).then_inc(s_act, 1)
                    act.wait_ge(s_dve, BIASED[half])
                    act.activation(e8[:, seqs, :], soft[:, seqs, :], ACT.Abs).then_inc(s_act, 1)
                    act.wait_ge(s_act, 4 * half + 3)
                    act.activation(e8[:, seqs, :], e8[:, seqs, :], ACT.Exp, scale=-1.0).then_inc(s_act, 1)

            @block.vector
            def _(dve):
                steps = [0]

                def link(ins):
                    steps[0] += 1
                    ins.then_inc(s_dve, 1)
                    dve.wait_ge(s_dve, steps[0])

                for h in range(2):
                    dve.memset(phase[64 * h:64 * h + 32, :], 0.25)
                    dve.memset(phase[64 * h + 32:64 * h + 64, :], 0.0)
                link(dve.memset(dt_bias[:, HEADS:], 0.0))
                dve.wait_ge(s_win, 16)
                dve.wait_ge(s_w, 48)
                link(dve.tensor_tensor(w_dx32[:, :].rearrange("p (h e) -> p h e", h=HEADS),
                                       w_in[:, O_X:O_X + D_INNER].rearrange("p (h e) -> p h e", h=HEADS),
                                       bc(d_skip[:, :, None], [P, HEADS, HD]), ALU.mult))
                parts = [(w_feat[:, :, c, :].rearrange("p v (h r) -> p v h r", h=4), bc(w_in[:, None, o:o + ROT], [P, 4, ROT]))
                         for c, o in ((0, O_B), (1, O_C))]
                parts += [(w_feat[:, :, c, 0:PLAIN], w_in[:, o + ROT:o + P]) for c, o in ((2, O_B), (3, O_C))]
                parts += [(w_z[:, :, :], w_in[:, O_Z:O_Z + D_INNER]), (w_x[:, :, :], w_in[:, O_X:O_X + D_INNER]),
                          (w_dx[:, :, :], w_dx32[:, :])]
                for w, src in parts:
                    dve.tensor_copy(w[:, 0], src).then_inc(s_dve, 1)
                steps[0] += len(parts)
                dve.wait_ge(s_dve, steps[0])
                for w, src in parts:
                    dve.tensor_tensor(w[:, 1], src, w[:, 0].bitcast(F32), ALU.subtract).then_inc(s_dve, 1)
                steps[0] += len(parts)
                dve.wait_ge(s_att, 9 * 16)
                link(dve.tensor_copy(a.wqk_hl[:, :, 0, :], wqk[:, :, :]))
                dve.tensor_tensor(a.wqk_hl[:, :, 1, :], wqk[:, :, :], a.wqk_hl[:, :, 0, :].bitcast(F32), ALU.subtract)
                for half, seqs in enumerate(HALVES):
                    u, e, s, q, p = (x[:, seqs, :] for x in (soft, e8, s8, q8, p8))
                    dve.wait_ge(s_ev, (half + 1) * NG // 2)
                    link(dve.tensor_tensor(u, small[:, seqs, 0:8], bc(dt_bias[:, None, :], [P, NSEQ // 2, 8]), ALU.add))
                    assert steps[0] == BIASED[half], steps
                    dve.wait_ge(s_act, 4 * half + 4)
                    link(dve.tensor_scalar(s, e, 2.0, None, ALU.add))
                    link(dve.reciprocal(q, s))
                    link(dve.tensor_tensor(s, e, q, ALU.mult))
                    link(dve.tensor_tensor(p, s, s, ALU.mult))
                    link(dve.tensor_scalar(q, p, 1.0 / 17, None, ALU.mult))
                    for k in range(7, 0, -1):
                        link(dve.scalar_tensor_tensor(q, q, 1.0 / (2 * k + 1), p, ALU.add, ALU.mult))
                    link(dve.scalar_tensor_tensor(q, q, 1.0, s, ALU.add, ALU.mult))
                    link(dve.tensor_scalar(p, u, 0.0, None, ALU.max))
                    link(dve.scalar_tensor_tensor(u, q, 2.0, p, ALU.mult, ALU.add))
                dve.tensor_scalar(half_dt[:, :, :], soft[:, :, 0:4], 0.5, None, ALU.mult)
                dve.tensor_scalar(decay[:, :, :], soft[:, :, 4:8], -1.0, -A_FLOOR, ALU.mult, ALU.min)

        if stop_at == "small":
            return

        xhl = sb("xhl", [P, 2, 2, GS, P + 1], F32R)
        xres = sb("xres", [P, 2, GS, P])
        turns = sb("turns", [P, GS, HEADS, 2, ROT])
        ang, whole, frac = sb("ang", [P, 2, GT]), sb("whole", [P, 2, GT]), sb("frac", [P, 2, GT])
        trig = sb("trig", [P, 2, GT])
        b_rot = sb("b_rot", [P, 2, 2, GT])
        c_rot = sb("c_rot", [P, 2, 2, GT])
        plain = sb("plain", [PLAIN, 2, 2, 2, GT], F32R)
        tz = sb("tz", [P, 2, 2, GT])
        ramp = sb("ramp", [P, 2, 2, HEADS, P], F32R)
        expo = sb("expo", [P, 2, HEADS, P])
        mix = sb("mix", [P, 2, HEADS, P])
        xg = sb("xg", [P, 2, D_INNER])
        w_tok = sb("w_tok", [P, 2, D_INNER])
        y = sb("y", [P, 2, GT])
        res, stats, mv, rstd = t["res"], t["stats"], t["mv"], t["rstd"]
        x1 = t["x1"]

        s_x = DmaSem(ctx, nc, "x_in")
        s_hi, s_lo = sem("x_hi"), sem("x_lo")
        s_gate, s_coef, s_alpha = (ctx.enter_context(nc.semaphore(n)) for n in ("gate_ready", "coefficients_pool", "alpha_ready"))
        s_turns, s_theta, s_ang = sem("turns_ready", 2), sem("theta_mm", 2), sem("ang_ready", 2)
        s_whole, s_frac, s_trig = sem("whole_ready", 2), sem("frac_ready", 2), sem("trig_ready", 2)
        s_feat = sem("feat_mm", 6)
        s_hiz = sem("feat_act", 4)
        s_prod = sem("feat_dve", 8)
        s_ramp = sem("ramp_ready", 8)
        s_dec = sem("decay_mm", GS)
        s_xx = sem("x_mm", GS)
        s_g = sem("g_mm", 2 * GS)
        s_exp = sem("expo_ready", GS)
        s_w = sem("w_ready", 3 * GS)
        s_mix = sem("mix_ready", GS)
        s_y = sem("y_mm", GS)
        s_yg = sem("y_gated", 2)
        s_o = sem("out_mm")
        s_res, s_x1 = t["x1_res"], t["x1_out"]
        s_zero = ctx.enter_context(nc.semaphore("x_zero_columns"))
        act_passed = ctx.enter_context(nc.semaphore("mixer_act_passed"))
        dve_passed = ctx.enter_context(nc.semaphore("mixer_dve_passed"))
        P0, P1, PX, PD, PG, PY0, PY1, PO = psum
        block = ctx.enter_context(nc.Block())

        @block.sync
        def _(sp):
            for s in (s_x, a.d_c, *a.stored, *a.stacked[0], *a.stacked[1]):
                s.prime(sp)
            a.d_c.prime(sp)

            def group(g, par, left):
                sp.wait_ge(s_res.sem, s_res.at(g - 2, 0))
                sp.dma_start(xres[:, par, :, :], d["x"].rearrange("(b t) d -> t b d", t=P)[:, bass.ds(g * GS, GS), :])\
                    .then_inc(s_x.sem[par], 16)
                if not left:
                    store_parts(sp, a, 0, 0, 1)
                    store_parts(sp, a, 0, 0, 0)

            pairs(sp, group)

        @block.scalar
        def _(act):
            for s in (s_hi, s_hiz, s_exp, s_ang, s_trig, a.a_c, a.a_x, *a.act):
                s.prime(act)

            def angles(g):
                for k in range(2):
                    act.wait_ge(s_theta.sem, s_theta.at(g, k))
                    act.wait_ge(s_frac.sem, s_frac.at(g - 1, k))
                    act.activation(ang[:, k, :], (P0, P1)[k][:, :], ACT.Identity, bias=phase[:, 0:1]).then_inc(s_ang.sem, 1)

            def sines(g):
                for k in range(2):
                    act.wait_ge(s_frac.sem, s_frac.at(g, k))
                    act.wait_ge(s_prod.sem, s_prod.at(g - 1, 3))
                    act.activation(trig[:, k, :], frac[:, k, :], ACT.Sin, scale=TWO_PI).then_inc(s_trig.sem, 1)

            def split(g, par):
                act.wait_ge(s_y.sem, s_y.at(g - 2, 3))
                act.sem_inc(act_passed, 1)
                act.activation(xhl[:, par, 0, :, 1:], xT[:, bass.ds(g * GS, GS), :], ACT.Copy).then_inc(s_hi.sem, 1)

            def plain_hi(g, par):
                for k in range(2):
                    act.wait_ge(s_feat.sem, s_feat.at(g, 2 + k))
                    act.wait_ge(s_g.sem, s_g.at(g - 2, 7))
                    act.activation(plain[:, par, k, 0, :], (P0, P1)[k][0:PLAIN, :], ACT.Copy).then_inc(s_hiz.sem, 1)

            def gates(g):
                for k in range(2):
                    act.wait_ge(s_feat.sem, s_feat.at(g, 4 + k))
                    act.wait_ge(s_yg.sem, s_yg.at(g - 1, k))
                    act.activation(tz[:, 0, k, :], (P0, P1)[k][:, :], ACT.Tanh, scale=0.5).then_inc(s_hiz.sem, 1)

            def group(g, par, left):
                if left:
                    split(g + 1, 1 - par)
                for b in range(GS):
                    act.wait_ge(s_dec.sem, s_dec.at(g, b))
                    act.wait_ge(s_mix.sem, s_mix.at(g, b - 2))
                    act.activation(expo[:, b % 2, :, :], PD[:, :], ACT.Exp).then_inc(s_exp.sem, 1)
                    if left and b == 0:
                        angles(g + 1)
                    if not left and b == 0:
                        inputs_hi(act, a, 0, 0, P0)
                    if not left and b == 2:
                        parts_act(act, a, 0, 0, 1, P1)
                    if left and b == SINES_AFTER:
                        sines(g + 1)
                    if left and b == 2:
                        plain_hi(g + 1, 1 - par)
                if left:
                    gates(g + 1)
                else:
                    parts_act(act, a, 0, 0, 0, P0)

            angles(0)
            split(0, 0)
            sines(0)
            act.wait_ge(s_coef, 1)
            act.activation(alpha[:, :, :], decay[:, :, :], ACT.Exp).then_inc(s_alpha, 1)
            plain_hi(0, 0)
            gates(0)
            pairs(act, group)

        @block.gpsimd
        def _(pool):
            for s in (s_ramp, s_x1, s_turns):
                s.prime(pool)

            def steps_of(g):
                pool.wait_ge(s_theta.sem, s_theta.at(g - 1, 1))
                for cs in range(2):
                    pool.tensor_tensor(turns[:, :, :, cs, :],
                                       bc(th[:, bass.ds(g * GS, GS), None, :], [P, GS, HEADS, ROT]),
                                       bc(half_dt[:, bass.ds(g * GS, GS), :, None], [P, GS, HEADS, ROT]),
                                       ALU.mult).then_inc(s_turns.sem, 1)

            def ramps(g, bs):
                for b in bs:
                    pool.wait_ge(s_dec.sem, s_dec.at(g, b - 2))
                    for v in range(2):
                        pool.tensor_tensor(ramp[:, b % 2, v, :, :], bc(upto[:, None, :], [P, HEADS, P]),
                                           bc(dec_hl[:, v, bass.ds(g * GS + b, 1), :].rearrange("p o h -> p (o h)")[:, :, None],
                                              [P, HEADS, P]), ALU.mult).then_inc(s_ramp.sem, 1)

            def group(g, par, left):
                ramps(g, (2, 3))
                if left:
                    ramps(g + 1, (0, 1))
                if left == 2:
                    steps_of(g + 2)
                if left:
                    normalise_pool(pool, g, s_res, s_x1, res, mv, rstd, norm_c, x1[:, bass.ds(g * GS, GS), :])

            steps_of(0)
            dt = soft[:, :, 0:4]
            pool.tensor_tensor(decay[:, :, :], decay[:, :, :], dt, ALU.mult).then_inc(s_coef, 1)
            pool.wait_ge(s_coef, 1)
            pool.tensor_copy(dec_r[:, :, :], decay[:, :, :]).then_inc(s_coef, 1)
            pool.wait_ge(s_gate, 2)
            pool.tensor_tensor(gamma[:, :, :], gate[:, :, :], dt, ALU.mult).then_inc(s_coef, 1)
            pool.wait_ge(s_coef, 3)
            pool.tensor_copy(dec_hl[:, 0, :, :], dec_r[:, :, :].bitcast(F32)).then_inc(s_coef, 1)
            pool.tensor_tensor(ngate[:, :, :], dt, gamma[:, :, :], ALU.subtract).then_inc(s_coef, 1)
            pool.wait_ge(s_coef, 5)
            pool.tensor_tensor(dec_hl[:, 1, :, :], decay[:, :, :], dec_hl[:, 0, :, :], ALU.subtract).then_inc(s_coef, 1)
            pool.wait_ge(s_coef, 6)
            ramps(0, (0, 1))
            pool.wait_ge(s_alpha, 1)
            pool.tensor_tensor(beta[:, :, :], ngate[:, :, :], alpha[:, :, :], ALU.mult).then_inc(s_coef, 1)
            steps_of(1)
            pairs(pool, group)

        @block.vector
        def _(dve):
            dve.memset(xhl[:, :, :, :, 0:1].bitcast(F32), 0.0).then_inc(s_zero, 1)
            for s in (s_lo, s_prod, s_w, s_mix, s_yg, s_res, s_whole, s_frac, a.v_c, a.v_x, *a.dve):
                s.prime(dve)

            def fractions(g):
                for k in range(2):
                    dve.wait_ge(s_ang.sem, s_ang.at(g, k))
                    dve.tensor_scalar(whole[:, k, :], ang[:, k, :], ROUND, -ROUND, ALU.add, ALU.add).then_inc(s_whole.sem, 1)
                for k in range(2):
                    dve.wait_ge(s_whole.sem, s_whole.at(g, k))
                    dve.wait_ge(s_trig.sem, s_trig.at(g - 1, k))
                    dve.tensor_tensor(frac[:, k, :], ang[:, k, :], whole[:, k, :], ALU.subtract).then_inc(s_frac.sem, 1)

            def split(g, par):
                dve.wait_ge(s_hi.sem, s_hi.at(g))
                dve.tensor_tensor(xhl[:, par, 1, :, 1:], xT[:, bass.ds(g * GS, GS), :], xhl[:, par, 0, :, 1:].bitcast(F32),
                                  ALU.subtract)\
                    .then_inc(s_lo.sem, 1)

            def rotate(g, par):
                for c, rot in ((0, b_rot), (1, c_rot)):
                    dve.wait_ge(s_feat.sem, s_feat.at(g, c))
                    dve.wait_ge(s_g.sem, s_g.at(g - 2, 7))
                    for k in range(2):
                        dve.wait_ge(s_trig.sem, s_trig.at(g, k))
                        dve.tensor_tensor(rot[:, par, k, :], (P0, P1)[c][:, :], trig[:, k, :], ALU.mult)\
                            .then_inc(s_prod.sem, 1)

            def plain_lo(g, par):
                for k in range(2):
                    dve.wait_ge(s_hiz.sem, s_hiz.at(g, k))
                    dve.tensor_tensor(plain[:, par, k, 1, :], (P0, P1)[k][0:PLAIN, :], plain[:, par, k, 0, :].bitcast(F32),
                                      ALU.subtract).then_inc(s_prod.sem, 1)

            def gates(g):
                for k in range(2):
                    dve.wait_ge(s_hiz.sem, s_hiz.at(g, 2 + k))
                    dve.wait_ge(s_yg.sem, s_yg.at(g - 1, k))
                    dve.scalar_tensor_tensor(tz[:, 1, k, :], tz[:, 0, k, :], 1.0, (P0, P1)[k][:, :], ALU.add, ALU.mult)\
                        .then_inc(s_prod.sem, 1)

            def inputs_of(g, b):
                dve.wait_ge(s_xx.sem, s_xx.at(g, b))
                heads = lambda ap: ap.rearrange("p (h e) -> p h e", h=HEADS)
                of = lambda co: bc(co[:, bass.ds(g * GS + b, 1), :].rearrange("p o h -> p (o h)")[:, :, None], [P, HEADS, HD])
                dve.wait_ge(s_w.sem, s_w.at(g, 3 * b - 1))
                dve.tensor_tensor(heads(xg[:, 0, :]), heads(PX[:, 0:D_INNER]), of(gamma), ALU.mult).then_inc(s_w.sem, 1)
                dve.tensor_tensor(heads(xg[:, 1, :]), heads(PX[:, D_INNER:]), of(beta), ALU.mult).then_inc(s_w.sem, 1)
                dve.wait_ge(s_w.sem, s_w.at(g, 3 * b + 1))
                dve.wait_ge(s_y.sem, s_y.at(g, b - 2))
                dve.tensor_tensor(w_tok[:, b % 2, :], xg[:, 0, :], xg[:, 1, :], ALU.add).then_inc(s_w.sem, 1)

            def group(g, par, left):
                if left:
                    split(g + 1, 1 - par)
                for b in range(GS):
                    inputs_of(g, b)
                    dve.wait_ge(s_g.sem, s_g.at(g, 2 * b + 1))
                    dve.wait_ge(s_exp.sem, s_exp.at(g, b))
                    dve.wait_ge(s_y.sem, s_y.at(g, b - 2))
                    dve.tensor_tensor(mix[:, b % 2, :, :], PG[:, :].rearrange("p (h t) -> p h t", h=HEADS),
                                      expo[:, b % 2, :, :], ALU.mult).then_inc(s_mix.sem, 1)
                    if left and b == 0:
                        fractions(g + 1)
                    if not left and b == 0:
                        inputs_lo(dve, a, 0, 0, P0)
                    if not left and b == 2:
                        parts_dve(dve, a, 0, 1, P1)
                    if left and b == 1:
                        rotate(g + 1, 1 - par)
                    if left and b == 2:
                        plain_lo(g + 1, 1 - par)
                dve.wait_ge(s_y.sem, s_y.at(g, 3))
                dve.wait_ge(s_o.sem, s_o.at(g - 1))
                dve.wait_ge(s_prod.sem, s_prod.at(g, 7))
                for k in range(2):
                    dve.scalar_tensor_tensor(y[:, k, :], tz[:, 1, k, :], 0.5, (PY0, PY1)[k][:, :], ALU.mult, ALU.mult)\
                        .then_inc(s_yg.sem, 1)
                if left:
                    gates(g + 1)
                else:
                    parts_dve(dve, a, 0, 0, P0)
                dve.wait_ge(s_o.sem, s_o.at(g))
                dve.wait_ge(s_x.sem[par], s_x.at(g, par))
                residual_dve(dve, g, PO, xres[:, par, :, :], s_x1, s_res, dve_passed, res, stats, mv)

            dve.tensor_scalar(gate[:, :, :], ngate[:, :, :], 1.0, None, ALU.add).then_inc(s_gate, 1)
            dve.wait_ge(s_gate, 1)
            dve.reciprocal(gate[:, :, :], gate[:, :, :]).then_inc(s_gate, 1)
            fractions(0)
            split(0, 0)
            rotate(0, 0)
            plain_lo(0, 0)
            gates(0)
            dve.wait_ge(s_coef, 7)
            pairs(dve, group)

        @block.tensor
        def _(pe):
            for s in (a.p_x, *a.mm, s_theta, s_feat, s_dec, s_xx, s_g, s_y, s_o):
                s.prime(pe)

            def theta(g):
                pe.wait_ge(s_turns.sem, s_turns.at(g, 1))
                for k in range(2):
                    pe.wait_ge(s_prod.sem, s_prod.at(g - 1, 6 + k))
                    for b in range(GS):
                        mm = pe.matmul((P0, P1)[k][:, b * P:(b + 1) * P],
                                       turns[:, b, 2 * k:2 * k + 2, :, :].rearrange("p h c r -> p (h c r)"),
                                       upto[:, :], start=True, stop=True)
                    mm.then_inc(s_theta.sem, 1)

            def features(g, par, cs):
                pe.wait_ge(s_lo.sem, s_lo.at(g))
                freed = [(s_ang, 0), (s_ang, 1), (s_prod, 1), (s_prod, 3), (s_prod, 4), (s_prod, 5)]
                for c in cs:
                    bank = (P0, P1)[c % 2]
                    pe.wait_ge(freed[c][0].sem, freed[c][0].at(g, freed[c][1]))
                    m = (P, P, PLAIN, PLAIN, P, P)[c]
                    w = w_feat[:, :, c, 0:m] if c < 4 else w_z[:, :, (c - 4) * P:(c - 3) * P]
                    for n, (a, v) in enumerate(((0, 0), (0, 1), (1, 0))):
                        mm = pe.matmul(bank[0:m, :], w[:, a, :], xhl[:, par, v, :, 1:], start=(n == 0), stop=(n == 2))
                    mm.then_inc(s_feat.sem, 1)

            def front(g, par, b):
                pe.wait_ge(s_ramp.sem, s_ramp.at(g, 2 * b + 1))
                pe.wait_ge(s_exp.sem, s_exp.at(g, b - 1))
                for v in range(2):
                    pe.matmul(PD[:, :], after[:, :], ramp[:, b % 2, v, :, :], start=(v == 0), stop=False)
                pe.matmul(PD[:, :], ident[:, :], bc(acausal[:, None, :], [P, HEADS, P]), start=False, stop=True)\
                    .then_inc(s_dec.sem, 1)
                pe.wait_ge(s_w.sem, s_w.at(g, 3 * b - 2))
                tokens(par, b, 0)

            def tokens(par, b, shift):
                for n, (a, v) in enumerate(((0, 0), (0, 1), (1, 0))):
                    mm = pe.matmul(PX[:, shift * D_INNER:(shift + 1) * D_INNER], xhl[:, par, a, b, 1 - shift:P + 1 - shift],
                                   w_x[:, v, :], start=(n == 0), stop=(n == 2))
                return mm

            def scores(g, par, b):
                pe.wait_ge(s_mix.sem, s_mix.at(g, b - 1))
                tok = slice(b * P, (b + 1) * P)
                for n, (a, v) in enumerate(((0, 0), (0, 1), (1, 0))):
                    pe.matmul(PG[:, :], plain[:, par, 0, a, tok], bc(plain[:, par, 1, v, None, tok], [PLAIN, HEADS, P]),
                              start=(n == 0), stop=False, skip_group_check=True)
                for half in range(2):
                    rows = slice(64 * half, 64 * half + 64)
                    for k in range(2):
                        h = 2 * k + half
                        mm = pe.matmul(PG[:, h * P:(h + 1) * P], b_rot[rows, par, k, tok], c_rot[rows, par, k, tok],
                                       start=False, stop=True, skip_group_check=True)
                    mm.then_inc(s_g.sem, 1)
                    if half == 0:
                        tokens(par, b, 1).then_inc(s_xx.sem, 1)
                        pe.wait_ge(s_g.sem, s_g.at(g, 2 * b))

            def skip(g, par):
                for k in range(2):
                    pe.wait_ge(s_yg.sem, s_yg.at(g - 1, k))
                    for n, (a, v) in enumerate(((0, 0), (0, 1), (1, 0))):
                        pe.matmul((PY0, PY1)[k][:, :], w_dx[:, a, k * P:(k + 1) * P], xhl[:, par, v, :, 1:],
                                  start=(n == 0), stop=False, skip_group_check=True)

            def back(g, b):
                pe.wait_ge(s_mix.sem, s_mix.at(g, b))
                pe.wait_ge(s_w.sem, s_w.at(g, 3 * b + 2))
                for h in range(HEADS):
                    mm = pe.matmul((PY0, PY1)[h // 2][64 * (h % 2):64 * (h % 2) + 64, b * P:(b + 1) * P],
                                   w_tok[:, b % 2, h * HD:(h + 1) * HD], mix[:, b % 2, h, :],
                                   start=False, stop=True, skip_group_check=True)
                mm.then_inc(s_y.sem, 1)

            def group(g, par, left):
                pe.wait_ge(s_prod.sem, s_prod.at(g, 5))
                scores(g, par, 0)
                if left:
                    theta(g + 1)
                else:
                    pe.wait_ge(s_x1.sem, s_x1.at(0, 3))
                    pe.wait_ge(s_prod.sem, s_prod.at(g, 7))
                    transpose_x1(pe, a, t, x1[:, 0:GS, :], P0)
                skip(g, par)
                for b in range(1, GS):
                    front(g, par, b)
                    back(g, b - 1)
                    scores(g, par, b)
                    if left and b < 3:
                        features(g + 1, 1 - par, (2 * b - 2, 2 * b - 1))
                    if not left and b < 3:
                        project(pe, a, 0, 2 - b, (P1, P0)[b - 1])
                if left:
                    features(g + 1, 1 - par, (4, 5))
                back(g, GS - 1)
                if left:
                    front(g + 1, 1 - par, 0)
                pe.wait_ge(s_yg.sem, s_yg.at(g, 1))
                pe.wait_ge(s_res.sem, s_res.at(g - 1, 0))
                for b in range(GS):
                    for k in range(2):
                        mm = pe.matmul(PO[:, b * P:(b + 1) * P], y[:, k, b * P:(b + 1) * P], w_out[:, k, :],
                                       start=(k == 0), stop=(k == 1))
                mm.then_inc(s_o.sem, 1)

            theta(0)
            pe.wait_ge(s_zero, 1)
            features(0, 0, range(6))
            front(0, 0, 0)
            pairs(pe, group)


def attention(nc, t, d, psum, a, e):
    NROW = NP * XD
    UNITS = 4
    DIAG = P + XD
    with ExitStack() as ctx:
        def sb(name, shape, dt=F32):
            return ctx.enter_context(nc.sbuf_tensor(name, shape, dt))

        def sem(name, n=1, by=1):
            return Sem(ctx, nc, name, n, by)

        def raw(name):
            return ctx.enter_context(nc.semaphore(name))

        w_v, w_o, b_v, b_o, cin = t["w_v"], t["w_o"], t["b_v"], t["b_o"], a.cin
        neg_i = sb("neg_i", [P, P], BF16)
        zeros = sb("zeros", [P, P])
        ones_d = sb("ones_d", [P, UNITS * DIAG])
        mask8 = sb("mask8", [P, 2, GS, P], U8)
        mask = sb("mask", [P, 2, GS, P], BF16)
        xs = sb("xs", [P, 2, GS, P])
        q_stack, k_stack = sb("q_stack", [P, 2, 8, GT], BF16), sb("k_stack", [P, 2, 8, GT], BF16)
        v_d = sb("v_d", [P, 2, GS, UNITS * DIAG])
        nmax = sb("nmax", [P, GS, XH])
        nrest = sb("nrest", [P, GS, XH])
        npart = sb("npart", [P, GS, 2, 3, 8], BF16)
        nmT = sb("nmT", [48, GT], BF16)
        prob = sb("prob", [P, 2, UNITS, UNITS, P])
        recip = sb("recip", [P, 2, P])
        ctxT = sb("ctxT", [P, GS, P])
        xb = sb("xb", [P, GS, P])
        res, stats, mv, rstd = t["res"], t["stats"], t["mv"], t["rstd"]
        x1, x2, ident, ident32, norm_c = (t[k] for k in ("x1", "x2", "ident", "ident32", "norm_c"))

        d_mask, d_xs = DmaSem(ctx, nc, "mask_in"), DmaSem(ctx, nc, "x1_staged")
        d_c, (d_q, d_k) = a.d_c, a.stacked
        d_m = [DmaSem(ctx, nc, f"max_stacked{h}_", 2) for h in range(2)]
        d_ms = [DmaSem(ctx, nc, f"max_stored{h}_") for h in range(2)]
        m_dram = nc.dram_tensor("max_scratch", (2, 2, 48, 2 * P), BF16, kind="Internal").ap()
        a_mask = sem("mask_ready")
        a_exp, a_mt = sem("prob_ready", 4 * GS), sem("nmT_ready", 2)
        p_x, v_x, (v_q, v_k) = a.p_x, a.v_x, a.dve
        v_v, v_norm, v_max = sem("v_ready", GS), sem("ctx_norm", 2 * GS), sem("max_ready", 4 * GS)
        v_split = sem("max_parts", 8)
        p_v = sem("v_mm")
        p_s, p_t, p_u = sem("score_mm", 4 * GS), sem("scoreT_mm", 4 * GS), sem("pv_mm", GS)
        p_mt, p_o = sem("max_mm", 2), sem("out_b_mm")
        g_x = sem("x1_biased")
        v_res, g_out, x1_out = t["x2_res"], t["x2_out"], t["x1_out"]
        g_init, v_init = raw("att_pool_init"), raw("att_dve_init")
        sp_passed, dve_passed, pe_passed = raw("att_sp_passed"), raw("att_dve_passed"), raw("att_pe_passed")

        TT0, TT1, SS0, SS1, U0, U1, PF, PO = psum
        FIRST = ((TT0, TT1, SS0, SS1), (U0, U1, PO, PF))
        block = ctx.enter_context(nc.Block())

        def unit_rows(u):
            return 64 * (u // 2), 4 * (u % 2)

        @block.sync
        def _(sp):
            for s in (d_mask, d_xs, *d_m, *d_ms):
                s.prime(sp)
            d_xs.prime(sp)

            def loads(g, par, first=False):
                if not first:
                    sp.wait_ge(p_v.sem, p_v.at(g - 2))
                    sp.dma_start(cin[:, par, :], d["ctxT"][:, bass.ds(g * GT, GT)]).then_inc(d_c.sem[par], 16)
                    sp.wait_ge(p_x.sem, p_x.at(g - 2))
                    sp.dma_start(xs[:, par, :, :], x1[:, bass.ds(g * GS, GS), :]).then_inc(d_xs.sem[par], 16)
                sp.wait_ge(a_mask.sem, a_mask.at(g - 2))
                sp.dma_start(mask8[:, par, :, :].bitcast(mybir.dt.int32), d["mask"].rearrange("b q k -> q b k")[:, bass.ds(g * GS, GS), :])\
                    .then_inc(d_mask.sem[par], 16)

            def stack(g, par, half, via, stored, dst, done):
                sp.wait_ge(stored.sem[par], stored.at(g, par))
                sp.sem_inc(sp_passed, 1)
                sp.wait_ge(p_t.sem, p_t.at(g - 2, 8 * half + 7))
                tok = slice(half * 2 * P, half * 2 * P + 2 * P)
                rows = via[par].rearrange("r (e j c) t -> j (r e) c t", e=XD, j=2)
                for j in range(2):
                    sp.dma_start(dst[64 * j:64 * j + NROW, par, :, tok], rows[j][:, :, tok]).then_inc(done[half].sem[par], 16)

            def store_max(g, par, half):
                sp.wait_ge(a_mt.sem, a_mt.at(g, half))
                sp.sem_inc(sp_passed, 1)
                sp.wait_ge(d_m[half].sem[par], d_m[half].at(g - 2, par))
                tok = slice(half * 2 * P, half * 2 * P + 2 * P)
                sp.dma_start(m_dram[par, half], nmT[:, tok]).then_inc(d_ms[half].sem[par], 16)

            def stack_max(g, par, half):
                sp.wait_ge(d_ms[half].sem[par], d_ms[half].at(g, par))
                tok = slice(half * 2 * P, half * 2 * P + 2 * P)
                for j in range(2):
                    row = 64 * j + NROW
                    sp.dma_start(q_stack[row:row + 3, par, :, tok],
                                 m_dram[par, half, 24 * j:24 * j + 24, :].rearrange("(r c) t -> r c t", r=3))\
                        .then_inc(d_m[half].sem[par], 16)

            def store_k(g, par):
                store_parts(sp, a, g, par, 1)

            def store_q(g, par):
                store_parts(sp, a, g, par, 0)

            def stacks(g, par, half):
                stack(g, par, half, a.dram[1], a.stored[1], k_stack, d_k)
                stack(g, par, half, a.dram[0], a.stored[0], q_stack, d_q)

            def group(g, par, left):
                if left == 2:
                    loads(g + 2, par)
                stack_max(g, par, 1)
                if left == 2:
                    store_k(g + 2, par)
                    store_q(g + 2, par)
                if left:
                    store_max(g + 1, 1 - par, 0)
                if left == 2:
                    stacks(g + 2, par, 0)
                if left:
                    stack_max(g + 1, 1 - par, 0)
                if left == 2:
                    stacks(g + 2, par, 1)
                if left:
                    store_max(g + 1, 1 - par, 1)

            for g in range(2):
                loads(g, g, first=True)
            for g in range(2):
                if g:
                    store_k(g, g)
                    store_q(g, g)
                sp.wait_ge(v_init, g + 1)
                stacks(g, g, 0)
                stacks(g, g, 1)
            store_max(0, 0, 0)
            stack_max(0, 0, 0)
            store_max(0, 0, 1)
            sp.wait_ge(x1_out.sem, x1_out.at(NG - 1, 3))
            pairs(sp, group)

        @block.gpsimd
        def _(pool):
            g_x.prime(pool)
            g_out.prime(pool)

            def group(g, par, left):
                pool.wait_ge(v_res.sem, v_res.at(g - 1, 0))
                pool.tensor_tensor(xb[:, :, :], x1[:, bass.ds(g * GS, GS), :], bc(b_o[:, None, :], [P, GS, P]), ALU.add)\
                    .then_inc(g_x.sem, 1)
                if left:
                    normalise_pool(pool, g, v_res, g_out, res, mv, rstd, norm_c, x2[:, bass.ds(g * GS, GS), :])

            pool.memset(zeros[:, :], 0.0).then_inc(g_init, 1)
            pool.wait_ge(g_init, 1)
            pool.affine_select(out=neg_i[:, :], in_=zeros[:, :], compare_op=ALU.not_equal, fill=MASKED, base=0,
                               pattern=[[1, P]], channel_multiplier=-1).then_inc(g_init, 1)
            pool.memset(v_d[:, 0], 0.0).then_inc(g_init, 1)
            pool.memset(v_d[:, 1], 0.0).then_inc(g_init, 1)
            pool.memset(ones_d[:, :], 0.0).then_inc(g_init, 1)
            pool.wait_ge(g_init, 5)
            pool.memset(ones_d[:, :].rearrange("p (i c) -> p i c", i=UNITS)[:, :, 0:P]
                        .rearrange("p i (c e) -> p i c e", e=4 * XD)[:, :, :, 0:XD], 1.0).then_inc(g_init, 1)
            normalise_pool(pool, NG - 1, t["x1_res"], x1_out, res, mv, rstd, norm_c, x1[:, NSEQ - GS:, :])
            pool.wait_ge(x1_out.sem, x1_out.at(NG - 1, 3))
            pool.wait_ge(p_s.sem, p_s.at(0, 0))
            prepare_pool(pool, d, e, prob[0:32, 0, 0:2, :, :].rearrange("p u i (x y) -> p (u i) x y", x=2))
            pairs(pool, group)

        @block.scalar
        def _(act):
            for s in (a_mask, a_exp, a_mt, e.a_x, e.a_l, e.a_c):
                s.prime(act)

            def inputs(g, par, bank=PF):
                inputs_hi(act, a, g, par, bank)

            def masks(g, par):
                act.wait_ge(d_mask.sem[par], d_mask.at(g, par))
                act.wait_ge(p_t.sem, p_t.at(g - 2, 4 * GS - 1))
                act.activation(mask[:, par, :, :], mask8[:, par, :, :], ACT.Copy).then_inc(a_mask.sem, 1)

            def exps(g, b):
                for u in range(UNITS):
                    act.wait_ge(p_t.sem, p_t.at(g, 4 * b + u))
                    act.wait_ge(p_u.sem, p_u.at(g, b - 2))
                    act.activation(prob[:, b % 2, u, :, :], (TT0, TT1)[u % 2][:, :], ACT.Exp, scale=XD ** -0.5)\
                        .then_inc(a_exp.sem, 1)

            def maxT(g, par, half):
                act.wait_ge(p_mt.sem, p_mt.at(g, half))
                act.wait_ge(d_ms[half].sem[1 - par], d_ms[half].at(g - 1, 1 - par))
                tok = slice(half * 2 * P, half * 2 * P + 2 * P)
                act.activation(nmT[:, tok], PF[:, :].bitcast(BF16)[0:48, tok], ACT.Copy).then_inc(a_mt.sem, 1)

            def k_parts(g, par, bank=PF):
                parts_act(act, a, g, par, 1, bank)

            def q_parts(g, par, bank=PF):
                parts_act(act, a, g, par, 0, bank)

            def group(g, par, left):
                exps(g, 0)
                if left == 2:
                    inputs(g + 2, par)
                if not left:
                    act.wait_ge(e.steps, PREPARED)
                    x2T_hi(act, e, 0, 0)
                exps(g, 1)
                if left == 2:
                    k_parts(g + 2, par)
                if not left:
                    logit_tanh(act, e, 0)
                exps(g, 2)
                if left == 2:
                    q_parts(g + 2, par)
                if left:
                    maxT(g + 1, 1 - par, 0)
                exps(g, 3)
                if not left:
                    copy_weights(act, e, 0, 0)
                if left == 2:
                    masks(g + 2, par)
                if left:
                    maxT(g + 1, 1 - par, 1)

            for g in range(2):
                if g:
                    inputs(g, g, FIRST[g][0])
                    k_parts(g, g, FIRST[g][1])
                    q_parts(g, g, FIRST[g][2])
                masks(g, g)
            maxT(0, 0, 0)
            maxT(0, 0, 1)
            act.wait_ge(e.steps, SPREAD)
            pairs(act, group)

        @block.vector
        def _(dve):
            dve.memset(e.open_[:, :, EXPERTS:], SENTINEL)
            for s in (v_v, v_norm, v_max, v_split, v_res, e.v_x, e.v_sc, e.v_grp, e.v_sel):
                s.prime(dve)

            def inputs(g, par, bank=PF):
                inputs_lo(dve, a, g, par, bank)

            def values(g, par, bank=PF):
                dve.wait_ge(p_v.sem, p_v.at(g))
                dve.wait_ge(p_u.sem, p_u.at(g - 2, GS - 1))
                for b in range(GS):
                    dst = v_d[:, par, b, :].rearrange("p (i c) -> p i c", i=UNITS)[:, :, 0:P]\
                        .rearrange("p i (c e) -> p i c e", e=4 * XD)[:, :, :, 0:XD]
                    dve.tensor_tensor(dst, bank[:, b * P:(b + 1) * P].rearrange("p (c i e) -> p i c e", c=4, i=4),
                                      b_v[:, :].rearrange("p (c i e) -> p i c e", c=4, i=4), ALU.add).then_inc(v_v.sem, 1)

            def maxima(g, b):
                for u in range(UNITS):
                    dve.wait_ge(p_s.sem, p_s.at(g, 4 * b + u))
                    dve.wait_ge(v_split.sem, v_split.at(g - 1, 7))
                    dve.tensor_reduce(nmax[:, b, 4 * u:4 * u + 4], (SS0, SS1)[u % 2][:, :].rearrange("p (i k) -> p i k", i=4),
                                      AX_X, ALU.max, negate=True).then_inc(v_max.sem, 1)

            def split_maxima(g, half):
                bs = slice(2 * half, 2 * half + 2)
                part = lambda r: npart[:, bs, :, r, :]
                of = lambda tile: tile[:, bs, :].rearrange("p b (j c) -> p b j c", j=2)
                dve.wait_ge(v_max.sem, v_max.at(g, 8 * half + 7))
                dve.wait_ge(p_mt.sem, p_mt.at(g - 1, half))
                dve.tensor_copy(part(0), of(nmax)).then_inc(v_split.sem, 1)
                dve.wait_ge(v_split.sem, v_split.at(g, 4 * half))
                dve.tensor_tensor(of(nrest), of(nmax), part(0), ALU.subtract).then_inc(v_split.sem, 1)
                dve.wait_ge(v_split.sem, v_split.at(g, 4 * half + 1))
                dve.tensor_copy(part(1), of(nrest)).then_inc(v_split.sem, 1)
                dve.wait_ge(v_split.sem, v_split.at(g, 4 * half + 2))
                dve.tensor_tensor(part(2), of(nrest), part(1), ALU.subtract).then_inc(v_split.sem, 1)

            def norm(g, b):
                bank = (U0, U1)[b % 2]
                dve.wait_ge(p_u.sem, p_u.at(g, b))
                dve.reciprocal(recip[:, b % 2, :], bank[:, P:2 * P]).then_inc(v_norm.sem, 1)
                dve.wait_ge(v_norm.sem, v_norm.at(g, 2 * b))
                dve.wait_ge(p_o.sem, p_o.at(g - 1))
                dve.tensor_tensor(ctxT[:, b, :], bank[:, 0:P], recip[:, b % 2, :], ALU.mult).then_inc(v_norm.sem, 1)

            def k_parts(g, bank=PF):
                parts_dve(dve, a, g, 1, bank)

            def q_parts(g, bank=PF):
                parts_dve(dve, a, g, 0, bank)

            def group(g, par, left):
                if left:
                    maxima(g + 1, 0)
                if left == 2:
                    inputs(g + 2, par)
                if left:
                    maxima(g + 1, 1)
                    split_maxima(g + 1, 0)
                if left == 2:
                    k_parts(g + 2)
                if not left:
                    dve.wait_ge(e.steps, PREPARED)
                    x2T_lo(dve, e, 0, 0)
                norm(g, 0)
                if not left:
                    expert_scores(dve, e, 0)
                    rank_groups(dve, e, 0)
                if left:
                    maxima(g + 1, 2)
                if left == 2:
                    q_parts(g + 2)
                norm(g, 1)
                if not left:
                    select_experts(dve, e, 0)
                if left:
                    maxima(g + 1, 3)
                    split_maxima(g + 1, 1)
                norm(g, 2)
                if not left:
                    share_weights(dve, e, 0)
                norm(g, 3)
                if left == 2:
                    values(g + 2, par)
                dve.wait_ge(p_o.sem, p_o.at(g))
                dve.wait_ge(g_x.sem, g_x.at(g))
                residual_dve(dve, g, PO, xb[:, :, :], g_out, v_res, dve_passed, res, stats, mv)

            for g in range(2):
                dve.memset(k_stack[:, g].bitcast(F32), TWO_ONES).then_inc(v_init, 1)
                if g:
                    inputs(g, g, FIRST[g][0])
                    k_parts(g, FIRST[g][1])
                    q_parts(g, FIRST[g][2])
                dve.wait_ge(g_init, 3 + g)
                values(g, g, FIRST[g][3])
            for b in range(GS):
                maxima(0, b)
                if b % 2:
                    split_maxima(0, b // 2)
            dve.wait_ge(x1_out.sem, x1_out.at(NG - 1, 3))
            pairs(dve, group)

        @block.tensor
        def _(pe):
            for s in (p_v, p_s, p_t, p_u, p_mt, p_o, e.p_x, e.p_l, e.p_c, e.p_u, e.p_w):
                s.prime(pe)

            def project_v(g, par, bank):
                for b in range(GS):
                    mm = pe.matmul(bank[:, b * P:(b + 1) * P], cin[:, par, b * P:(b + 1) * P], w_v[:, :], start=True, stop=True)
                mm.then_inc(p_v.sem, 1)

            def x1T(g, par):
                pe.wait_ge(d_xs.sem[par], d_xs.at(g, par))
                pe.wait_ge(a_mt.sem, a_mt.at(g - 2, 1))
                pe.wait_ge(v_v.sem, v_v.at(g - 1, GS - 1))
                transpose_x1(pe, a, t, xs[:, par], PF)

            def k_proj(g):
                pe.wait_ge(v_x.sem, v_x.at(g))
                project(pe, a, g, 1, PF)

            def q_proj(g):
                pe.wait_ge(v_k.sem, v_k.at(g, 0))
                project(pe, a, g, 0, PF)

            def values(g, par, freed):
                pe.wait_ge(*freed)
                project_v(g, par, PF)

            def stacked(g, par, half):
                pe.wait_ge(d_k[half].sem[par], d_k[half].at(g, par))
                pe.wait_ge(d_q[half].sem[par], d_q[half].at(g, par))
                pe.wait_ge(a_mask.sem, a_mask.at(g))

            def scores(g, par, b, u):
                tok = slice(b * P, (b + 1) * P)
                row, c0 = unit_rows(u)
                bank = (SS0, SS1)[u % 2]
                pe.wait_ge(v_max.sem, v_max.at(g, 4 * b + u - 2))
                pe.matmul(bank[:, :], neg_i[:, :], bc(mask[:, par, b, None, :], [P, 4, P]), start=True, stop=False,
                          skip_group_check=True)
                for i in range(4):
                    mm = pe.matmul(bank[:, i * P:(i + 1) * P], q_stack[row:row + NROW, par, c0 + i, tok],
                                   k_stack[row:row + NROW, par, c0 + i, tok], start=False, stop=True, skip_group_check=True)
                mm.then_inc(p_s.sem, 1)

            def scoresT(g, par, b, u):
                tok = slice(b * P, (b + 1) * P)
                row, c0 = unit_rows(u)
                bank = (TT0, TT1)[u % 2]
                pe.wait_ge(a_exp.sem, a_exp.at(g, 4 * b + u - 2))
                pe.matmul(bank[:, :], mask[:, par, b, :], bc(neg_i[:, None, :], [P, 4, P]), start=True, stop=False,
                          skip_group_check=True)
                for i in range(4):
                    mm = pe.matmul(bank[:, i * P:(i + 1) * P], k_stack[row:row + NROW + 3, par, c0 + i, tok],
                                   q_stack[row:row + NROW + 3, par, c0 + i, tok], start=False, stop=True,
                                   skip_group_check=True)
                mm.then_inc(p_t.sem, 1)

            def both(g, par, b, left):
                pe.wait_ge(d_m[b // 2].sem[par], d_m[b // 2].at(g, par))
                for u in range(UNITS):
                    scoresT(g, par, b, u)
                    if left:
                        if b % 2 == 0 and u == 0:
                            stacked(g + 1, 1 - par, b // 2)
                        scores(g + 1, 1 - par, b, u)

            def weigh(g, par, b):
                bank = (U0, U1)[b % 2]
                pe.wait_ge(a_exp.sem, a_exp.at(g, 4 * b + 3))
                pe.wait_ge(v_v.sem, v_v.at(g, b))
                pe.wait_ge(v_norm.sem, v_norm.at(g, 2 * b - 3))
                for k, src in enumerate((v_d[:, par, b, :], ones_d[:, :])):
                    for i in range(4):
                        for u in range(UNITS):
                            mm = pe.matmul(bank[32 * u:32 * u + 32, k * P:(k + 1) * P], src[:, i * P + 32 * u:i * P + 32 * u + 32],
                                           prob[:, b % 2, u, i, :], start=(i == 0), stop=(i == 3), skip_group_check=True)
                mm.then_inc(p_u.sem, 1)

            def max_rows(g, half, freed):
                pe.wait_ge(v_split.sem, v_split.at(g, 4 * half + 3))
                pe.wait_ge(*freed)
                pe.sem_inc(pe_passed, 1)
                for b in range(2 * half, 2 * half + 2):
                    mm = pe.transpose(PF[:, :].bitcast(BF16)[0:48, b * P:(b + 1) * P],
                                      npart[:, b, :, :, :].rearrange("p j r c -> p (j r c)"), ident[:, :])
                mm.then_inc(p_mt.sem, 1)

            def output(g):
                pe.wait_ge(v_norm.sem, v_norm.at(g, 7))
                pe.wait_ge(v_res.sem, v_res.at(g - 1, 0))
                for b in range(GS):
                    mm = pe.matmul(PO[:, b * P:(b + 1) * P], ctxT[:, b, :], w_o[:, :], start=True, stop=True)
                mm.then_inc(p_o.sem, 1)

            def group(g, par, left):
                both(g, par, 0, left)
                if left == 2:
                    x1T(g + 2, par)
                if not left:
                    pe.wait_ge(e.steps, PREPARED)
                    pe.wait_ge(g_out.sem, g_out.at(0, 3))
                    pe.wait_ge(a_mt.sem, a_mt.at(g, 1))
                    transpose_x2(pe, e, x2[:, 0:GS, :])
                both(g, par, 1, left)
                if left == 2:
                    k_proj(g + 2)
                if not left:
                    expert_logits(pe, e, 0, 0)
                weigh(g, par, 0)
                both(g, par, 2, left)
                if left == 2:
                    q_proj(g + 2)
                weigh(g, par, 1)
                if left:
                    max_rows(g + 1, 0, (v_q.sem, v_q.at(g + 2, 0)) if left == 2 else (v_v.sem, v_v.at(g + 1, GS - 1)))
                both(g, par, 3, left)
                weigh(g, par, 2)
                if left:
                    max_rows(g + 1, 1, (a_mt.sem, a_mt.at(g + 1, 0)))
                weigh(g, par, 3)
                if left == 2:
                    values(g + 2, par, (a_mt.sem, a_mt.at(g + 1, 1)))
                output(g)
                if not left:
                    transpose_weights(pe, e, 0)

            for g in range(2):
                if g:
                    transpose_x1(pe, a, t, x1[:, g * GS:(g + 1) * GS, :], FIRST[g][0])
                    project(pe, a, g, 1, FIRST[g][1])
                    project(pe, a, g, 0, FIRST[g][2])
                project_v(g, g, FIRST[g][3])
            pe.wait_ge(g_init, 6)
            for b in range(GS):
                if b % 2 == 0:
                    stacked(0, 0, b // 2)
                for u in range(UNITS):
                    scores(0, 0, b, u)
                if b == 1:
                    max_rows(0, 0, (v_v.sem, v_v.at(1, GS - 1)))
                if b == 3:
                    max_rows(0, 1, (a_mt.sem, a_mt.at(0, 0)))
            pairs(pe, group)


class ExpertState:
    pass


def expert_tensors(ctx, nc, t, psum):
    def sb(name, shape, dt=F32):
        return ctx.enter_context(nc.sbuf_tensor(name, shape, dt))

    def sem(name, n=1):
        return Sem(ctx, nc, name, n)

    e = ExpertState()
    e.PF, e.ident32 = psum[6], t["ident32"]
    e.w_raw = sb("w_raw", [P, 2, NC, P])
    e.w_up = sb("w_up", [P, 2, 2, NC, P], F32R)
    e.w_down = sb("w_down", [P, NC, P])
    e.wg_raw = sb("wg_raw", [P, EXPERTS])
    e.w_gate = sb("w_gate", [P, 2, EXPERTS], F32R)
    e.bias = sb("bias", [P, EXPERTS])
    e.spread = sb("spread", [32, CHUNKS, P], F32R)
    e.before = sb("before", [P, 4, 4])
    e.xT_hl = [sb("xT_hl_c0", [P, 2, GT], F32R)]
    e.cwT = [sb("cwT0", [32, GT], F32R)]
    e.th16 = sb("th16", [P, GS, EXPERTS])
    e.score, e.biased = sb("score", [P, GS, EXPERTS]), sb("biased", [P, GS, EXPERTS])
    e.hi2, e.lo2, e.sum2 = (sb(n, [P, GS * 4, 2]) for n in ("hi2", "lo2", "sum2"))
    e.cross, e.gsum = sb("cross", [P, GS * 4]), sb("gsum", [P, GS, 4])
    e.above, e.tie = sb("above", [P, GS, 4, 4]), sb("tie", [P, GS, 4, 4])
    e.rank, e.penalty = sb("rank", [P, GS, 4]), sb("penalty", [P, GS, 4])
    e.open_ = sb("open_", [P, GS, EXPERTS + 4])
    e.top = sb("top", [P, GS, 8])
    e.marked = sb("marked", [P, GS, EXPERTS + 4])
    e.chosen, e.wsum = sb("chosen", [P, GS, EXPERTS]), sb("wsum", [P, GS])
    e.cw, e.cw_hl = sb("cw", [P, GS, EXPERTS]), sb("cw_hl", [P, GS, 2, EXPERTS], F32R)
    e.loaded, e.steps, e.dve_passed = (ctx.enter_context(nc.semaphore(n)) for n in
                                       ("expert_weights", "expert_pool_steps", "expert_dve_passed"))
    e.p_x, e.p_l, e.p_c = sem("x2T_mm"), sem("logit_mm"), sem("cwT_mm")
    e.p_u, e.p_w = sem("up_mm", NC), sem("weight_mm", CHUNKS)
    e.a_x, e.a_l, e.a_c = sem("x2T_hi"), sem("logit_tanh"), sem("cwT_ready")
    e.v_x, e.v_sc, e.v_grp, e.v_sel = sem("x2T_lo"), sem("scores_ready", 2), sem("groups_ranked", 13), sem("select_dve", 18)
    return e


def prepare_pool(pool, d, e, pick):
    w_raw, w_up, w_down, wg_raw, w_gate = (e.w_raw, e.w_up, e.w_down, e.wg_raw, e.w_gate)
    before, loaded, steps = e.before, e.loaded, e.steps
    for k, (name, shared) in enumerate((("WgT", "Ws_gT"), ("WuT", "Ws_uT"))):
        pool.dma_start(w_raw[:, k, 0, :], d[shared]).then_inc(loaded, 16)
        pool.dma_start(w_raw[:, k, 1:, :], d[name].rearrange("p (c n) -> p c n", n=P)).then_inc(loaded, 16)
    pool.dma_start(w_down[:, 0, :], d["Ws_dT"]).then_inc(loaded, 16)
    pool.dma_start(w_down[:, 1:, :], d["WdT"].rearrange("(c p) n -> p c n", p=P)).then_inc(loaded, 16)
    pool.dma_start(wg_raw[:, :], d["gate_wT"]).then_inc(loaded, 16)
    pool.dma_start(e.bias[:, :], d["gate_bias"].partition_broadcast(P)).then_inc(loaded, 16)
    pool.memset(pick[:, :, :, :], 1.0).then_inc(steps, 1)
    pool.memset(before[:, :, :], 1.0).then_inc(steps, 1)
    pool.wait_ge(steps, 2)
    pool.affine_select(out=pick[:, :, :, :], in_=pick[:, :, :, :], compare_op=ALU.is_equal, fill=0.0, base=0,
                       pattern=[[-2, CHUNKS], [-1, 2], [0, EI]], channel_multiplier=1).then_inc(steps, 1)
    pool.affine_select(out=before[:, :, :], in_=before[:, :, :], compare_op=ALU.is_gt, fill=0.0, base=0,
                       pattern=[[1, 4], [-1, 4]], channel_multiplier=0).then_inc(steps, 1)
    pool.wait_ge(steps, 4)
    pool.affine_select(out=pick[:, :, :, :], in_=pick[:, :, :, :], compare_op=ALU.not_equal, fill=1.0, base=-EXPERTS,
                       pattern=[[-2, CHUNKS], [-1, 2], [0, EI]], channel_multiplier=1).then_inc(steps, 1)
    pool.wait_ge(steps, 5)
    pool.tensor_copy(e.spread[:, :, :], pick[:, :, :, :].rearrange("p c e i -> p c (e i)")).then_inc(steps, 1)
    pool.wait_ge(loaded, 8 * 16)
    for k in range(2):
        pool.tensor_copy(w_up[:, k, 0], w_raw[:, k]).then_inc(steps, 1)
    pool.tensor_copy(w_gate[:, 0, :], wg_raw[:, :]).then_inc(steps, 1)
    pool.wait_ge(steps, 9)
    for k in range(2):
        pool.tensor_tensor(w_up[:, k, 1], w_raw[:, k], w_up[:, k, 0].bitcast(F32), ALU.subtract).then_inc(steps, 1)
    pool.tensor_tensor(w_gate[:, 1, :], wg_raw[:, :], w_gate[:, 0, :].bitcast(F32), ALU.subtract).then_inc(steps, 1)




def x2T_hi(act, e, g, par):
    act.wait_ge(e.p_x.sem, e.p_x.at(g))
    act.wait_ge(e.p_u.sem, e.p_u.at(g - 2, NC - 1))
    act.activation(e.xT_hl[par][:, 0, :], e.PF[:, :], ACT.Copy).then_inc(e.a_x.sem, 1)


def logit_tanh(act, e, g):
    act.wait_ge(e.p_l.sem, e.p_l.at(g))
    act.wait_ge(e.v_sc.sem, e.v_sc.at(g - 1, 0))
    act.activation(e.th16[:, :, :], e.PF[:, 0:GS * EXPERTS], ACT.Tanh, scale=0.5).then_inc(e.a_l.sem, 1)


def copy_weights(act, e, g, par):
    act.wait_ge(e.p_c.sem, e.p_c.at(g))
    act.wait_ge(e.p_w.sem, e.p_w.at(g - 2, CHUNKS - 1))
    act.activation(e.cwT[par][:, :], e.PF[0:32, :], ACT.Copy).then_inc(e.a_c.sem, 1)


def x2T_lo(dve, e, g, par):
    dve.wait_ge(e.a_x.sem, e.a_x.at(g))
    dve.tensor_tensor(e.xT_hl[par][:, 1, :], e.PF[:, :], e.xT_hl[par][:, 0, :].bitcast(F32), ALU.subtract).then_inc(e.v_x.sem, 1)


def expert_scores(dve, e, g):
    dve.wait_ge(e.a_l.sem, e.a_l.at(g))
    dve.wait_ge(e.v_sel.sem, e.v_sel.at(g - 1, 11))
    dve.tensor_scalar(e.score[:, :, :], e.th16[:, :, :], 0.5, 0.5, ALU.mult, ALU.add).then_inc(e.v_sc.sem, 1)
    dve.wait_ge(e.v_sc.sem, e.v_sc.at(g, 0))
    dve.wait_ge(e.v_grp.sem, e.v_grp.at(g - 1, 1))
    dve.tensor_tensor(e.biased[:, :, :], e.score[:, :, :], bc(e.bias[:, None, :], [P, GS, EXPERTS]), ALU.add)\
        .then_inc(e.v_sc.sem, 1)


def rank_groups(dve, e, g):
    def step(k, ins):
        ins.then_inc(e.v_grp.sem, 1)
        dve.wait_ge(e.v_grp.sem, e.v_grp.at(g, k))

    dve.wait_ge(e.v_sc.sem, e.v_sc.at(g, 1))
    four = e.biased[:, :, :].rearrange("p b (q n e) -> p (b q) n e", q=4, n=2)
    step(0, dve.tensor_tensor(e.hi2[:, :, :], four[:, :, :, 0], four[:, :, :, 1], ALU.max))
    step(1, dve.tensor_tensor(e.lo2[:, :, :], four[:, :, :, 0], four[:, :, :, 1], ALU.min))
    step(2, dve.tensor_tensor(e.sum2[:, :, :], e.hi2[:, :, :], e.lo2[:, :, :], ALU.add))
    step(3, dve.tensor_tensor(e.cross[:, :], e.hi2[:, :, 0], e.hi2[:, :, 1], ALU.add))
    gs = e.gsum[:, :, :].rearrange("p b q -> p (b q)")
    step(4, dve.tensor_tensor(gs, e.sum2[:, :, 0], e.sum2[:, :, 1], ALU.max))
    step(5, dve.tensor_tensor(gs, gs, e.cross[:, :], ALU.max))
    mine, other = bc(e.gsum[:, :, :, None], [P, GS, 4, 4]), bc(e.gsum[:, :, None, :], [P, GS, 4, 4])
    step(6, dve.tensor_tensor(e.above[:, :, :, :], other, mine, ALU.is_gt))
    step(7, dve.tensor_tensor(e.tie[:, :, :, :], other, mine, ALU.is_ge))
    step(8, dve.tensor_tensor(e.tie[:, :, :, :], e.tie[:, :, :, :], bc(e.before[:, None, :, :], [P, GS, 4, 4]), ALU.mult))
    step(9, dve.tensor_tensor(e.above[:, :, :, :], e.above[:, :, :, :], e.tie[:, :, :, :], ALU.max))
    step(10, dve.tensor_tensor(e.tie[:, :, :, 0:2], e.above[:, :, :, 0:2], e.above[:, :, :, 2:4], ALU.add))
    step(11, dve.tensor_tensor(e.rank[:, :, :], e.tie[:, :, :, 0], e.tie[:, :, :, 1], ALU.add))
    dve.wait_ge(e.v_sel.sem, e.v_sel.at(g - 1, 0))
    step(12, dve.tensor_scalar(e.penalty[:, :, :], e.rank[:, :, :], 2.0, -1.0e30, ALU.is_ge, ALU.mult))


def select_experts(dve, e, g):
    def step(k, ins):
        ins.then_inc(e.v_sel.sem, 1)
        dve.wait_ge(e.v_sel.sem, e.v_sel.at(g, k))

    dve.wait_ge(e.v_grp.sem, e.v_grp.at(g, 12))
    step(0, dve.tensor_tensor(e.open_[:, :, 0:EXPERTS].rearrange("p b (q e) -> p b q e", q=4),
                              e.biased[:, :, :].rearrange("p b (q e) -> p b q e", q=4),
                              bc(e.penalty[:, :, :, None], [P, GS, 4, 4]), ALU.add))
    dve.sem_inc(e.dve_passed, 1)
    for b in range(GS):
        dve.max(e.top[:, b, :], e.open_[:, b, 0:EXPERTS]).then_inc(e.v_sel.sem, 1)
    dve.wait_ge(e.v_sel.sem, e.v_sel.at(g, 4))
    step(5, dve.memset(e.top[:, :, 4:], SENTINEL))
    dve.sem_inc(e.dve_passed, 1)
    for b in range(GS):
        dve.match_replace(e.marked[:, b, :], e.top[:, b, :], e.open_[:, b, :], TAKEN).then_inc(e.v_sel.sem, 1)
    dve.wait_ge(e.v_sel.sem, e.v_sel.at(g, 9))


def share_weights(dve, e, g):
    def step(k, ins):
        ins.then_inc(e.v_sel.sem, 1)
        dve.wait_ge(e.v_sel.sem, e.v_sel.at(g, k))

    step(10, dve.tensor_scalar(e.chosen[:, :, :], e.marked[:, :, 0:EXPERTS], TAKEN, None, ALU.is_ge))
    step(11, dve.tensor_tensor(e.chosen[:, :, :], e.chosen[:, :, :], e.score[:, :, :], ALU.mult))
    step(12, dve.tensor_reduce(e.wsum[:, :], e.chosen[:, :, :], AX_X, ALU.add))
    step(13, dve.tensor_scalar(e.wsum[:, :], e.wsum[:, :], 1e-20, None, ALU.add))
    step(14, dve.reciprocal(e.wsum[:, :], e.wsum[:, :]))
    step(15, dve.scalar_tensor_tensor(e.cw[:, :, :], e.chosen[:, :, :], SCALE, bc(e.wsum[:, :, None], [P, GS, EXPERTS]),
                                      ALU.mult, ALU.mult))
    dve.wait_ge(e.p_c.sem, e.p_c.at(g - 1))
    step(16, dve.tensor_copy(e.cw_hl[:, :, 0, :], e.cw[:, :, :]))
    step(17, dve.tensor_tensor(e.cw_hl[:, :, 1, :], e.cw[:, :, :], e.cw_hl[:, :, 0, :].bitcast(F32), ALU.subtract))


def transpose_x2(pe, e, src):
    for b in range(GS):
        mm = pe.transpose(e.PF[:, b * P:(b + 1) * P], src[:, b, :], e.ident32[:, :])
    mm.then_inc(e.p_x.sem, 1)


def expert_logits(pe, e, g, par):
    pe.wait_ge(e.v_x.sem, e.v_x.at(g))
    for b in range(GS):
        for n, (a, v) in enumerate(((0, 0), (0, 1), (1, 0))):
            mm = pe.matmul(e.PF[:, b * EXPERTS:(b + 1) * EXPERTS], e.xT_hl[par][:, a, b * P:(b + 1) * P], e.w_gate[:, v, :],
                           start=(n == 0), stop=(n == 2))
    mm.then_inc(e.p_l.sem, 1)


def transpose_weights(pe, e, g):
    pe.wait_ge(e.v_sel.sem, e.v_sel.at(g, 17))
    pe.wait_ge(e.a_l.sem, e.a_l.at(g))
    for b in range(GS):
        mm = pe.transpose(e.PF[0:32, b * P:(b + 1) * P],
                          e.cw_hl[:, b, :, :].rearrange("p v e -> p (v e)").bitcast(F32), e.ident32[:, :])
    mm.then_inc(e.p_c.sem, 1)


def experts(nc, t, d, out, psum, e):
    with ExitStack() as ctx:
        def sb(name, shape, dt=F32):
            return ctx.enter_context(nc.sbuf_tensor(name, shape, dt))

        def sem(name, n=1, by=1):
            return Sem(ctx, nc, name, n, by)

        def raw(name):
            return ctx.enter_context(nc.semaphore(name))

        w_up, w_down, spread, xT_hl, cwT = e.w_up, e.w_down, e.spread, e.xT_hl, e.cwT
        xT_hl.append(sb("xT_hl_c1", [P, 2, GT], F32R))
        cwT.append(sb("cwT1", [32, GT], F32R))
        xs = sb("xs_c", [P, 2, GS, P])
        sg = sb("sg", [P, 2, GT])
        gu = sb("gu", [P, 2, GT])
        hid = sb("hid", [P, NC, GT])
        res, stats, mv, rstd = t["res"], t["stats"], t["mv"], t["rstd"]
        normed = sb("normed", [P, 2, GS, P])
        x2, ident32, norm_c = t["x2"], t["ident32"], t["norm_c"]

        d_x, d_out = DmaSem(ctx, nc, "x2_staged"), DmaSem(ctx, nc, "out_stored")
        p_x, p_u, p_w, a_c = e.p_x, e.p_u, e.p_w, e.a_c
        p_g, p_d, a_s = sem("gate_mm", NC), sem("down_mm", NC), sem("silu_ready", NC)
        v_gu, v_hid = sem("gu_ready", NC), sem("hid_ready", CHUNKS)
        v_res, g_out, x2_out = sem("res_c_ready", 1 + 2 * GS), sem("out_ready", 4), t["x2_out"]
        dve_passed = e.dve_passed

        GG, UU, WW, PF, PO = psum[0:2], psum[2:4], psum[4:6], psum[6], psum[7]
        block = ctx.enter_context(nc.Block())

        @block.sync
        def _(sp):
            d_x.prime(sp)
            sp.sem_inc(d_x.sem[0], 16)
            d_out.prime(sp)

            def load(g, par):
                sp.wait_ge(p_x.sem, p_x.at(g - 2))
                sp.dma_start(xs[:, par, :, :], x2[:, bass.ds(g * GS, GS), :]).then_inc(d_x.sem[par], 16)

            def group(g, par, left):
                if left == 2:
                    load(g + 2, par)
                sp.wait_ge(g_out.sem, g_out.at(g, 3))
                sp.dma_start(out.rearrange("(b t) d -> t b d", t=P)[:, bass.ds(g * GS, GS), :], normed[:, par, :, :])\
                    .then_inc(d_out.sem[par], 16)

            load(1, 1)
            sp.wait_ge(x2_out.sem, x2_out.at(NG - 1, 3))
            pairs(sp, group)
            for g in (NG - 2, NG - 1):
                sp.wait_ge(d_out.sem[g % 2], d_out.at(g, g % 2))

        @block.gpsimd
        def _(pool):
            g_out.prime(pool)

            def group(g, par, left):
                normalise_pool(pool, g, v_res, g_out, res, mv, rstd, norm_c, normed[:, par, :, :],
                               (d_out.sem[par], d_out.at(g - 2, par)))

            normalise_pool(pool, NG - 1, t["x2_res"], x2_out, res, mv, rstd, norm_c, x2[:, NSEQ - GS:, :])
            pairs(pool, group)

        @block.scalar
        def _(act):
            a_s.prime(act)

            def silu(g, par, c):
                k = (par + c) % 2
                act.wait_ge(p_g.sem, p_g.at(g, c))
                act.wait_ge(v_gu.sem, v_gu.at(g, c - 2))
                act.activation(sg[:, k, :], GG[k][:, :], ACT.Silu).then_inc(a_s.sem, 1)

            def group(g, par, left):
                nxt = (g + 1, 1 - par)
                for c in range(2, NC):
                    silu(g, par, c)
                    if left and c == 2:
                        x2T_hi(act, e, *nxt)
                    if left and c == 3:
                        logit_tanh(act, e, g + 1)
                if left:
                    silu(*nxt, 0)
                    copy_weights(act, e, *nxt)
                    silu(*nxt, 1)

            silu(0, 0, 0)
            silu(0, 0, 1)
            pairs(act, group)

        @block.vector
        def _(dve):
            for s in (v_gu, v_hid, v_res):
                s.prime(dve)

            def hidden(g, par, c):
                k = (par + c) % 2
                dve.wait_ge(a_s.sem, a_s.at(g, c))
                dve.wait_ge(p_u.sem, p_u.at(g, c))
                dve.wait_ge(p_d.sem, p_d.at(g - 1, c))
                if c:
                    dve.wait_ge(v_hid.sem, v_hid.at(g, max(c - 3, -1)))
                dst = hid[:, 0, :] if c == 0 else gu[:, k, :]
                dve.tensor_tensor(dst, sg[:, k, :], UU[k][:, :], ALU.mult).then_inc(v_gu.sem, 1)
                if c:
                    dve.wait_ge(v_gu.sem, v_gu.at(g, c))
                    dve.wait_ge(p_w.sem, p_w.at(g, c - 1))
                    dve.tensor_tensor(hid[:, c, :], gu[:, k, :], WW[(c - 1) % 2][:, :], ALU.mult).then_inc(v_hid.sem, 1)

            def group(g, par, left):
                nxt = (g + 1, 1 - par)
                for c in range(2, NC):
                    hidden(g, par, c)
                    if left and c == 2:
                        x2T_lo(dve, e, *nxt)
                    if left and c == 3:
                        expert_scores(dve, e, g + 1)
                    if left and c == 4:
                        rank_groups(dve, e, g + 1)
                    if left and c == 5:
                        select_experts(dve, e, g + 1)
                    if left and c == 6:
                        share_weights(dve, e, g + 1)
                if left:
                    hidden(*nxt, 0)
                    hidden(*nxt, 1)
                dve.wait_ge(p_d.sem, p_d.at(g, NC - 1))
                residual_dve(dve, g, PO, x2[:, bass.ds(g * GS, GS), :], g_out, v_res, dve_passed, res, stats, mv, times=2.0)

            hidden(0, 0, 0)
            hidden(0, 0, 1)
            dve.wait_ge(x2_out.sem, x2_out.at(NG - 1, 3))
            pairs(dve, group)

        @block.tensor
        def _(pe):
            for s in (p_g, p_d):
                s.prime(pe)

            def x2T(g, par):
                pe.wait_ge(d_x.sem[par], d_x.at(g, par))
                pe.wait_ge(a_c.sem, a_c.at(g - 1))
                transpose_x2(pe, e, xs[:, par])

            def up(g, par, c):
                k = (par + c) % 2
                for which, bank, freed, done in ((0, GG[k], a_s, p_g), (1, UU[k], v_gu, p_u)):
                    pe.wait_ge(freed.sem, freed.at(g, c - 2))
                    for n, (a, v) in enumerate(((0, 0), (0, 1), (1, 0))):
                        mm = pe.matmul(bank[:, :], w_up[:, which, a, c, :], xT_hl[par][:, v, :], start=(n == 0), stop=(n == 2))
                    mm.then_inc(done.sem, 1)
                if c:
                    pe.wait_ge(a_c.sem, a_c.at(g))
                    pe.wait_ge(v_hid.sem, v_hid.at(g, c - 3))
                    pe.matmul(WW[(c - 1) % 2][:, :], spread[:, c - 1, :], cwT[par][:, :], start=True, stop=True)\
                        .then_inc(p_w.sem, 1)

            def down(g, c):
                if c == 0:
                    pe.wait_ge(v_gu.sem, v_gu.at(g, 0))
                    pe.wait_ge(v_res.sem, v_res.at(g - 1, 0))
                else:
                    pe.wait_ge(v_hid.sem, v_hid.at(g, c - 1))
                for b in range(GS):
                    mm = pe.matmul(PO[:, b * P:(b + 1) * P], hid[:, c, b * P:(b + 1) * P], w_down[:, c, :],
                                   start=(c == 0 and b == 0), stop=(c == NC - 1), skip_group_check=True)
                mm.then_inc(p_d.sem, 1)

            def group(g, par, left):
                nxt = (g + 1, 1 - par)
                for c in range(2, NC):
                    up(g, par, c)
                    down(g, c - 2)
                    if left and c == 2:
                        x2T(*nxt)
                    if left and c == 3:
                        expert_logits(pe, e, *nxt)
                if left:
                    up(*nxt, 0)
                    transpose_weights(pe, e, g + 1)
                down(g, NC - 2)
                if left:
                    up(*nxt, 1)
                down(g, NC - 1)

            up(0, 0, 0)
            up(0, 0, 1)
            pairs(pe, group)


def build(nc, d, out, stop_at=None):
    with ExitStack() as ctx:
        psum = [ctx.enter_context(nc.psum_tensor(f"bank{k}", [P, 512], F32)) for k in range(8)]
        t = {k: ctx.enter_context(nc.sbuf_tensor(k, [P, NSEQ, P], F32)) for k in ("x1", "x2")}
        t["ident"] = ctx.enter_context(nc.sbuf_tensor("ident", [P, P], BF16))
        t["ident32"] = ctx.enter_context(nc.sbuf_tensor("ident32", [P, P], F32))
        for name in ("w_v", "w_o", "b_v", "b_o"):
            t[name] = ctx.enter_context(nc.sbuf_tensor(name, [P, P], F32))
        a = projection_tensors(ctx, nc, t)
        for name, shape in (("res", [P, GS, P]), ("stats", [P, GS, 6]), ("mv", [P, GS, 2]), ("rstd", [P, GS])):
            t[name] = ctx.enter_context(nc.sbuf_tensor(name, shape, F32))
        for x in ("x1", "x2"):
            t[x + "_res"], t[x + "_out"] = Sem(ctx, nc, x + "_sum_ready", 1 + 2 * GS), Sem(ctx, nc, x + "_ready", 4)
        t["norm_c"] = ctx.enter_context(nc.sbuf_tensor("norm_c", [P, 2, GS], F32))
        mixer(nc, t, d, psum, a, stop_at)
        if stop_at in ("small", "trig", "mixer"):
            return
        e = expert_tensors(ctx, nc, t, psum)
        attention(nc, t, d, psum, a, e)
        experts(nc, t, d, out, psum, e)


_DRAM = {
    "x": "x", "xT": "x", "ctxT": "ctx_1024", "mask": "mask_Bx1xSxS2_bk1", "w_inT": "L0_attn_w_in", "w_outT": "L0_attn_w_out",
    "dt_bias": "L0_attn_dt_bias", "D": "L0_attn_D", "Wq": "L0_xattn_Wq", "bq": "L0_xattn_bq", "Wk": "L0_xattn_Wk",
    "bk": "L0_xattn_bk", "Wv": "L0_xattn_Wv", "bv": "L0_xattn_bv", "Wo": "L0_xattn_Wo", "bo": "L0_xattn_bo",
    "gate_wT": "L0_ffn_gate_w", "gate_bias": "L0_ffn_gate_bias", "WgT": "L0_ffn_Wg", "WuT": "L0_ffn_Wu", "WdT": "L0_ffn_Wd",
    "Ws_gT": "L0_ffn_Ws_g", "Ws_uT": "L0_ffn_Ws_u", "Ws_dT": "L0_ffn_Ws_d",
}


def lay_out(inputs):
    import numpy as np
    a = {k: np.asarray(inputs[v]) for k, v in _DRAM.items()}
    a["x"] = a["x"].reshape(-1, P)
    a["xT"] = a["xT"].reshape(-1, P).T
    a["ctxT"] = a["ctxT"].reshape(-1, P).T
    a["mask"] = np.ascontiguousarray(a["mask"]).reshape(NSEQ, P, P).view(np.int32)
    for k in ("Wq", "bq", "Wk", "bk"):
        a[k] = a[k].reshape(-1, XH, XD).swapaxes(-1, -2).reshape(a[k].shape)
    for k in ("w_inT", "w_outT", "gate_wT", "Ws_gT", "Ws_uT", "Ws_dT"):
        a[k] = a[k].T
    a["WgT"] = a["WgT"].reshape(EXPERTS * EI, P).T
    a["WuT"] = a["WuT"].reshape(EXPERTS * EI, P).T
    a["WdT"] = a["WdT"].transpose(0, 2, 1).reshape(EXPERTS * EI, P)
    return {k: np.ascontiguousarray(v) for k, v in a.items()}


def kernel(**inputs):
    import concourse.bacc as bacc
    from concourse.bass_utils import run_bass_kernel_spmd

    nc = bacc.Bacc("TRN2", target_bir_lowering=False, num_devices=1)
    arrays = lay_out(inputs)
    d = {k: nc.dram_tensor(k + "_in", a.shape, mybir.dt.from_np(a.dtype), kind="ExternalInput").ap() for k, a in arrays.items()}
    out = nc.dram_tensor("out", (NSEQ * P, P), F32, kind="ExternalOutput").ap()
    build(nc, d, out)
    r = run_bass_kernel_spmd(nc, [{k + "_in": a for k, a in arrays.items()}], core_ids=[0])
    return r.results[0]["out"].reshape(NSEQ, P, P)
```
